# Optimizing a Trainium2 kernel written in Bass

```python
import numpy as np
import jax
import jax.numpy as jnp

def _softmax(x, axis=-1):
    return jax.nn.softmax(x, axis=axis)

def _gelu(x):
    return jax.nn.gelu(x, approximate=True)

def _silu(x):
    return jax.nn.silu(x)

def _sigmoid(x):
    return jax.nn.sigmoid(x)

def _layernorm(x, axis=-1, eps=1e-05):
    m = jnp.mean(x, axis=axis, keepdims=True)
    v = jnp.var(x, axis=axis, keepdims=True)
    return (x - m) / jnp.sqrt(v + eps)

def _scatter_add(tgt, idx, src, axis=0):
    return tgt.at[idx].add(src)

def _segment_sum(src, seg, n):
    return jax.ops.segment_sum(src, seg, n)
kernel_name = 'mk_flamingo_gated_d2_seqx_r4_cf8d42'

def setup_inputs(seed: int=0):
    np.random.seed(seed)
    _w = jnp.asarray

    def _rec_inputs():
        import jax
        import jax.numpy as jnp
        _rk = jax.random.key(seed)
        x = 0.002226 + 0.9996 * jax.random.normal(jax.random.fold_in(_rk, 1), (16, 112, 256), jnp.float32)
        _lenS = 112 - jax.random.randint(jax.random.fold_in(_rk, 7), (16,), 0, max(1, 112 // 4) + 1, jnp.int32)
        _lenS2 = 375 - jax.random.randint(jax.random.fold_in(_rk, 8), (16,), 0, max(1, 375 // 4) + 1, jnp.int32)
        _ctx_1024P = jax.random.normal(jax.random.fold_in(_rk, 11), (16, 16, 256), jnp.float32)
        _ctx_1024c = jax.random.dirichlet(jax.random.fold_in(_rk, 511), 0.3 * jnp.ones((16,), jnp.float32), (16, 375))
        _ctx_1024t = jnp.einsum('bsk,bkd->bsd', _ctx_1024c, _ctx_1024P)
        _ctx_1024t = _ctx_1024t * jax.lax.rsqrt(jnp.mean(jnp.square(_ctx_1024t)) + 1e-12) * 0.953939
        ctx_1024 = -7.10856e-05 + 0.999911 * (_ctx_1024t + 0.3 * jax.random.normal(jax.random.fold_in(_rk, 611), (16, 375, 256), jnp.float32))
        _validS = jnp.arange(112)[None, :] < _lenS[:, None]
        _validS2 = jnp.arange(375)[None, :] < _lenS2[:, None]
        _causal = jnp.tril(jnp.ones((112, 112), dtype=bool))
        mask_BxS2_bk0 = jnp.logical_not(jnp.broadcast_to(_validS2[:, :], (16, 375)))
        _g = jax.random.normal(jax.random.fold_in(_rk, 9001), (2, 2), jnp.float32)
        _g = jnp.sign(_g) * jnp.maximum(jnp.abs(_g), 1.0) + (_g == 0) * 1.0
        g_xattn = _g[0]
        g_ffn = _g[1]
        return (x, ctx_1024, mask_BxS2_bk0, g_xattn, g_ffn)
    x, ctx_1024, mask_BxS2_bk0, g_xattn, g_ffn = _rec_inputs()

    def _L0_xattn_setup():
        import jax, jax.numpy as jnp
        import numpy as np
        HEADS = 8
        DIM_HEAD = 64
        SCALE = DIM_HEAD ** (-0.5)
        LN_EPS = 1e-05
        NEG_INF = -1e+30

        def layernorm(x, gamma, beta):
            mu = jnp.mean(x, axis=-1, keepdims=True)
            var = jnp.var(x, axis=-1, keepdims=True)
            return (x - mu) * jax.lax.rsqrt(var + LN_EPS) * gamma + beta
        key = jax.random.key(seed)
        ks = jax.random.split(key, 8)
        b, f, n, d, inner = (8, 2048, 64, 256, HEADS * DIM_HEAD)
        x = jax.random.normal(ks[0], (b, f, d), dtype=jnp.float32)
        latents = jax.random.normal(ks[1], (b, n, d), dtype=jnp.float32)
        key_padding_mask = jax.random.randint(ks[2], (b, f), 0, 2) > 0
        s = 0.02
        return {'x': x, 'latents': latents, 'key_padding_mask': key_padding_mask, 'kv_gate': jnp.float32(-4.0), 'gamma_media': jnp.ones((d,), jnp.float32), 'beta_media': jnp.zeros((d,), jnp.float32), 'gamma_lat': jnp.ones((d,), jnp.float32), 'beta_lat': jnp.zeros((d,), jnp.float32), 'Wq': jax.random.normal(ks[3], (d, inner), jnp.float32) * s, 'Wk': jax.random.normal(ks[4], (d, inner), jnp.float32) * s, 'Wv': jax.random.normal(ks[5], (d, inner), jnp.float32) * s, 'Wout': jax.random.normal(ks[6], (inner, d), jnp.float32) * s}
    _L0_xattn_all = _L0_xattn_setup()
    _L0_xattn_in = {k: v for k, v in _L0_xattn_all.items() if k in ('kv_gate', 'gamma_media', 'beta_media', 'gamma_lat', 'beta_lat', 'Wq', 'Wk', 'Wv', 'Wout')}
    del _L0_xattn_all

    def _L0_ffn_setup():
        import jax, jax.numpy as jnp
        import numpy as np
        B, S, H = (1, 256, 256)
        E, I = (8, 512)
        JITTER_EPS = 0.01

        def _sparse_mixer_top2(scores, jitter_eps):
            vals, idx = jax.lax.top_k(scores, 2)
            neg_inf = jnp.array(-jnp.inf, scores.dtype)
            t1 = vals[:, :1]
            f1 = jnp.maximum(jnp.abs(scores), t1)
            m1 = (t1 - scores) / f1 > 2 * jitter_eps
            p1 = jax.nn.softmax(jnp.where(m1, neg_inf, scores), axis=-1)
            mult1 = jnp.take_along_axis(p1, idx[:, :1], axis=-1)
            t2 = vals[:, 1:2]
            f2 = jnp.maximum(jnp.abs(scores), t2)
            m2 = (t2 - scores) / f2 > 2 * jitter_eps
            rows = jnp.arange(scores.shape[0])[:, None]
            s2 = scores.at[rows, idx[:, :1]].set(neg_inf)
            p2 = jax.nn.softmax(jnp.where(m2, neg_inf, s2), axis=-1)
            mult2 = jnp.take_along_axis(p2, idx[:, 1:2], axis=-1)
            return (jnp.concatenate([mult1, mult2], axis=-1), idx)
        key = jax.random.key(seed)
        ks = jax.random.split(key, 5)
        s_h = 1.0 / np.sqrt(H)
        s_i = 1.0 / np.sqrt(I)
        return {'hidden_states': jax.random.normal(ks[0], (B, S, H), jnp.float32), 'gate_w': jax.random.normal(ks[1], (E, H), jnp.float32) * s_h, 'w1': jax.random.normal(ks[2], (E, I, H), jnp.float32) * s_h, 'w2': jax.random.normal(ks[3], (E, H, I), jnp.float32) * s_i, 'w3': jax.random.normal(ks[4], (E, I, H), jnp.float32) * s_h}
    _L0_ffn_all = _L0_ffn_setup()
    _L0_ffn_in = {k: v for k, v in _L0_ffn_all.items() if k in ('gate_w', 'w1', 'w2', 'w3')}
    del _L0_ffn_all

    def _L1_xattn_setup():
        import jax, jax.numpy as jnp
        import numpy as np
        EPS = 1e-05

        def layer_norm(x, g, b):
            mu = jnp.mean(x, axis=-1, keepdims=True)
            var = jnp.mean((x - mu) ** 2, axis=-1, keepdims=True)
            return (x - mu) * jax.lax.rsqrt(var + EPS) * g + b
        key = jax.random.key(seed)
        ks = jax.random.split(key, 8)
        b, n, l, D = (8, 1024, 64, 256)
        heads, dim_head = (16, 64)
        inner = heads * dim_head
        x = jax.random.normal(ks[0], (b, n, D), dtype=jnp.float32)
        latents = jax.random.normal(ks[1], (b, l, D), dtype=jnp.float32)
        mask = jax.random.randint(ks[2], (b, n), 0, 2) > 0
        Wq = jax.random.normal(ks[3], (D, inner), dtype=jnp.float32) * D ** (-0.5)
        Wkv = jax.random.normal(ks[4], (D, 2 * inner), dtype=jnp.float32) * D ** (-0.5)
        Wout = jax.random.normal(ks[5], (inner, D), dtype=jnp.float32) * inner ** (-0.5)
        g1 = jnp.ones((D,), jnp.float32)
        b1 = jnp.zeros((D,), jnp.float32)
        g2 = jnp.ones((D,), jnp.float32)
        b2 = jnp.zeros((D,), jnp.float32)
        return {'x': x, 'latents': latents, 'mask': mask, 'g1': g1, 'b1': b1, 'g2': g2, 'b2': b2, 'Wq': Wq, 'Wkv': Wkv, 'Wout': Wout}
    _L1_xattn_all = _L1_xattn_setup()
    _L1_xattn_in = {k: v for k, v in _L1_xattn_all.items() if k in ('g1', 'b1', 'g2', 'b2', 'Wq', 'Wkv', 'Wout')}
    del _L1_xattn_all

    def _L1_ffn_setup():
        import jax, jax.numpy as jnp
        import numpy as np
        B, S, D_MODEL, D_HIDDEN = (4, 512, 256, 1024)

        def act_quant(x):
            scale = 127.0 / jnp.clip(jnp.max(jnp.abs(x), axis=-1, keepdims=True), 1e-05)
            return jnp.clip(jnp.round(x * scale), -128, 127) / scale

        def weight_quant(w):
            scale = 1.0 / jnp.clip(jnp.mean(jnp.abs(w)), 1e-05)
            return jnp.clip(jnp.round(w * scale), -1, 1) / scale

        def bit_linear(x, w):
            xq = x + jax.lax.stop_gradient(act_quant(x) - x)
            wq = w + jax.lax.stop_gradient(weight_quant(w) - w)
            return jnp.einsum('bsd,hd->bsh', xq, wq)

        def depthwise_conv1d(x_bcl, w, b):
            y = jax.lax.conv_general_dilated(x_bcl, w, window_strides=(1,), padding=[(1, 1)], dimension_numbers=('NCH', 'OIH', 'NCH'), feature_group_count=x_bcl.shape[1])
            return y + b[None, :, None]
        key = jax.random.key(seed)
        ks = jax.random.split(key, 5)
        lim1 = 1.0 / np.sqrt(D_MODEL)
        lim2 = 1.0 / np.sqrt(D_HIDDEN)
        limc = 1.0 / np.sqrt(3.0)
        return {'x': jax.random.normal(ks[0], (B, S, D_MODEL), dtype=jnp.float32), 'w1': jax.random.uniform(ks[1], (D_HIDDEN, D_MODEL), jnp.float32, -lim1, lim1), 'conv_w': jax.random.uniform(ks[2], (D_HIDDEN, 1, 3), jnp.float32, -limc, limc), 'conv_b': jax.random.uniform(ks[3], (D_HIDDEN,), jnp.float32, -limc, limc), 'w2': jax.random.uniform(ks[4], (D_MODEL, D_HIDDEN), jnp.float32, -lim2, lim2)}
    _L1_ffn_all = _L1_ffn_setup()
    _L1_ffn_in = {k: v for k, v in _L1_ffn_all.items() if k in ('w1', 'conv_w', 'conv_b', 'w2')}
    del _L1_ffn_all
    return {'x': x, 'ctx_1024': ctx_1024, 'mask_BxS2_bk0': mask_BxS2_bk0, 'g_xattn': g_xattn, 'g_ffn': g_ffn, 'L0_xattn_kv_gate': _L0_xattn_in['kv_gate'], 'L0_xattn_gamma_media': _L0_xattn_in['gamma_media'], 'L0_xattn_beta_media': _L0_xattn_in['beta_media'], 'L0_xattn_gamma_lat': _L0_xattn_in['gamma_lat'], 'L0_xattn_beta_lat': _L0_xattn_in['beta_lat'], 'L0_xattn_Wq': _L0_xattn_in['Wq'], 'L0_xattn_Wk': _L0_xattn_in['Wk'], 'L0_xattn_Wv': _L0_xattn_in['Wv'], 'L0_xattn_Wout': _L0_xattn_in['Wout'], 'L0_ffn_gate_w': _L0_ffn_in['gate_w'], 'L0_ffn_w1': _L0_ffn_in['w1'], 'L0_ffn_w2': _L0_ffn_in['w2'], 'L0_ffn_w3': _L0_ffn_in['w3'], 'L1_xattn_g1': _L1_xattn_in['g1'], 'L1_xattn_b1': _L1_xattn_in['b1'], 'L1_xattn_g2': _L1_xattn_in['g2'], 'L1_xattn_b2': _L1_xattn_in['b2'], 'L1_xattn_Wq': _L1_xattn_in['Wq'], 'L1_xattn_Wkv': _L1_xattn_in['Wkv'], 'L1_xattn_Wout': _L1_xattn_in['Wout'], 'L1_ffn_w1': _L1_ffn_in['w1'], 'L1_ffn_conv_w': _L1_ffn_in['conv_w'], 'L1_ffn_conv_b': _L1_ffn_in['conv_b'], 'L1_ffn_w2': _L1_ffn_in['w2']}

def reference(x, ctx_1024, mask_BxS2_bk0, g_xattn, g_ffn, L0_xattn_kv_gate, L0_xattn_gamma_media, L0_xattn_beta_media, L0_xattn_gamma_lat, L0_xattn_beta_lat, L0_xattn_Wq, L0_xattn_Wk, L0_xattn_Wv, L0_xattn_Wout, L0_ffn_gate_w, L0_ffn_w1, L0_ffn_w2, L0_ffn_w3, L1_xattn_g1, L1_xattn_b1, L1_xattn_g2, L1_xattn_b2, L1_xattn_Wq, L1_xattn_Wkv, L1_xattn_Wout, L1_ffn_w1, L1_ffn_conv_w, L1_ffn_conv_b, L1_ffn_w2):
    import jax
    import jax.numpy as jnp

    def _L0_xattn_ref(x, latents, key_padding_mask, kv_gate, gamma_media, beta_media, gamma_lat, beta_lat, Wq, Wk, Wv, Wout):
        import jax, jax.numpy as jnp
        import numpy as np
        HEADS = 8
        DIM_HEAD = 64
        SCALE = DIM_HEAD ** (-0.5)
        LN_EPS = 1e-05
        NEG_INF = -1e+30

        def layernorm(x, gamma, beta):
            mu = jnp.mean(x, axis=-1, keepdims=True)
            var = jnp.var(x, axis=-1, keepdims=True)
            return (x - mu) * jax.lax.rsqrt(var + LN_EPS) * gamma + beta
        b, f, d = x.shape
        n = latents.shape[1]
        x = layernorm(x, gamma_media, beta_media)
        latents = layernorm(latents, gamma_lat, beta_lat)
        kv = jnp.concatenate((x, latents * kv_gate), axis=1)
        q = (latents @ Wq).reshape(b, n, HEADS, DIM_HEAD)
        k = (kv @ Wk).reshape(b, f + n, HEADS, DIM_HEAD)
        v = (kv @ Wv).reshape(b, f + n, HEADS, DIM_HEAD)
        sim = jnp.einsum('bqhd,bkhd->bhqk', q * SCALE, k)
        sim = sim - jax.lax.stop_gradient(jnp.max(sim, axis=-1, keepdims=True))
        valid_feat = ~key_padding_mask
        valid_full = jnp.concatenate((valid_feat, jnp.ones((b, n), dtype=bool)), axis=1)
        sim = jnp.where(valid_full[:, None, None, :], sim, NEG_INF)
        attn = jax.nn.softmax(sim, axis=-1)
        out = jnp.einsum('bhqk,bkhd->bqhd', attn, v).reshape(b, n, HEADS * DIM_HEAD)
        return out @ Wout

    def _L0_ffn_ref(hidden_states, gate_w, w1, w2, w3):
        import jax, jax.numpy as jnp
        import numpy as np
        B, S, H = (1, 256, 256)
        E, I = (8, 512)
        JITTER_EPS = 0.01

        def _sparse_mixer_top2(scores, jitter_eps):
            vals, idx = jax.lax.top_k(scores, 2)
            neg_inf = jnp.array(-jnp.inf, scores.dtype)
            t1 = vals[:, :1]
            f1 = jnp.maximum(jnp.abs(scores), t1)
            m1 = (t1 - scores) / f1 > 2 * jitter_eps
            p1 = jax.nn.softmax(jnp.where(m1, neg_inf, scores), axis=-1)
            mult1 = jnp.take_along_axis(p1, idx[:, :1], axis=-1)
            t2 = vals[:, 1:2]
            f2 = jnp.maximum(jnp.abs(scores), t2)
            m2 = (t2 - scores) / f2 > 2 * jitter_eps
            rows = jnp.arange(scores.shape[0])[:, None]
            s2 = scores.at[rows, idx[:, :1]].set(neg_inf)
            p2 = jax.nn.softmax(jnp.where(m2, neg_inf, s2), axis=-1)
            mult2 = jnp.take_along_axis(p2, idx[:, 1:2], axis=-1)
            return (jnp.concatenate([mult1, mult2], axis=-1), idx)
        b, s, h = hidden_states.shape
        x = hidden_states.reshape(-1, h)
        T = x.shape[0]
        logits = x @ gate_w.T
        mult, sel = _sparse_mixer_top2(logits, JITTER_EPS)
        rows = jnp.arange(T)[:, None]
        dense_w = jnp.zeros((T, E), x.dtype).at[rows, sel].set(mult)
        h1 = jnp.einsum('th,eih->eti', x, w1)
        h3 = jnp.einsum('th,eih->eti', x, w3)
        act = jax.nn.silu(h1) * h3
        y = jnp.einsum('eti,ehi->eth', act, w2)
        out = jnp.einsum('eth,te->th', y, dense_w)
        return out.reshape(b, s, h)

    def _L1_xattn_ref(x, latents, mask, g1, b1, g2, b2, Wq, Wkv, Wout):
        import jax, jax.numpy as jnp
        import numpy as np
        EPS = 1e-05

        def layer_norm(x, g, b):
            mu = jnp.mean(x, axis=-1, keepdims=True)
            var = jnp.mean((x - mu) ** 2, axis=-1, keepdims=True)
            return (x - mu) * jax.lax.rsqrt(var + EPS) * g + b
        heads, dim_head = (16, 64)
        b, n, D = x.shape
        l = latents.shape[1]
        xn = layer_norm(x, g1, b1)
        ln_lat = layer_norm(latents, g2, b2)
        q = ln_lat @ Wq
        kv = jnp.concatenate([xn, ln_lat], axis=1) @ Wkv
        k, v = jnp.split(kv, 2, axis=-1)

        def to_heads(t):
            return t.reshape(t.shape[0], t.shape[1], heads, dim_head).transpose(0, 2, 1, 3)
        q, k, v = (to_heads(q), to_heads(k), to_heads(v))
        scale = 1.0 / np.sqrt(np.sqrt(dim_head)).astype(np.float32)
        weight = jnp.einsum('bhld,bhnd->bhln', q * scale, k * scale)
        full_mask = jnp.concatenate([mask, jnp.ones((b, l), dtype=bool)], axis=1)
        neg = -jnp.finfo(weight.dtype).max
        weight = jnp.where(full_mask[:, None, None, :], weight, neg)
        weight = jax.nn.softmax(weight.astype(jnp.float32), axis=-1).astype(q.dtype)
        out = jnp.einsum('bhln,bhnd->bhld', weight, v)
        out = out.transpose(0, 2, 1, 3).reshape(b, l, heads * dim_head)
        return out @ Wout

    def _L1_ffn_ref(x, w1, conv_w, conv_b, w2):
        import jax, jax.numpy as jnp
        import numpy as np
        B, S, D_MODEL, D_HIDDEN = (4, 512, 256, 1024)

        def act_quant(x):
            scale = 127.0 / jnp.clip(jnp.max(jnp.abs(x), axis=-1, keepdims=True), 1e-05)
            return jnp.clip(jnp.round(x * scale), -128, 127) / scale

        def weight_quant(w):
            scale = 1.0 / jnp.clip(jnp.mean(jnp.abs(w)), 1e-05)
            return jnp.clip(jnp.round(w * scale), -1, 1) / scale

        def bit_linear(x, w):
            xq = x + jax.lax.stop_gradient(act_quant(x) - x)
            wq = w + jax.lax.stop_gradient(weight_quant(w) - w)
            return jnp.einsum('bsd,hd->bsh', xq, wq)

        def depthwise_conv1d(x_bcl, w, b):
            y = jax.lax.conv_general_dilated(x_bcl, w, window_strides=(1,), padding=[(1, 1)], dimension_numbers=('NCH', 'OIH', 'NCH'), feature_group_count=x_bcl.shape[1])
            return y + b[None, :, None]
        h = bit_linear(x, w1)
        h = depthwise_conv1d(h.transpose(0, 2, 1), conv_w, conv_b)
        h = h.transpose(0, 2, 1)
        h = jax.nn.silu(h)
        return bit_linear(h, w2)
    x = x + jnp.tanh(g_xattn[0]) * _L0_xattn_ref(ctx_1024, _layernorm(x, axis=-1), mask_BxS2_bk0, L0_xattn_kv_gate, L0_xattn_gamma_media, L0_xattn_beta_media, L0_xattn_gamma_lat, L0_xattn_beta_lat, L0_xattn_Wq, L0_xattn_Wk, L0_xattn_Wv, L0_xattn_Wout)
    x = x + jnp.tanh(g_ffn[0]) * _L0_ffn_ref(_layernorm(x, axis=-1), L0_ffn_gate_w, L0_ffn_w1, L0_ffn_w2, L0_ffn_w3)
    x = x + jnp.tanh(g_xattn[1]) * _L1_xattn_ref(ctx_1024, _layernorm(x, axis=-1), mask_BxS2_bk0, L1_xattn_g1, L1_xattn_b1, L1_xattn_g2, L1_xattn_b2, L1_xattn_Wq, L1_xattn_Wkv, L1_xattn_Wout)
    x = x + jnp.tanh(g_ffn[1]) * _L1_ffn_ref(_layernorm(x, axis=-1), L1_ffn_w1, L1_ffn_conv_w, L1_ffn_conv_b, L1_ffn_w2)
    return x

_drawn_inputs = setup_inputs


def setup_inputs(seed=0):
    import zlib

    import numpy as np

    out = dict(_drawn_inputs(seed))
    spreads = {'g_ffn': (-1.0, 0.6),
     'L0_xattn_gamma_media': (1.0, 0.2),
     'L0_xattn_beta_media': (0.0, 0.1),
     'L0_xattn_gamma_lat': (1.0, 0.2),
     'L0_xattn_beta_lat': (0.0, 0.1),
     'L1_xattn_g1': (1.0, 0.2),
     'L1_xattn_b1': (0.0, 0.303),
     'L1_xattn_g2': (1.0, 0.2),
     'L1_xattn_b2': (0.0, 0.1)}
    factors = {}
    for name, (base, spread) in spreads.items():
        noise = np.random.default_rng([zlib.crc32(name.encode()), seed]).standard_normal(out[name].shape)
        drawn = base * np.exp(spread * noise) if base else spread * noise
        out[name] = jnp.asarray(drawn.astype(out[name].dtype))
    for name, factor in factors.items():
        out[name] = (out[name] * factor).astype(out[name].dtype)
    return out
```

```python
from contextlib import ExitStack

import concourse.bass as bass
from concourse import mybir

F32 = mybir.dt.float32
F16 = mybir.dt.float16
BF16 = mybir.dt.bfloat16
U8 = mybir.dt.uint8
ALU = mybir.AluOpType
ACT = mybir.ActivationFunctionType
AX = mybir.AxisListType

NSEQ, TOK, DIM = 16, 112, 256
CTX = 375
CT, CP = 3, 125
KEYS = TOK + CTX
KW = 488
KB = 2
HEADS, HD = 8, 64
PAIRS = 4
EXPERTS, EB = 8, 4
FB = 8
CHUNK = 512
WSCALE = 64.0
LN_EPS = 1e-5
MASKED = 1e30
ROUND = 12582912.0
QMAX = 127.0
QMIN_SCALE = 1e-5
JITTER = 0.02

L0_Q, L0_K, L0_V, L0_O = 0, 2, 4, 6
MOE0 = 8
MOE_CHUNKS = 6
L1_Q = MOE0 + EXPERTS * MOE_CHUNKS
L1_K, L1_V, L1_O = L1_Q + 4, L1_Q + 8, L1_Q + 12
CHUNKS = L1_Q + 16
SHIFT = 2
FFN_WORDS = (KB * FB * 128 + FB * DIM) // 2

V_GAMMA, V_BETA, V_GLAT, V_BLAT = 0, 2, 4, 6
V_CONVW, V_CONVB = 16, 16 + 3 * FB
NVEC = V_CONVB + FB

OFFSET = {"P": 0, "A": 1, "M": 2, "B": 3, "F": 4}
LOOP = (5, 16)
LAST = NSEQ + OFFSET["F"]
SLOTS = 26

UNITS = {"A": HEADS, "B": 2 * HEADS}
PAIR = {"A": PAIRS, "B": 2 * PAIRS}
GROUP = {"A": 1, "B": 2}
HALVES = {"M": 2 * EXPERTS}


class Iteration:

    def __init__(self, n, like):
        self.n, self.like = n, like
        self.on = {s for s, o in OFFSET.items() if o <= like < o + NSEQ}
        self.tasks = timeline(self.on)
        flat = [t for slot in self.tasks for t in slot]
        self.x0 = [t for t in flat if t[0] in ("q", "m_gate", "m_down")]
        self.x1 = [t for t in flat if t[0] in X1_TASKS]
        self.units = sum(UNITS[s] for s in "AB" if s in self.on)

    def at(self, per, local=0):
        if isinstance(self.n, int):
            past = {s: min(max(self.n - OFFSET[s], 0), NSEQ) for s in per}
            return max(0, sum(k * past[s] for s, k in per.items()) + local)
        slope = sum(per.values())
        return self.n * slope + (local - sum(k * OFFSET[s] for s, k in per.items()))

    def x0_at(self, task, local=1):
        return self.at(X0_PER, self.x0.index(task) + local)

    def x1_at(self, task, local=1):
        return self.at(X1_PER, self.x1.index(task) + local)

    def seq(self, stage):
        return self.n - OFFSET[stage]

    def group_of(self, unit):
        return self.pair_group(unit // 2)

    def pair_group(self, pair):
        if "A" in self.on:
            if pair < PAIRS:
                return 0, 0, pair
            pair -= PAIRS
        return 1, pair // PAIRS, pair % PAIRS


X1_TASKS = ("p_turn", "p_lat", "b_turn", "b_lat", "o_turn", "o_proj", "m_turn",
            "f_turn", "f_up", "f_max", "f_rate", "f_down")
X0_PER = {"A": PAIRS, "B": 2 * PAIRS, "M": 1 + EXPERTS}
X1_PER = {"P": 3, "B": 3 + 2, "A": 2, "M": 1, "F": 2 + 7}


def timeline(on):
    slots = [[] for _ in range(SLOTS + 2)]

    def put(slot, *task):
        slots[slot].append(task)

    pairs = sum(PAIR[s] for s in "AB" if s in on)
    early = "A" not in on
    if "M" in on:
        put(0, "m_norm")
        put(0 if early else 1, "m_turn")
    if "F" in on:
        put(0 if early else 1, "o_turn", "F")
        put(0 if early else 2, "o_proj", "F")
        put(0 if early else 2, "f_norm")
    if "B" in on:
        put(0 if early else 3, "b_norm")
        for kb in range(KB):
            put(0 if early else 4 + kb, "b_turn", kb)
        put(0 if early else 6, "b_lat")
    for p in range(pairs):
        slot = 2 * p - 1 if p else 0
        put(slot, "q", p)
        put(slot, "k", p)
        put(slot + 1 if p else 0, "v", p)
    if "M" in on:
        put(2, "m_gate")
        for h in range(2 * EXPERTS):
            slot = 3 + h * 21 // 16
            put(slot, "m_up", h)
            if h % 2 == 0 and h:
                put(slot, "m_down", h // 2 - 1)
        put(24, "m_down", EXPERTS - 1)
    if "F" in on:
        put(4, "f_turn")
        put(6, "f_up", 0)
        put(8, "f_act", 0)
        put(9, "f_up", 1)
        put(10, "f_max", 0)
        put(12, "f_act", 1)
        put(14, "f_max", 1)
        put(16, "f_rate")
        put(18, "f_down")
    if "A" in on:
        put(11, "o_turn", "A")
        put(12, "o_proj", "A")
    if "B" in on:
        first = HEADS if "A" in on else 0
        put(first + HEADS + 3, "o_turn", "B")
        put(first + HEADS + 4, "o_proj", "B")
    if "P" in on:
        put(13, "p_norm")
        for kb in range(KB):
            put(14 + kb, "p_turn", kb)
        put(16, "p_lat")
    return slots


def build(nc, x_in, ctx_in, mask_in, weights_in, ffn_in, vectors_in, router_in, gates_in, out):
    with ExitStack() as stack:
        def sb(name, shape, dt=F32):
            return stack.enter_context(nc.sbuf_tensor(name, shape, dt))

        def ps(name):
            return stack.enter_context(nc.psum_tensor(name, [128, 512], F32))

        def sem(name):
            return stack.enter_context(nc.semaphore(name))

        W = sb("weights", [128, CHUNKS * CHUNK + FFN_WORDS])
        WH = W[:].bitcast(F16)
        ffn0 = CHUNKS * 2 * CHUNK
        w_up = WH[:, ffn0:ffn0 + KB * FB * 128].rearrange("p (k c) -> p k c", k=KB)
        w_down = WH[:, ffn0 + KB * FB * 128:ffn0 + KB * FB * 128 + FB * DIM].rearrange(
            "p (k c) -> p k c", k=FB)
        vec = sb("vectors", [128, NVEC])
        gates = sb("gates", [128, 5])
        tgate = sb("tanh_gates", [128, 4])
        tgs = sb("tanh_gates_unscaled", [128, 4])
        router = sb("router", [128, KB, EXPERTS])
        idf = sb("identity_f32", [128, 128])
        idh = sb("identity_f16", [128, 128], F16)
        minus_half = sb("minus_half", [128, 4])
        eps = sb("eps", [128, 4])
        ones = sb("ones", [128, 1])
        rev = sb("rev_index", [TOK, EXPERTS])
        wabs = sb("weight_abs_sums", [128, 8])
        wtot = sb("weight_abs_total", [128, 2])
        wmean = sb("weight_means", [128, 2])
        winv = sb("weight_inverse_means", [128, 2])
        qfac = sb("dequant_factors", [128, 2])

        kv = {0: sb("kv_A", [128, KB, 2, 512], F16), 1: sb("kv_B", [128, KB, 2, 512], F16)}
        latq = sb("latents_A", [128, KB, 2, TOK], F16)
        kT = sb("keys", [128, 2, 2, KW], F16)
        vN = sb("values", [128, 2, 2, 4, 128], F16)
        qT = sb("queries", [128, 2, 2, 2, 128], F16)
        S = sb("scores", [128, 2, KEYS + 1])
        PR = sb("probs", [128, 2, 512], F16)
        PT = sb("probs_turned", [128, 2, 4, 128], F16)
        mask = {0: sb("mask_A", [TOK, KEYS + 1], BF16), 1: sb("mask_B", [TOK, KEYS + 1], BF16)}
        mask8 = sb("mask_bytes", [TOK, CTX], U8)
        rmin = sb("score_min", [128, 2])
        rsum = sb("prob_sums", [128, 3, HEADS])
        rinv = sb("prob_sum_inverse", [128, HEADS])
        wide = sb("wide", [128, 512])
        oT = sb("heads_turned", [128, 2, 4, 128], F16)
        ctxb = sb("context", [128, CT, DIM])
        xa = sb("x_A", [TOK, DIM])
        x1 = sb("x_after_A", [TOK, DIM])
        xm = sb("x_M", [TOK, DIM])
        xb = sb("x_B", [TOK, DIM])
        xf = sb("x_F", [TOK, DIM])
        xn = sb("x_normed", [TOK, DIM])
        bn = sb("bn_stats", [128, 4, 6])
        mv = {s: sb(f"mean_var_{s}", [128, 4, 2]) for s in "PBMF"}
        rs = {s: sb(f"rstd_{s}", [128, 6]) for s in "PBMF"}
        xmF = sb("moe_in_f32", [128, KB, TOK])
        xmT = sb("moe_in", [128, 2, KB, TOK], F16)
        act = sb("moe_hidden_f32", [128, 2 * TOK])
        aT = sb("moe_hidden", [128, 2, EB, 128], F16)
        lg = sb("logits", [TOK, EXPERTS])
        rk = sb("route_ranks", [TOK, 2, EXPERTS])
        one = sb("route_onehot", [TOK, 2, EXPERTS])
        sh = sb("route_shifted", [TOK, 2, EXPERTS])
        gk = sb("route_keep", [TOK, 2, EXPERTS])
        s2 = sb("logits_without_first", [TOK, EXPERTS])
        rsc = sb("route_scalars", [TOK, 8])
        dw = sb("dense_weights", [TOK, EXPERTS])
        hpad = sb("ffn_hidden_padded", [128, 4, TOK + 2])
        hact = sb("ffn_hidden", [128, FB, TOK])
        q2T = hpad[:].rearrange("p a b -> p (a b)").bitcast(F16)[:, 0:FB * TOK].rearrange(
            "p (k t) -> p k t", k=FB)
        xqT = sb("ffn_in_quantised", [128, KB, TOK], F16)
        rate = sb("ffn_rate", [128, TOK])
        fs = sb("ffn_scalars", [TOK, 8])
        xqh = sb("x_quantised", [TOK, DIM], F16)
        hact_flat = hact[:].rearrange("p a b -> p (a b)")
        kvb_flat = kv[1][:].rearrange("p a b c -> p (a b c)").bitcast(F32)
        staging = [hact_flat[:, 0:CHUNK], kvb_flat[:, 0:CHUNK], kvb_flat[:, CHUNK:2 * CHUNK]]

        bS, bT, bO, bK, bV, bH, bX0, bX1 = (ps(n) for n in (
            "bank_scores", "bank_turn", "bank_out", "bank_keys", "bank_values", "bank_hidden",
            "bank_x0", "bank_x1"))
        bT16 = bT[:].bitcast(F16)[:, 0:2 * 4 * TOK].rearrange("p (a t c) -> p a t c", a=2, t=4)
        bX1h = bX1[:].bitcast(F16)

        consts_set = sem("consts_set")
        zeros_set = sem("zeros_set")
        vectors_loaded = sem("vectors_loaded")
        gates_ready = sem("gates_ready")
        gates_scaled = sem("gates_scaled")
        w_loaded = [sem(f"weights_loaded_{i}") for i in range(3)]
        w_hi, w_split = sem("weights_hi"), sem("weights_split")
        raw_loaded = [sem(f"ffn_raw_loaded_{i}") for i in range(3)]
        raw_used = sem("ffn_raw_used")
        wsum_ready, wsum_spread, ffn_w_ready = sem("wsum_ready"), sem("wsum_spread"), sem("ffn_w_ready")
        p_loaded, b_loaded = sem("p_loaded"), sem("b_loaded")
        stored = sem("stored")

        stats_ready = {s: sem(f"stats_ready_{s}") for s in "PBMF"}
        rstd_ready = {s: sem(f"rstd_ready_{s}") for s in "PBMF"}
        norm_ready = {s: sem(f"norm_ready_{s}") for s in "PBM"}
        kv_hi = {0: sem("kv_hi_A"), 1: sem("kv_hi_B")}
        kv_ready = {0: sem("kv_ready_A"), 1: sem("kv_ready_B")}
        lat_ready = {0: sem("lat_ready_A"), 1: sem("lat_ready_B")}

        k_ready, k_hi, k_split = sem("k_ready"), sem("k_hi"), sem("k_split")
        v_ready, v_hi, v_split = sem("v_ready"), sem("v_hi"), sem("v_split")
        q_hi = sem("q_hi")
        scores_ready, scores_masked = sem("scores_ready"), sem("scores_masked")
        probs_ready, probs_split = sem("probs_ready"), sem("probs_split")
        probs_turned, turned_copied = sem("probs_turned"), sem("turned_copied")
        values_summed = sem("values_summed")
        out_normed, o_hi, x1_ready = sem("out_normed"), sem("o_hi"), sem("x1_ready")

        moe_hi, moe_ready = sem("moe_hi"), sem("moe_ready")
        route_shifted, route_exp = sem("route_shifted"), sem("route_exp")
        up_ready, tanh_ready = sem("up_ready"), sem("tanh_ready")
        gated, act_split = sem("gated"), sem("act_split")
        x0_filled, x0_drained = sem("x0_filled"), sem("x0_drained")
        x1_filled, x1_drained = sem("x1_filled"), sem("x1_drained")
        xq_ready = sem("xq_ready")
        conv_begun, conv_done, ffn_tanh, ffn_act = (
            sem("conv_begun"), sem("conv_done"), sem("ffn_tanh"), sem("ffn_act"))
        rate_ready, q2_ready, out_ready = sem("rate_ready"), sem("q2_ready"), sem("out_ready")

        def w(chunk, part, col, n):
            at = (2 * chunk + part) * CHUNK + col
            return WH[:, at:at + n]

        def layer_chunks(layer, group):
            if layer == 0:
                return L0_Q, L0_K, L0_V, L0_O, 1
            return L1_Q + group, L1_K + group, L1_V + group, L1_O + 2 * group, 2

        PASSES = ((0, 0), (0, 1), (1, 0))

        def every_iteration(eng, body, between):
            for n in range(LOOP[0]):
                between(n)
                body(Iteration(n, n))
            with eng.Fori(LOOP[0], LOOP[1]) as n:
                body(Iteration(n, LOOP[0]))
            for n in range(LOOP[1], LAST):
                body(Iteration(n, n))

        block = stack.enter_context(nc.Block())

        @block.sync
        def _(sp):
            sp.dma_start(vec[:], vectors_in).then_inc(vectors_loaded, 16)
            sp.dma_start(gates[:], gates_in.to_broadcast([128, 5])).then_inc(vectors_loaded, 16)
            sp.dma_start(router[:], router_in).then_inc(vectors_loaded, 16)

            def load_p(it):
                b = it.seq("P")
                sp.wait_ge(x1_ready, it.at({"A": 1}, 1 if "A" in it.on else 0))
                if "B" in it.on:
                    sp.wait_ge(x1_drained, it.x1_at(("b_turn", KB - 1)))
                elif it.like > 0:
                    before = Iteration(it.n - 1, it.like - 1)
                    sp.wait_ge(x1_drained, before.x1_at(("p_turn", KB - 1)))
                sp.dma_start(xa[:], x_in[b]).then_inc(p_loaded, 16)
                sp.dma_start(ctxb[0:CP], ctx_in[b].rearrange("(t p) d -> p t d", p=CP)).then_inc(p_loaded, 16)
                sp.dma_start(mask8[:], mask_in[b].to_broadcast([TOK, CTX])).then_inc(p_loaded, 16)

            def load_b(it):
                b = it.seq("B")
                before = Iteration(it.n - 1, it.like - 1 if isinstance(it.n, int) else it.like)
                last = ("p_turn", KB - 1) if "P" in before.on else ("b_turn", KB - 1)
                sp.wait_ge(x1_drained, before.x1_at(last))
                sp.dma_start(ctxb[0:CP], ctx_in[b].rearrange("(t p) d -> p t d", p=CP)).then_inc(b_loaded, 16)
                sp.dma_start(mask8[:], mask_in[b].to_broadcast([TOK, CTX])).then_inc(b_loaded, 16)

            def body(it):
                if "B" in it.on:
                    load_b(it)
                for slot in it.tasks:
                    for task in slot:
                        if task[0] == "p_norm":
                            load_p(it)
                        if task[0] == "f_down":
                            sp.wait_ge(out_ready, it.at({"F": 1}, 1))
                            sp.dma_start(out[it.seq("F")], xf[:]).then_inc(stored, 16)

            def between(n):
                if n == 1:
                    for i, (a, b) in enumerate(((0, MOE0), (MOE0, L1_Q), (L1_Q, CHUNKS))):
                        sp.dma_start(W[:, (a + SHIFT) * CHUNK:(b + SHIFT) * CHUNK],
                                     weights_in[:, a * CHUNK:b * CHUNK]).then_inc(w_loaded[i], 16)
                if n == 3:
                    for c in range(16):
                        if c >= 3:
                            sp.wait_ge(raw_used, c - 2)
                        sp.dma_start(staging[c % 3], ffn_in[:, (c % 8) * CHUNK:(c % 8 + 1) * CHUNK])\
                            .then_inc(raw_loaded[c % 3], 16)

            every_iteration(sp, body, between)
            sp.wait_ge(stored, 16 * NSEQ)

        @block.gpsimd
        def _(pool):
            pool.memset(idf[:], 0.0)
            pool.memset(idh[:], 0.0)
            pool.memset(ones[:], 1.0)
            pool.memset(minus_half[:], -0.5)
            pool.memset(eps[:], LN_EPS)
            pool.iota(rev[:], pattern=[[-1, EXPERTS]], base=EXPERTS, channel_multiplier=0,
                      allow_small_or_imprecise_dtypes=True)
            pool.drain()
            for m in (idf, idh):
                last = pool.affine_select(out=m[:], in_=m[:], compare_op=ALU.not_equal, fill=1.0,
                                          base=0, pattern=[[-1, 128]], channel_multiplier=1)
            last.then_inc(consts_set, 1)
            for s in "PBMF":
                last = pool.memset(mv[s][:], 1.0)
            last.then_inc(consts_set, 1)

            def rstd(stage, it, cols, twice):
                m, r = mv[stage], rs[stage]
                pool.wait_ge(stats_ready[stage], it.at({stage: 1}, 1))
                pool.tensor_tensor(r[:, 0:cols], m[:, 0:cols, 1], eps[:, 0:cols], ALU.add)
                pool.drain()
                last = pool.tensor_tensor(r[:, 0:cols], r[:, 0:cols], minus_half[:, 0:cols], ALU.pow)
                if twice:
                    c = cols - 1
                    pool.drain()
                    pool.tensor_tensor(r[:, 4:5], m[:, c, 1:2], r[:, c:c + 1], ALU.mult)
                    pool.drain()
                    pool.tensor_tensor(r[:, 4:5], r[:, 4:5], r[:, c:c + 1], ALU.mult)
                    pool.drain()
                    pool.tensor_scalar(r[:, 4:5], r[:, 4:5], LN_EPS, None, ALU.add)
                    pool.drain()
                    pool.tensor_tensor(r[:, 4:5], r[:, 4:5], minus_half[:, 0:1], ALU.pow)
                    pool.drain()
                    last = pool.tensor_tensor(r[:, c:c + 1], r[:, c:c + 1], r[:, 4:5], ALU.mult)
                last.then_inc(rstd_ready[stage], 1)

            def body(it):
                for slot in it.tasks:
                    for task in slot:
                        name = task[0]
                        if name in ("p_norm", "b_norm"):
                            rstd(name[0].upper(), it, CT + 1, True)
                        elif name in ("m_norm", "f_norm"):
                            rstd(name[0].upper(), it, 1, False)
                        elif name == "m_up":
                            h = task[1]
                            m0 = 2 * (h % 2)
                            f = act[:].rearrange("p (m t) -> p m t", m=2)
                            made = pool.to_reg(it.at(HALVES, h + 1))
                            if h >= 2:
                                multiplied = pool.to_reg(it.x0_at(("m_down", h // 2 - 1)))
                            pool.wait_ge(zeros_set, 1)
                            if h >= 2:
                                pool.wait_ge(x0_filled, multiplied)
                            pool.wait_ge(gated, made)
                            pool.tensor_copy(aT[:, 0, m0:m0 + 2, 0:TOK], f)
                            pool.drain()
                            pool.tensor_tensor(aT[:, 1, m0:m0 + 2, 0:TOK], f, aT[:, 0, m0:m0 + 2, 0:TOK],
                                               ALU.subtract).then_inc(act_split, 1)

            every_iteration(pool, body, lambda n: None)

        @block.scalar
        def _(act_e):
            act_e.wait_ge(vectors_loaded, 48)
            act_e.activation(tgate[:], gates[:, 0:4], ACT.Tanh).then_inc(gates_ready, 1)

            def split_weights(a, b):
                for c in range(a, b):
                    act_e.wait_ge(w_split, max(0, c - SHIFT + 1))
                    act_e.activation(w(c, 0, 0, CHUNK), W[:, (c + SHIFT) * CHUNK:(c + SHIFT + 1) * CHUNK],
                                     ACT.Copy, scale=WSCALE).then_inc(w_hi, 1)

            def split_experts():
                with act_e.Fori(0, EXPERTS) as e:
                    for i in range(MOE_CHUNKS):
                        c = e * MOE_CHUNKS + (MOE0 + i)
                        act_e.wait_ge(w_split, c - (SHIFT - 1))
                        act_e.activation(WH[:, bass.ds(c * (2 * CHUNK), CHUNK)],
                                         W[:, bass.ds((c + SHIFT) * CHUNK, CHUNK)],
                                         ACT.Copy, scale=WSCALE).then_inc(w_hi, 1)

            def between(n):
                if n == 1:
                    act_e.wait_ge(w_loaded[0], 16)
                    split_weights(0, MOE0)
                if n == 2:
                    act_e.wait_ge(w_loaded[1], 16)
                    split_experts()
                if n == 3:
                    act_e.wait_ge(w_loaded[2], 16)
                    split_weights(L1_Q, CHUNKS)

            def turned_copy(it, k):
                act_e.wait_ge(probs_turned, it.at(UNITS, k + 1))
                act_e.wait_ge(values_summed, it.at(UNITS, k))
                act_e.activation(PT[:, :, :, 0:TOK], bT16, ACT.Copy).then_inc(turned_copied, 1)

            def exp(it, k):
                layer, group, _ = it.group_of(k)
                g = layer + group
                act_e.wait_ge(scores_masked, it.at(UNITS, k + 1))
                act_e.activation(S[0:TOK, k % 2, 0:KEYS], S[0:TOK, k % 2, 0:KEYS], ACT.Exp,
                                 bias=rmin[0:TOK, k % 2:k % 2 + 1], scale=-1.0,
                                 accum_out=rsum[0:TOK, g, k % HEADS:k % HEADS + 1]).then_inc(probs_ready, 1)

            def part(it, task):
                name = task[0]
                if name == "q":
                    p = task[1]
                    act_e.wait_ge(x0_filled, it.x0_at(task))
                    act_e.wait_ge(scores_ready, it.at(UNITS, 2 * p - 2))
                    for h in range(2):
                        r = slice(64 * h, 64 * h + 64)
                        last = act_e.activation(qT[r, p % 2, h, 0, 0:TOK], bX0[r, 0:TOK], ACT.Copy,
                                                scale=-0.125 / WSCALE)
                    last.then_inc(q_hi, 1)
                elif name == "k":
                    p = task[1]
                    act_e.wait_ge(k_ready, it.at(PAIR, p + 1))
                    act_e.wait_ge(scores_ready, it.at(UNITS, 2 * p - 2))
                    act_e.activation(kT[:, p % 2, 0, :], bK[:, 0:KW], ACT.Copy, scale=1 / WSCALE)\
                        .then_inc(k_hi, 1)
                elif name == "v":
                    p = task[1]
                    act_e.wait_ge(v_ready, it.at(PAIR, p + 1))
                    act_e.wait_ge(values_summed, it.at(UNITS, 2 * p - 2))
                    act_e.activation(vN[:, p % 2, 0], bV[:].rearrange("p (t d) -> p t d", t=4), ACT.Copy,
                                     scale=1 / WSCALE).then_inc(v_hi, 1)
                elif name in ("p_turn", "b_turn"):
                    layer, kb = int(name == "b_turn"), task[1]
                    stage = "PB"[layer]
                    act_e.wait_ge(x1_drained, it.x1_at(task))
                    act_e.activation(kv[layer][:, kb, 0, TOK:KEYS], wide[:, 0:CTX], ACT.Copy)\
                        .then_inc(kv_hi[layer], 1)
                elif name in ("p_lat", "b_lat"):
                    layer = int(name == "b_lat")
                    stage = "PB"[layer]
                    act_e.wait_ge(lat_ready[layer], it.at({stage: 1}, 1))
                    lat = wide[:, 0:KB * TOK].rearrange("p (k t) -> p k t", k=KB)
                    if layer == 0:
                        gatedlat = wide[:, KB * TOK:2 * KB * TOK].rearrange("p (k t) -> p k t", k=KB)
                        act_e.activation(latq[:, :, 0, :], lat, ACT.Copy)
                        lat = gatedlat
                    act_e.activation(kv[layer][:, :, 0, 0:TOK], lat, ACT.Copy).then_inc(kv_hi[layer], 1)
                elif name == "o_turn":
                    act_e.wait_ge(x1_filled, it.x1_at(task))
                    act_e.activation(oT[:, 0, :, 0:TOK], bX1[:, 0:4 * TOK].rearrange("p (m t) -> p m t", m=4),
                                     ACT.Copy).then_inc(o_hi, 1)
                elif name == "m_turn":
                    act_e.wait_ge(x1_drained, it.x1_at(task))
                    act_e.activation(xmT[:, 0], xmF[:], ACT.Copy).then_inc(moe_hi, 1)
                elif name == "m_gate":
                    act_e.wait_ge(route_shifted, it.at({"M": 1}, 1))
                    act_e.activation(sh[:], sh[:], ACT.Exp).then_inc(route_exp, 1)
                elif name == "m_up":
                    h = task[1]
                    act_e.wait_ge(up_ready, it.at(HALVES, h + 1))
                    act_e.wait_ge(act_split, it.at(HALVES, h))
                    act_e.activation(act[:], bH[:, 0:2 * TOK], ACT.Tanh, scale=0.5 / WSCALE).then_inc(tanh_ready, 1)
                elif name == "f_up":
                    j = task[1]
                    act_e.wait_ge(x1_drained, it.x1_at(task))
                    for i in range(4):
                        b = 4 * j + i
                        last = act_e.activation(hact[:, b, :], hpad[:, i, 0:TOK], ACT.Identity,
                                                scale=vec[:, V_CONVW + b:V_CONVW + b + 1],
                                                bias=vec[:, V_CONVB + b:V_CONVB + b + 1])
                    last.then_inc(conv_begun, 1)
                elif name == "f_act":
                    j = task[1]
                    act_e.wait_ge(conv_done, it.at({"F": 2}, j + 1))
                    act_e.activation(hpad[:, :, 1:TOK + 1], hact[:, 4 * j:4 * j + 4, :], ACT.Tanh, scale=0.5)\
                        .then_inc(ffn_tanh, 1)

            def body(it):
                for s, slot in enumerate(it.tasks):
                    k = s - 1
                    if 0 <= k < it.units:
                        exp(it, k)
                    for task in slot:
                        part(it, task)
                    if 1 <= k <= it.units:
                        turned_copy(it, k - 1)

            every_iteration(act_e, body, between)

        @block.tensor
        def _(pe):
            pe.wait_ge(consts_set, 2)
            pe.wait_ge(zeros_set, 1)

            def proj_q(it, p):
                layer, group, j = it.pair_group(p)
                wq, _, _, _, step = layer_chunks(layer, group)
                pe.wait_ge(x0_drained, it.x0_at(("q", p), 0))
                n = 0
                for kb in range(KB):
                    for a, b in PASSES:
                        rhs = latq[:, kb, b, :] if layer == 0 else kv[1][:, kb, b, 0:TOK]
                        last = pe.matmul(bX0[:, 0:TOK], w(wq + kb * step, a, 128 * j, 128), rhs,
                                         start=n == 0, stop=n == 5)
                        n += 1
                last.then_inc(x0_filled, 1)

            def proj_k(it, p):
                layer, group, j = it.pair_group(p)
                _, wk, _, _, step = layer_chunks(layer, group)
                pe.wait_ge(k_split, it.at(PAIR, p))
                n = 0
                for kb in range(KB):
                    for a, b in PASSES:
                        last = pe.matmul(bK[:, 0:KW], w(wk + kb * step, a, 128 * j, 128),
                                         kv[layer][:, kb, b, 0:KW], start=n == 0, stop=n == 5)
                        n += 1
                last.then_inc(k_ready, 1)

            def proj_v(it, p):
                layer, group, j = it.pair_group(p)
                _, _, wv, _, step = layer_chunks(layer, group)
                pe.wait_ge(v_split, it.at(PAIR, p))
                for t in range(4):
                    n = 0
                    for kb in range(KB):
                        for a, b in PASSES:
                            last = pe.matmul(bV[:, 128 * t:128 * t + 128],
                                             kv[layer][:, kb, a, 128 * t:128 * t + 128],
                                             w(wv + kb * step, b, 128 * j, 128),
                                             start=n == 0, stop=n == 5)
                            n += 1
                last.then_inc(v_ready, 1)

            def scores(it, k):
                p, h = k // 2, k % 2
                pe.wait_ge(x0_drained, it.x0_at(("q", p)))
                pe.wait_ge(k_split, it.at(PAIR, p + 1))
                pe.wait_ge(scores_masked, it.at(UNITS, k))
                for n, (a, b) in enumerate(PASSES):
                    last = pe.matmul(bS[:, 0:KW], qT[:, p % 2, h, a, :], kT[:, p % 2, b, :],
                                     start=n == 0, stop=n == 2)
                last.then_inc(scores_ready, 1)

            def turn_probs(it, k):
                pe.wait_ge(probs_split, it.at(UNITS, k + 1))
                pe.wait_ge(turned_copied, it.at(UNITS, k))
                for a in range(2):
                    for t in range(4):
                        last = pe.transpose(bT16[:, a, t, :], PR[0:TOK, a, 128 * t:128 * t + 128],
                                            idh[0:TOK, 0:TOK])
                last.then_inc(probs_turned, 1)

            def sum_values(it, k):
                p, h = k // 2, k % 2
                pe.wait_ge(turned_copied, it.at(UNITS, k + 1))
                pe.wait_ge(v_split, it.at(PAIR, p + 1))
                if k % HEADS == 0:
                    pe.wait_ge(out_normed, it.at(GROUP, k // HEADS))
                n = 0
                col = HD * (k % HEADS)
                for t in range(4):
                    for a, b in PASSES:
                        last = pe.matmul(bO[:, col:col + HD], PT[:, a, t, :],
                                         vN[:, p % 2, b, t, HD * h:HD * h + HD], start=n == 0, stop=n == 11)
                        n += 1
                last.then_inc(values_summed, 1)

            def group_of_task(it, stage):
                if stage == "A":
                    return 0, 0, it.at(GROUP, 1)
                if stage == "B":
                    return 1, 0, it.at(GROUP, 2 if "A" in it.on else 1)
                return 1, 1, it.at(GROUP, 0)

            def part(it, task):
                name = task[0]
                if name in ("q", "k", "v"):
                    p = task[1]
                    layer, _, j = it.pair_group(p)
                    if name == "q" and (p == 0 or (p == PAIRS and "A" in it.on)):
                        stage = "PB"[layer]
                        pe.wait_ge(kv_ready[layer], it.at({stage: 1}, layer))
                    {"q": proj_q, "k": proj_k, "v": proj_v}[name](it, p)
                    return
                if name in X1_TASKS:
                    pe.wait_ge(x1_drained, it.x1_at(task, 0))
                if name in ("p_turn", "b_turn"):
                    stage, kb = name[0].upper(), task[1]
                    pe.wait_ge(norm_ready[stage], it.at({stage: 2}, 1))
                    for t in range(CT):
                        last = pe.transpose(bX1[:, CP * t:CP * t + CP], ctxb[0:CP, t, 128 * kb:128 * kb + 128],
                                            idf[0:CP, 0:CP])
                    last.then_inc(x1_filled, 1)
                elif name in ("p_lat", "b_lat", "m_turn"):
                    stage = name[0].upper()
                    pe.wait_ge(norm_ready[stage], it.at({stage: 1 if stage == "M" else 2},
                                                        1 if stage == "M" else 2))
                    for kb in range(KB):
                        last = pe.transpose(bX1[:, TOK * kb:TOK * kb + TOK], xn[:, 128 * kb:128 * kb + 128],
                                            idf[0:TOK, 0:TOK])
                    last.then_inc(x1_filled, 1)
                elif name == "o_turn":
                    pe.wait_ge(out_normed, group_of_task(it, task[1])[2])
                    for m in range(4):
                        last = pe.transpose(bX1[:, TOK * m:TOK * m + TOK], wide[0:TOK, 128 * m:128 * m + 128],
                                            idf[0:TOK, 0:TOK])
                    last.then_inc(x1_filled, 1)
                elif name == "o_proj":
                    layer, group, _ = group_of_task(it, task[1])
                    wo = layer_chunks(layer, group)[3]
                    n = 0
                    for m in range(4):
                        for a, b in PASSES:
                            last = pe.matmul(bX1[:, 0:DIM], oT[:, a, m, :],
                                             w(wo + m // 2, b, DIM * (m % 2), DIM), start=n == 0, stop=n == 11)
                            n += 1
                    last.then_inc(x1_filled, 1)
                elif name == "m_gate":
                    pe.wait_ge(x0_drained, it.x0_at(task, 0))
                    pe.wait_ge(x1_drained, it.x1_at(("m_turn",)))
                    for kb in range(KB):
                        last = pe.matmul(bX0[0:TOK, 0:EXPERTS], xmF[:, kb, :], router[:, kb, :],
                                         start=kb == 0, stop=kb == 1)
                    last.then_inc(x0_filled, 1)
                elif name == "m_up":
                    h = task[1]
                    e = h // 2
                    if h == 0:
                        pe.wait_ge(moe_ready, it.at({"M": 1}, 1))
                    pe.wait_ge(gated, it.at(HALVES, h))
                    first = MOE0 + MOE_CHUNKS * e
                    for i in range(4):
                        mat, m = i // 2, 2 * (h % 2) + i % 2
                        n = 0
                        for kb in range(KB):
                            for a, b in PASSES:
                                last = pe.matmul(bH[:, TOK * i:TOK * i + TOK],
                                                 w(first + 2 * mat + kb, a, 128 * m, 128), xmT[:, b, kb, :],
                                                 start=n == 0, stop=n == 5)
                                n += 1
                    last.then_inc(up_ready, 1)
                elif name == "m_down":
                    e = task[1]
                    pe.wait_ge(x0_drained, it.x0_at(task, 0))
                    pe.wait_ge(act_split, it.at(HALVES, 2 * e + 2))
                    first = MOE0 + MOE_CHUNKS * e + 4
                    n = 0
                    for m in range(EB):
                        for a, b in PASSES:
                            last = pe.matmul(bX0[:, 0:DIM], aT[:, a, m, :],
                                             w(first + m // 2, b, DIM * (m % 2), DIM), start=n == 0, stop=n == 11)
                            n += 1
                    last.then_inc(x0_filled, 1)
                elif name == "f_turn":
                    pe.wait_ge(xq_ready, it.at({"F": 1}, 1))
                    pe.matmul(bX1[:, 256:256 + TOK], fs[:, 2:3].to_broadcast([TOK, 128]), idf[0:TOK, 0:TOK],
                              start=True, stop=True)
                    for kb in range(KB):
                        last = pe.transpose(bX1h[:, TOK * kb:TOK * kb + TOK], xqh[:, 128 * kb:128 * kb + 128],
                                            idh[0:TOK, 0:TOK])
                    last.then_inc(x1_filled, 1)
                elif name == "f_up":
                    j = task[1]
                    for i in range(4):
                        for kb in range(KB):
                            last = pe.matmul(bX1[:, TOK * i:TOK * i + TOK],
                                             w_up[:, kb, 128 * (4 * j + i):128 * (4 * j + i) + 128],
                                             xqT[:, kb, :], start=kb == 0, stop=kb == 1)
                    last.then_inc(x1_filled, 1)
                elif name == "f_max":
                    j = task[1]
                    pe.wait_ge(ffn_act, it.at({"F": 2}, j + 1))
                    for i in range(4):
                        last = pe.transpose(bX1[0:TOK, 128 * i:128 * i + 128], hact[:, 4 * j + i, :], idf[:])
                    last.then_inc(x1_filled, 1)
                elif name == "f_rate":
                    pe.wait_ge(rate_ready, it.at({"F": 1}, 1))
                    pe.matmul(bX1[:, 0:TOK], fs[:, 6:7].to_broadcast([TOK, 128]), idf[0:TOK, 0:TOK],
                              start=True, stop=True).then_inc(x1_filled, 1)
                elif name == "f_down":
                    pe.wait_ge(q2_ready, it.at({"F": 1}, 1))
                    for b in range(FB):
                        last = pe.matmul(bX1[0:TOK, 0:DIM], q2T[:, b, :], w_down[:, b, :],
                                         start=b == 0, stop=b == FB - 1)
                    last.then_inc(x1_filled, 1)

            def between(n):
                if n == 1:
                    pe.wait_ge(w_split, MOE0)
                if n == 2:
                    pe.wait_ge(w_split, L1_Q)
                if n == 3:
                    pe.wait_ge(wsum_ready, 1)
                    pe.matmul(bS[:, 0:2], ones[:].to_broadcast([128, 128]), wtot[:], start=True,
                              stop=True).then_inc(wsum_spread, 1)
                    pe.wait_ge(w_split, CHUNKS)
                    pe.wait_ge(ffn_w_ready, 1)

            def body(it):
                for s, slot in enumerate(it.tasks):
                    k = s - 1
                    if 0 <= k < it.units:
                        scores(it, k)
                    if 2 <= k <= it.units + 1:
                        sum_values(it, k - 2)
                    for task in slot:
                        part(it, task)
                    if 1 <= k <= it.units:
                        turn_probs(it, k - 1)

            every_iteration(pe, body, between)

        @block.vector
        def _(dve):
            for t in (qT, PR, PT, oT, aT, kv[0], kv[1]):
                dve.memset(t[:], 0.0)
            for m in (mask[0], mask[1], hpad):
                last = dve.memset(m[:], 0.0)
            last.then_inc(zeros_set, 1)
            dve.wait_ge(gates_ready, 1)
            dve.wait_ge(consts_set, 2)
            dve.tensor_scalar(tgs[:], tgate[:], 1 / WSCALE, None, ALU.mult).then_inc(gates_scaled, 1)
            dve.drain()

            def split_chunk(raw, hi, lo, c):
                dve.wait_ge(w_hi, c + 1)
                dve.scalar_tensor_tensor(lo, raw, WSCALE, hi, ALU.mult, ALU.subtract).then_inc(w_split, 1)

            def split_weights(a, b):
                for c in range(a, b):
                    split_chunk(W[:, (c + SHIFT) * CHUNK:(c + SHIFT + 1) * CHUNK], w(c, 0, 0, CHUNK),
                                w(c, 1, 0, CHUNK), c)

            def split_experts():
                with dve.Fori(0, EXPERTS) as e:
                    for i in range(MOE_CHUNKS):
                        c = e * MOE_CHUNKS + (MOE0 + i)
                        split_chunk(W[:, bass.ds((c + SHIFT) * CHUNK, CHUNK)],
                                    WH[:, bass.ds(c * (2 * CHUNK), CHUNK)],
                                    WH[:, bass.ds(c * (2 * CHUNK) + CHUNK, CHUNK)], c)

            def quantise_ffn_weights():
                for c in range(8):
                    dve.wait_ge(raw_loaded[c % 3], 16 * (c // 3 + 1))
                    dve.tensor_reduce(wabs[:, c:c + 1], staging[c % 3], AX.X, ALU.add,
                                      apply_absolute_value=True).then_inc(raw_used, 1)
                dve.drain()
                dve.tensor_reduce(wtot[:], wabs[:].rearrange("p (m c) -> p m c", m=2), AX.X, ALU.add)\
                    .then_inc(wsum_ready, 1)
                dve.wait_ge(wsum_spread, 1)
                dve.tensor_scalar(wmean[:], bS[:, 0:2], 1 / (FB * 128 * DIM), QMIN_SCALE, ALU.mult, ALU.max)
                dve.drain()
                dve.reciprocal(winv[:], wmean[:])
                dve.tensor_scalar(qfac[:, 0:1], wmean[:, 0:1], 1 / QMAX, None, ALU.mult)
                dve.tensor_scalar(qfac[:, 1:2], wmean[:, 1:2], 0.5 / QMAX, tgate[:, 3:4], ALU.mult, ALU.mult)
                dve.drain()
                for c in range(8, 16):
                    raw = staging[c % 3]
                    i = c - 8
                    dve.wait_ge(raw_loaded[c % 3], 16 * (c // 3 + 1))
                    dve.tensor_scalar(raw, raw, winv[:, i // 4:i // 4 + 1], ROUND, ALU.mult, ALU.add)
                    dve.drain()
                    dve.tensor_scalar(raw, raw, ROUND, -1.0, ALU.subtract, ALU.max)
                    dve.drain()
                    at = ffn0 + i * CHUNK
                    last = dve.tensor_scalar(WH[:, at:at + CHUNK], raw, 1.0, None, ALU.min)
                    last.then_inc(raw_used, 1)
                dve.drain()
                dve.memset(kv[1][:], 0.0).then_inc(ffn_w_ready, 1)
                dve.drain()

            def between(n):
                if n == 1:
                    split_weights(0, MOE0)
                if n == 2:
                    split_experts()
                if n == 3:
                    split_weights(L1_Q, CHUNKS)
                    quantise_ffn_weights()

            def mask_scores(it, k):
                layer = it.group_of(k)[0]
                made = dve.to_reg(it.at(UNITS, k + 1))
                dve.wait_ge(zeros_set, 1)
                dve.wait_ge(scores_ready, made)
                dve.tensor_tensor_reduce(out=S[0:TOK, k % 2, 0:KEYS], in0=bS[0:TOK, 0:KEYS],
                                         in1=mask[layer][:, 0:KEYS], scale=1.0, scalar=3.0e38,
                                         op0=ALU.add, op1=ALU.min,
                                         accum_out=rmin[0:TOK, k % 2:k % 2 + 1]).then_inc(scores_masked, 1)

            def split_probs(it, k):
                dve.wait_ge(probs_ready, it.at(UNITS, k + 1))
                dve.wait_ge(probs_turned, it.at(UNITS, k))
                dve.tensor_copy(PR[0:TOK, 0, 0:KEYS], S[0:TOK, k % 2, 0:KEYS])
                dve.drain()
                dve.tensor_tensor(PR[0:TOK, 1, 0:KEYS], S[0:TOK, k % 2, 0:KEYS], PR[0:TOK, 0, 0:KEYS],
                                  ALU.subtract).then_inc(probs_split, 1)

            def norm_out(it, k):
                layer, group, _ = it.group_of(k)
                dve.wait_ge(values_summed, it.at(UNITS, k + 1))
                dve.reciprocal(rinv[0:TOK, :], rsum[0:TOK, layer + group, :])
                dve.drain()
                dve.tensor_tensor(wide[0:TOK, :].rearrange("p (h d) -> p h d", h=HEADS),
                                  bO[0:TOK, :].rearrange("p (h d) -> p h d", h=HEADS),
                                  rinv[0:TOK, :].rearrange("p (h o) -> p h o", o=1).to_broadcast([TOK, HEADS, HD]),
                                  ALU.mult).then_inc(out_normed, 1)

            def stats(stage, x, col):
                dve.bn_stats(bn[0:TOK, col, :], x[:])
                dve.drain()
                return dve.bn_aggr(mv[stage][0:TOK, col, :], bn[0:TOK, col, :])

            def norm_kv(it, stage, x):
                layer = "PB".index(stage)
                loaded, each = (p_loaded, 48) if stage == "P" else (b_loaded, 32)
                dve.wait_ge(loaded, it.at({stage: each}, each))
                for t in range(CT):
                    dve.bn_stats(bn[0:CP, t, :], ctxb[0:CP, t, :])
                dve.bn_stats(bn[0:TOK, CT, :], x[:])
                dve.drain()
                for t in range(CT):
                    dve.bn_aggr(mv[stage][0:CP, t, :], bn[0:CP, t, :])
                dve.bn_aggr(mv[stage][0:TOK, CT, :], bn[0:TOK, CT, :]).then_inc(stats_ready[stage], 1)
                a, b = (MASKED, 0.0) if layer == 0 else (-MASKED, MASKED)
                dve.tensor_scalar(mask[layer][:, TOK:KEYS], mask8[:], a, b, ALU.mult, ALU.add)
                dve.wait_ge(rstd_ready[stage], it.at({stage: 1}, 1))
                r = rs[stage]
                for t in range(CT):
                    last = dve.tensor_scalar(ctxb[0:CP, t, :], ctxb[0:CP, t, :], mv[stage][0:CP, t, 0:1],
                                             r[0:CP, t:t + 1], ALU.subtract, ALU.mult)
                last.then_inc(norm_ready[stage], 1)
                dve.tensor_scalar(xn[:], x[:], mv[stage][0:TOK, CT, 0:1], r[0:TOK, CT:CT + 1],
                                  ALU.subtract, ALU.mult).then_inc(norm_ready[stage], 1)

            def norm_x(it, stage, x):
                stats(stage, x, 0).then_inc(stats_ready[stage], 1)
                dve.wait_ge(rstd_ready[stage], it.at({stage: 1}, 1))
                return dve.tensor_scalar(xn[:], x[:], mv[stage][0:TOK, 0, 0:1], rs[stage][0:TOK, 0:1],
                                         ALU.subtract, ALU.mult)

            def route(it, task):
                v1, v2 = rsc[:, 0:1], rsc[:, 1:2]
                dve.wait_ge(x0_filled, it.x0_at(task))
                dve.tensor_copy(lg[:], bX0[0:TOK, 0:EXPERTS]).then_inc(x0_drained, 1)
                dve.drain()
                for i, (s, v) in enumerate(((lg, v1), (s2, v2))):
                    dve.tensor_reduce(v, s[:], AX.X, ALU.max)
                    dve.drain()
                    dve.scalar_tensor_tensor(rk[:, i, :], s[:], v, rev[:], ALU.is_equal, ALU.mult)
                    dve.drain()
                    dve.tensor_reduce(rsc[:, 2 + i:3 + i], rk[:, i, :], AX.X, ALU.max)
                    dve.drain()
                    dve.tensor_scalar(one[:, i, :], rk[:, i, :], rsc[:, 2 + i:3 + i], None, ALU.is_equal)
                    dve.tensor_scalar(gk[:, i, :], lg[:], -1.0, v, ALU.mult, ALU.max)
                    last = dve.tensor_scalar(sh[:, i, :], lg[:], v, 0.0, ALU.subtract, ALU.min)
                    if i == 0:
                        dve.drain()
                        dve.scalar_tensor_tensor(s2[:], one[:, 0, :], -3.0e38, lg[:], ALU.mult, ALU.add)
                        dve.drain()
                dve.drain()
                for i in range(2):
                    dve.tensor_tensor(gk[:, i, :], gk[:, i, :], lg[:], ALU.max)
                dve.drain()
                dve.scalar_tensor_tensor(gk[:], gk[:], JITTER, sh[:], ALU.mult, ALU.add)\
                    .then_inc(route_shifted, 1)
                dve.wait_ge(route_exp, it.at({"M": 1}, 1))
                dve.scalar_tensor_tensor(rk[:, 0, :], gk[:, 0, :], 0.0, sh[:, 0, :], ALU.is_ge, ALU.mult,
                                         accum_out=rsc[:, 4:5])
                dve.scalar_tensor_tensor(rk[:, 1, :], gk[:, 1, :], 0.0, sh[:, 1, :], ALU.is_ge, ALU.mult)
                dve.drain()
                dve.scalar_tensor_tensor(gk[:, 1, :], one[:, 0, :], 0.5, rk[:, 1, :], ALU.is_lt, ALU.mult,
                                         accum_out=rsc[:, 5:6])
                dve.drain()
                dve.reciprocal(rsc[:, 6:8], rsc[:, 4:6])
                dve.drain()
                dve.tensor_scalar(dw[:], one[:, 0, :], rsc[:, 6:7], None, ALU.mult)
                dve.drain()
                dve.scalar_tensor_tensor(dw[:], one[:, 1, :], rsc[:, 7:8], dw[:], ALU.mult, ALU.add)
                dve.drain()
                dve.tensor_scalar(dw[:], dw[:], tgs[0:TOK, 2:3], None, ALU.mult)
                dve.drain()

            def quantise(dst, src, scale_col, tmp):
                dve.tensor_scalar(tmp, src, scale_col, ROUND, ALU.mult, ALU.add)
                dve.drain()
                return dve.tensor_scalar(dst, tmp, ROUND, None, ALU.subtract)

            def part(it, task):
                name = task[0]
                if name == "q":
                    p = task[1]
                    dve.wait_ge(q_hi, it.at(PAIR, p + 1))
                    for h in range(2):
                        r = slice(64 * h, 64 * h + 64)
                        last = dve.scalar_tensor_tensor(qT[r, p % 2, h, 1, 0:TOK], bX0[r, 0:TOK],
                                                        -0.125 / WSCALE, qT[r, p % 2, h, 0, 0:TOK],
                                                        ALU.mult, ALU.subtract)
                    last.then_inc(x0_drained, 1)
                elif name == "k":
                    p = task[1]
                    dve.wait_ge(k_hi, it.at(PAIR, p + 1))
                    dve.scalar_tensor_tensor(kT[:, p % 2, 1, :], bK[:, 0:KW], 1 / WSCALE, kT[:, p % 2, 0, :],
                                             ALU.mult, ALU.subtract).then_inc(k_split, 1)
                elif name == "v":
                    p = task[1]
                    dve.wait_ge(v_hi, it.at(PAIR, p + 1))
                    dve.scalar_tensor_tensor(vN[:, p % 2, 1].rearrange("p t d -> p (t d)"), bV[:], 1 / WSCALE,
                                             vN[:, p % 2, 0].rearrange("p t d -> p (t d)"),
                                             ALU.mult, ALU.subtract).then_inc(v_split, 1)
                elif name == "p_norm":
                    norm_kv(it, "P", xa)
                elif name == "b_norm":
                    dve.tensor_copy(xb[:], xm[:])
                    dve.drain()
                    norm_kv(it, "B", xb)
                elif name == "m_norm":
                    norm_x(it, "M", x1).then_inc(norm_ready["M"], 1)
                elif name in ("p_turn", "b_turn"):
                    layer, kb = int(name == "b_turn"), task[1]
                    stage = "PB"[layer]
                    dve.wait_ge(x1_filled, it.x1_at(task))
                    c = 8 * layer + kb
                    dve.tensor_scalar(wide[:, 0:CTX], bX1[:, 0:CTX], vec[:, c + V_GAMMA:c + V_GAMMA + 1],
                                      vec[:, c + V_BETA:c + V_BETA + 1], ALU.mult, ALU.add).then_inc(x1_drained, 1)
                    dve.wait_ge(kv_hi[layer], it.at({stage: 3}, kb + 1))
                    dve.tensor_tensor(kv[layer][:, kb, 1, TOK:KEYS], wide[:, 0:CTX],
                                      kv[layer][:, kb, 0, TOK:KEYS], ALU.subtract)
                    dve.drain()
                elif name in ("p_lat", "b_lat"):
                    layer = int(name == "b_lat")
                    stage = "PB"[layer]
                    dve.wait_ge(x1_filled, it.x1_at(task))
                    for kb in range(KB):
                        c = 8 * layer + kb
                        last = dve.tensor_scalar(wide[:, TOK * kb:TOK * kb + TOK], bX1[:, TOK * kb:TOK * kb + TOK],
                                                 vec[:, c + V_GLAT:c + V_GLAT + 1],
                                                 vec[:, c + V_BLAT:c + V_BLAT + 1], ALU.mult, ALU.add)
                    last.then_inc(x1_drained, 1)
                    dve.drain()
                    n = KB * TOK
                    dve.tensor_scalar(wide[:, n:2 * n], wide[:, 0:n], gates[:, 4:5] if layer == 0 else 1.0,
                                      None, ALU.mult).then_inc(lat_ready[layer], 1)
                    dve.wait_ge(kv_hi[layer], it.at({stage: 3}, 3))
                    lat = wide[:, 0:n].rearrange("p (k t) -> p k t", k=KB)
                    if layer == 0:
                        dve.tensor_tensor(latq[:, :, 1, :], lat, latq[:, :, 0, :], ALU.subtract)
                        lat = wide[:, n:2 * n].rearrange("p (k t) -> p k t", k=KB)
                    dve.tensor_tensor(kv[layer][:, :, 1, 0:TOK], lat, kv[layer][:, :, 0, 0:TOK],
                                      ALU.subtract).then_inc(kv_ready[layer], 1)
                elif name == "o_turn":
                    dve.wait_ge(o_hi, it.at({"A": 1, "B": 1, "F": 1}, [t for t in it.x1 if t[0] == name].index(task) + 1))
                    dve.tensor_tensor(oT[:, 1, :, 0:TOK], bX1[:, 0:4 * TOK].rearrange("p (m t) -> p m t", m=4),
                                      oT[:, 0, :, 0:TOK], ALU.subtract).then_inc(x1_drained, 1)
                elif name == "o_proj":
                    dve.wait_ge(x1_filled, it.x1_at(task))
                    dst, src, g = {"A": (x1, xa, 0), "B": (xb, xb, 1), "F": (xf, xb, 1)}[task[1]]
                    if task[1] == "F":
                        dve.wait_ge(stored, it.at({"F": 16}, 0))
                    dve.scalar_tensor_tensor(dst[:], bX1[0:TOK, 0:DIM], tgs[0:TOK, g:g + 1], src[:],
                                             ALU.mult, ALU.add).then_inc(x1_drained, 1)
                    dve.drain()
                    if task[1] == "A":
                        dve.memset(fs[:, 7:8], 0.0).then_inc(x1_ready, 1)
                elif name == "m_turn":
                    dve.wait_ge(x1_filled, it.x1_at(task))
                    dve.tensor_copy(xmF[:], bX1[:, 0:KB * TOK].rearrange("p (k t) -> p k t", k=KB))\
                        .then_inc(x1_drained, 1)
                    dve.wait_ge(moe_hi, it.at({"M": 1}, 1))
                    dve.tensor_tensor(xmT[:, 1], xmF[:], xmT[:, 0], ALU.subtract).then_inc(moe_ready, 1)
                elif name == "m_gate":
                    route(it, task)
                elif name == "m_up":
                    h = task[1]
                    n = 2 * TOK
                    dve.wait_ge(tanh_ready, it.at(HALVES, h + 1))
                    dve.scalar_tensor_tensor(act[:], act[:], 1.0, bH[:, 0:n], ALU.add, ALU.mult)
                    dve.drain()
                    dve.scalar_tensor_tensor(act[:], act[:], 0.5 / (WSCALE * WSCALE), bH[:, n:2 * n],
                                             ALU.mult, ALU.mult).then_inc(gated, 1)
                elif name == "m_down":
                    e = task[1]
                    dve.wait_ge(x0_filled, it.x0_at(task))
                    dve.scalar_tensor_tensor(xm[:], bX0[0:TOK, 0:DIM], dw[:, e:e + 1], (x1 if e == 0 else xm)[:],
                                             ALU.mult, ALU.add).then_inc(x0_drained, 1)
                    dve.drain()
                elif name == "f_norm":
                    norm_x(it, "F", xf)
                    dve.drain()
                    dve.tensor_reduce(fs[:, 0:1], xn[:], AX.X, ALU.max, apply_absolute_value=True)
                    dve.drain()
                    dve.tensor_scalar(fs[:, 0:1], fs[:, 0:1], QMIN_SCALE, None, ALU.max)
                    dve.drain()
                    dve.reciprocal(fs[:, 1:2], fs[:, 0:1])
                    dve.tensor_scalar(fs[:, 2:3], fs[:, 0:1], qfac[0:TOK, 0:1], None, ALU.mult)
                    dve.drain()
                    dve.tensor_scalar(fs[:, 1:2], fs[:, 1:2], QMAX, None, ALU.mult)
                    dve.drain()
                    quantise(xqh[:], xn[:], fs[:, 1:2], xn[:]).then_inc(xq_ready, 1)
                elif name == "f_turn":
                    dve.wait_ge(x1_filled, it.x1_at(task))
                    dve.tensor_copy(xqT[:], bX1h[:, 0:KB * TOK].rearrange("p (k t) -> p k t", k=KB))
                    dve.tensor_copy(rate[:], bX1[:, 256:256 + TOK]).then_inc(x1_drained, 1)
                    dve.memset(hpad[:, :, 0:1], 0.0)
                    dve.memset(hpad[:, :, TOK + 1:TOK + 2], 0.0)
                    dve.drain()
                elif name == "f_up":
                    j = task[1]
                    dve.wait_ge(x1_filled, it.x1_at(task))
                    dve.tensor_tensor(hpad[:, :, 1:TOK + 1], bX1[:, 0:4 * TOK].rearrange("p (m t) -> p m t", m=4),
                                      rate[:].rearrange("p (o t) -> p o t", o=1).to_broadcast([128, 4, TOK]),
                                      ALU.mult).then_inc(x1_drained, 1)
                    dve.wait_ge(conv_begun, it.at({"F": 2}, j + 1))
                    for tap in (1, 2):
                        for i in range(4):
                            b = 4 * j + i
                            c = V_CONVW + FB * tap + b
                            last = dve.scalar_tensor_tensor(hact[:, b, :], hpad[:, i, tap:tap + TOK], vec[:, c:c + 1],
                                                            hact[:, b, :], ALU.mult, ALU.add)
                        if tap == 1:
                            dve.drain()
                    last.then_inc(conv_done, 1)
                elif name == "f_act":
                    j = task[1]
                    dve.wait_ge(ffn_tanh, it.at({"F": 2}, j + 1))
                    dve.scalar_tensor_tensor(hact[:, 4 * j:4 * j + 4, :], hpad[:, :, 1:TOK + 1], 1.0,
                                             hact[:, 4 * j:4 * j + 4, :], ALU.add, ALU.mult).then_inc(ffn_act, 1)
                    dve.drain()
                elif name == "f_max":
                    j = task[1]
                    dve.wait_ge(x1_filled, it.x1_at(task))
                    dve.tensor_reduce(fs[:, 3 + j:4 + j], bX1[0:TOK, :], AX.X, ALU.max,
                                      apply_absolute_value=True).then_inc(x1_drained, 1)
                    if j == 1:
                        dve.drain()
                        dve.tensor_scalar(fs[:, 5:6], fs[:, 3:4], fs[:, 4:5], 2 * QMIN_SCALE, ALU.max, ALU.max)
                        dve.drain()
                        dve.reciprocal(fs[:, 6:7], fs[:, 5:6])
                        dve.tensor_scalar(fs[:, 5:6], fs[:, 5:6], qfac[0:TOK, 1:2], None, ALU.mult)
                        dve.drain()
                        dve.tensor_scalar(fs[:, 6:7], fs[:, 6:7], QMAX, None, ALU.mult).then_inc(rate_ready, 1)
                elif name == "f_rate":
                    dve.wait_ge(x1_filled, it.x1_at(task))
                    dve.tensor_copy(rate[:], bX1[:, 0:TOK]).then_inc(x1_drained, 1)
                    dve.drain()
                    dve.tensor_tensor(hact[:], hact[:],
                                      rate[:].rearrange("p (o t) -> p o t", o=1).to_broadcast([128, FB, TOK]), ALU.mult)
                    dve.drain()
                    dve.tensor_scalar(hact[:], hact[:], ROUND, None, ALU.add)
                    dve.drain()
                    dve.tensor_scalar(q2T, hact[:], ROUND, None, ALU.subtract).then_inc(q2_ready, 1)
                elif name == "f_down":
                    dve.wait_ge(x1_filled, it.x1_at(task))
                    dve.scalar_tensor_tensor(xf[:], bX1[0:TOK, 0:DIM], fs[:, 5:6], xf[:], ALU.mult, ALU.add)\
                        .then_inc(x1_drained, 1)
                    dve.drain()
                    dve.memset(fs[:, 7:8], 0.0).then_inc(out_ready, 1)

            def body(it):
                for s, slot in enumerate(it.tasks):
                    k = s - 1
                    if 0 <= k < it.units:
                        mask_scores(it, k)
                    for task in slot:
                        part(it, task)
                    if 0 <= k < it.units:
                        split_probs(it, k)
                    if 2 <= k <= it.units + 1 and (k - 2) % HEADS == HEADS - 1:
                        norm_out(it, k - 2)

            every_iteration(dve, body, between)


def kernel(x, ctx_1024, mask_BxS2_bk0, g_xattn, g_ffn, L0_xattn_kv_gate, L0_xattn_gamma_media,
           L0_xattn_beta_media, L0_xattn_gamma_lat, L0_xattn_beta_lat, L0_xattn_Wq, L0_xattn_Wk,
           L0_xattn_Wv, L0_xattn_Wout, L0_ffn_gate_w, L0_ffn_w1, L0_ffn_w2, L0_ffn_w3, L1_xattn_g1,
           L1_xattn_b1, L1_xattn_g2, L1_xattn_b2, L1_xattn_Wq, L1_xattn_Wkv, L1_xattn_Wout,
           L1_ffn_w1, L1_ffn_conv_w, L1_ffn_conv_b, L1_ffn_w2):
    import numpy as np
    import concourse.bacc as bacc
    from concourse.bass_utils import run_bass_kernel_spmd

    arr = np.asarray

    def rows(m):
        m = arr(m)
        return m.reshape(m.shape[0] // 128, 128, m.shape[1]).transpose(1, 0, 2)

    def flat(m):
        return rows(m).reshape(128, -1)

    inner = L1_xattn_Wq.shape[1]
    experts = []
    for e in range(L0_ffn_w1.shape[0]):
        experts += [flat(arr(L0_ffn_w1)[e].T), flat(arr(L0_ffn_w3)[e].T), flat(arr(L0_ffn_w2)[e].T)]
    weights = np.concatenate(
        [flat(L0_xattn_Wq), flat(L0_xattn_Wk), flat(L0_xattn_Wv), flat(L0_xattn_Wout)] + experts +
        [flat(L1_xattn_Wq), flat(arr(L1_xattn_Wkv)[:, :inner]), flat(arr(L1_xattn_Wkv)[:, inner:]),
         flat(L1_xattn_Wout)], axis=1)
    ffn = np.concatenate([flat(arr(L1_ffn_w1).T), flat(arr(L1_ffn_w2).T)], axis=1)

    def cols(v):
        v = arr(v)
        return v.reshape(-1, 128).T

    conv_w = arr(L1_ffn_conv_w)[:, 0, :]
    vectors = np.concatenate(
        [cols(v) for v in (L0_xattn_gamma_media, L0_xattn_beta_media, L0_xattn_gamma_lat,
                           L0_xattn_beta_lat, L1_xattn_g1, L1_xattn_b1, L1_xattn_g2, L1_xattn_b2)] +
        [cols(conv_w[:, t]) for t in range(3)] + [cols(L1_ffn_conv_b)], axis=1)
    gates = np.concatenate([arr(g_xattn), arr(g_ffn), arr(L0_xattn_kv_gate).reshape(1)]).reshape(1, 5)
    arrays = {
        "x": arr(x), "ctx": arr(ctx_1024), "mask": arr(mask_BxS2_bk0).reshape(NSEQ, 1, CTX),
        "weights": weights, "ffn_weights": ffn, "vectors": vectors,
        "router": rows(arr(L0_ffn_gate_w).T), "gates": gates,
    }
    arrays = {f"in_{k}": np.ascontiguousarray(v) for k, v in arrays.items()}
    nc = bacc.Bacc("TRN2", target_bir_lowering=False, num_devices=1)
    args = [nc.dram_tensor(k, v.shape, mybir.dt.from_np(v.dtype), kind="ExternalInput").ap()
            for k, v in arrays.items()]
    out = nc.dram_tensor("out_y", (NSEQ, TOK, DIM), F32, kind="ExternalOutput").ap()
    build(nc, *args, out)
    r = run_bass_kernel_spmd(nc, [arrays], core_ids=[0])
    return r.results[0]["out_y"]
```

```python
from contextlib import ExitStack

import concourse.bass as bass
from concourse import mybir

F32 = mybir.dt.float32
F16 = mybir.dt.float16
BF16 = mybir.dt.bfloat16
U8 = mybir.dt.uint8
ALU = mybir.AluOpType
ACT = mybir.ActivationFunctionType
AX = mybir.AxisListType

NSEQ, TOK, DIM = 16, 112, 256
CTX = 375
CT, CP = 3, 125
KEYS = TOK + CTX
KW = 488
KB = 2
HEADS, HD = 8, 64
PAIRS = 4
EXPERTS, EB = 8, 4
FB = 8
CHUNK = 512
WSCALE = 64.0
LN_EPS = 1e-5
MASKED = 1e30
ROUND = 12582912.0
QMAX = 127.0
QMIN_SCALE = 1e-5
JITTER = 0.02

L0_Q, L0_K, L0_V, L0_O = 0, 2, 4, 6
MOE0 = 8
MOE_CHUNKS = 6
L1_Q = MOE0 + EXPERTS * MOE_CHUNKS
L1_K, L1_V, L1_O = L1_Q + 4, L1_Q + 8, L1_Q + 12
CHUNKS = L1_Q + 16
SHIFT = 2
FFN_WORDS = (KB * FB * 128 + FB * DIM) // 2

V_GAMMA, V_BETA, V_GLAT, V_BLAT = 0, 2, 4, 6
V_CONVW, V_CONVB = 16, 16 + 3 * FB
NVEC = V_CONVB + FB
V_GATED = NVEC

OFFSET = {"P": 0, "A": 1, "M": 2, "B": 3, "F": 4}
LOOP = (5, 16)
LAST = NSEQ + OFFSET["F"]
SLOTS = 29

UNITS = {"A": HEADS, "B": 2 * HEADS}
PAIR = {"A": PAIRS, "B": 2 * PAIRS}
GROUP = {"A": 1, "B": 2}
HALVES = {"M": 2 * EXPERTS}


class Iteration:

    def __init__(self, n, like):
        self.n, self.like = n, like
        self.on = {s for s, o in OFFSET.items() if o <= like < o + NSEQ}
        self.tasks = timeline(self.on)
        self.lead = lead_of(self.on)
        flat = [t for slot in self.tasks for t in slot]
        self.x0 = [t for t in flat if t[0] in ("q", "m_gate", "m_down")]
        self.x1 = [t for t in flat if t[0] in X1_TASKS]
        self.units = sum(UNITS[s] for s in "AB" if s in self.on)

    def at(self, per, local=0):
        if isinstance(self.n, int):
            past = {s: min(max(self.n - OFFSET[s], 0), NSEQ) for s in per}
            return max(0, sum(k * past[s] for s, k in per.items()) + local)
        slope = sum(per.values())
        return self.n * slope + (local - sum(k * OFFSET[s] for s, k in per.items()))

    def taken_up(self):
        before = []
        for slot in self.tasks:
            own = ("m_up",) + APPLIES + NORMS
            yield ([t for t in before if t[0] not in own][::-1] +
                   [t for name in own for t in slot if t[0] == name])
            before = slot

    def x0_at(self, task, local=1):
        return self.at(X0_PER, self.x0.index(task) + local)

    def x1_at(self, task, local=1):
        return self.at(X1_PER, self.x1.index(task) + local)

    def seq(self, stage):
        return self.n - OFFSET[stage]

    def group_of(self, unit):
        return self.pair_group(unit // 2)

    def pair_group(self, pair):
        if "A" in self.on:
            if pair < PAIRS:
                return 0, 0, pair
            pair -= PAIRS
        return 1, pair // PAIRS, pair % PAIRS


ORDER = ("m_up", "k", "v", "q", "m_gate", "m_down")
NORMS = ("p_norm", "m_norm", "b_norm", "f_norm")
APPLIES = ("p_apply", "m_apply", "b_apply", "f_apply")
X1_TASKS = ("p_turn", "p_lat", "b_turn", "b_lat", "o_turn", "o_proj", "m_turn",
            "f_turn", "f_up", "f_max", "f_rate", "f_down")
X0_PER = {"A": PAIRS, "B": 2 * PAIRS, "M": 1 + EXPERTS}
X1_PER = {"P": 3, "B": 3 + 2, "A": 2, "M": 1, "F": 2 + 7}


def lead_of(on):
    return 9 if "B" in on and "A" not in on else 1


def timeline(on):
    lead = lead_of(on)
    slots = [[] for _ in range(SLOTS)]

    def put(slot, *task):
        slots[slot].append(task)

    if "F" in on:
        put(0, "o_turn", "F")
        put(2, "o_proj", "F")
        put(4, "f_norm")
        put(6, "f_apply")
    if "M" in on:
        put(0, "m_apply")
        put(1, "m_turn")
    if "B" in on:
        put(0, "b_norm")
        put(2, "b_apply")
        for kb in range(KB):
            put(3 + kb, "b_turn", kb)
        put(5, "b_lat")
    for p in range(sum(PAIR[s] for s in "AB" if s in on)):
        put(lead + 2 * p - 1, "q", p)
        put(lead + 2 * p - 1, "k", p)
        put(lead + 2 * p + 2, "v", p)
    if "M" in on:
        put(3, "m_gate")
        put(5, "m_route")
        for e in range(EXPERTS):
            put(3 * e + 4, "m_up", 2 * e)
            put(3 * e + 5, "m_up", 2 * e + 1)
            put(3 * e + 7 - e % 2, "m_down", e)
    if "F" in on:
        put(8, "f_turn")
        for j, (up, top) in enumerate(((10, 16), (15, 23))):
            put(up, "f_up", j)
            put(up + 1, "f_conv", j)
            put(up + 3, "f_act", j)
            put(top, "f_max", j)
        put(25, "f_rate")
        put(27, "f_down")
    if "A" in on:
        put(12, "o_turn", "A")
        put(13, "o_proj", "A")
        put(19, "m_norm")
    if "B" in on:
        first = lead + (HEADS if "A" in on else 0)
        put(first + HEADS + 3, "o_turn", "B")
        put(first + HEADS + 5, "o_proj", "B")
    if "P" in on:
        put(15, "p_norm")
        put(17, "p_apply")
        for kb in range(KB):
            put(18 + 3 * kb, "p_turn", kb)
        put(24, "p_lat")
    return [sorted(slot, key=lambda t: ORDER.index(t[0]) if t[0] in ORDER else len(ORDER)) for slot in slots]


def build(nc, x_in, ctx_in, mask_in, weights_in, ffn_in, vectors_in, router_in, gates_in, out):
    with ExitStack() as stack:
        def sb(name, shape, dt=F32):
            return stack.enter_context(nc.sbuf_tensor(name, shape, dt))

        def ps(name):
            return stack.enter_context(nc.psum_tensor(name, [128, 512], F32))

        def sem(name):
            return stack.enter_context(nc.semaphore(name))

        W = sb("weights", [128, CHUNKS * CHUNK + FFN_WORDS])
        WH = W[:].bitcast(F16)
        ffn0 = CHUNKS * 2 * CHUNK
        w_up = WH[:, ffn0:ffn0 + KB * FB * 128].rearrange("p (k c) -> p k c", k=KB)
        w_down = WH[:, ffn0 + KB * FB * 128:ffn0 + KB * FB * 128 + FB * DIM].rearrange(
            "p (k c) -> p k c", k=FB)
        vec = sb("vectors", [128, NVEC + 2 * KB])
        gates = sb("gates", [128, 5])
        tgate = sb("tanh_gates", [128, 4])
        tgs = sb("tanh_gates_unscaled", [128, 4])
        router = sb("router", [128, KB, EXPERTS])
        idf = sb("identity_f32", [128, 128])
        idh = sb("identity_f16", [128, 128], F16)
        minus_half = sb("minus_half", [128, 4])
        eps = sb("eps", [128, 4])
        ones = sb("ones", [128, 1])
        rev = sb("rev_index", [TOK, EXPERTS])
        wabs = sb("weight_abs_sums", [128, 8])
        wtot = sb("weight_abs_total", [128, 2])
        wmean = sb("weight_means", [128, 2])
        winv = sb("weight_inverse_means", [128, 2])
        qfac = sb("dequant_factors", [128, 2])

        kv = {0: sb("kv_A", [128, KB, 2, 512], F16), 1: sb("kv_B", [128, KB, 2, 512], F16)}
        latq = sb("latents_A", [128, KB, 2, TOK], F16)
        kT = sb("keys", [128, 2, 2, KW], F16)
        vN = sb("values", [128, 2, 2, 4, 128], F16)
        qT = sb("queries", [128, 2, 2, 2, 128], F16)
        S = sb("scores", [128, 2, KEYS + 1])
        PR = sb("probs", [128, 2, 2, 512], F16)
        PT = sb("probs_turned", [128, 2, 4, 128], F16)
        mask = {0: sb("mask_A", [TOK, KEYS + 1], BF16), 1: sb("mask_B", [TOK, KEYS + 1], BF16)}
        mask8 = sb("mask_bytes", [TOK, CTX], U8)
        rmin = sb("score_min", [128, 2])
        rsum = sb("prob_sums", [128, 3, HEADS])
        rinv = sb("prob_sum_inverse", [128, HEADS])
        wide = sb("wide", [128, 512])
        oT = sb("heads_turned", [128, 2, 4, TOK], F16)
        ctxb = sb("context", [128, CT, DIM])
        xa = sb("x_A", [TOK, DIM])
        x1 = sb("x_after_A", [TOK, DIM])
        xm = sb("x_M", [TOK, DIM])
        xb = sb("x_B", [TOK, DIM])
        xf = sb("x_F", [TOK, DIM])
        xn = sb("x_normed", [TOK, DIM])
        bn = sb("bn_stats", [128, 4, 6])
        mv = {s: sb(f"mean_var_{s}", [128, 4, 2]) for s in "PBMF"}
        rs = {s: sb(f"rstd_{s}", [128, 6]) for s in "PBMF"}
        xmF = sb("moe_in_f32", [128, KB, TOK])
        xmT = sb("moe_in", [128, 2, KB, TOK], F16)
        act = xmF[:].rearrange("p k t -> p (k t)")
        aT = sb("moe_hidden", [128, 2, EB, TOK], F16)
        lg = sb("logits", [TOK, EXPERTS])
        rk = sb("route_ranks", [TOK, 2, EXPERTS])
        one = sb("route_onehot", [TOK, 2, EXPERTS])
        sh = sb("route_shifted", [TOK, 2, EXPERTS])
        gk = sb("route_keep", [TOK, 2, EXPERTS])
        s2 = sb("logits_without_first", [TOK, EXPERTS])
        rsc = sb("route_scalars", [TOK, 8])
        dw = sb("dense_weights", [TOK, EXPERTS])
        hpad = sb("ffn_hidden_padded", [128, 4, TOK + 2])
        hact = sb("ffn_hidden", [128, FB, TOK])
        q2T = hpad[:].rearrange("p a b -> p (a b)").bitcast(F16)[:, 0:FB * TOK].rearrange(
            "p (k t) -> p k t", k=FB)
        rate = sb("ffn_rate", [128, TOK])
        fs = sb("ffn_scalars", [TOK, 8])
        hact16 = hact[:].rearrange("p a b -> p (a b)").bitcast(F16)
        xqh = hact16[0:TOK, 8 * TOK:8 * TOK + DIM]
        xqT = hact16[:, 12 * TOK:12 * TOK + KB * TOK].rearrange("p (k t) -> p k t", k=KB)
        hact_flat = hact[:].rearrange("p a b -> p (a b)")
        kvb_flat = kv[1][:].rearrange("p a b c -> p (a b c)").bitcast(F32)
        staging = [hact_flat[:, 0:CHUNK], kvb_flat[:, 0:CHUNK], kvb_flat[:, CHUNK:2 * CHUNK]]

        bS, bT, bO, bK, bV, bH, bX0, bX1 = (ps(n) for n in (
            "bank_scores", "bank_turn", "bank_out", "bank_keys", "bank_values", "bank_hidden",
            "bank_x0", "bank_x1"))
        bT16 = bT[:].bitcast(F16)[:, 0:2 * 4 * TOK].rearrange("p (a t c) -> p a t c", a=2, t=4)
        bX1h = bX1[:].bitcast(F16)

        consts_set = sem("consts_set")
        zeros_set = sem("zeros_set")
        vectors_loaded = sem("vectors_loaded")
        gates_ready = sem("gates_ready")
        gates_scaled = sem("gates_scaled")
        w_loaded = [sem(f"weights_loaded_{i}") for i in range(3)]
        w_hi, w_split = sem("weights_hi"), sem("weights_split")
        raw_loaded = [sem(f"ffn_raw_loaded_{i}") for i in range(3)]
        raw_used = sem("ffn_raw_used")
        wsum_ready, wsum_spread, ffn_w_ready = sem("wsum_ready"), sem("wsum_spread"), sem("ffn_w_ready")
        p_loaded, b_loaded = sem("p_loaded"), sem("b_loaded")
        stored = sem("stored")

        stats_ready = {s: sem(f"stats_ready_{s}") for s in "PBMF"}
        rstd_ready = {s: sem(f"rstd_ready_{s}") for s in "PBMF"}
        norm_ready = {s: sem(f"norm_ready_{s}") for s in "PBM"}
        kv_hi = {0: sem("kv_hi_A"), 1: sem("kv_hi_B")}
        kv_ready = {0: sem("kv_ready_A"), 1: sem("kv_ready_B")}

        k_ready, k_hi, k_split = sem("k_ready"), sem("k_hi"), sem("k_split")
        v_ready, v_hi, v_split = sem("v_ready"), sem("v_hi"), sem("v_split")
        q_hi = sem("q_hi")
        scores_ready, scores_masked = sem("scores_ready"), sem("scores_masked")
        probs_ready, probs_split = sem("probs_ready"), sem("probs_split")
        probs_turned, turned_copied = sem("probs_turned"), sem("turned_copied")
        values_summed = sem("values_summed")
        out_normed, o_hi, x1_ready = sem("out_normed"), sem("o_hi"), sem("x1_ready")

        moe_hi, moe_ready = sem("moe_hi"), sem("moe_ready")
        route_shifted, route_exp = sem("route_shifted"), sem("route_exp")
        up_ready, tanh_ready = sem("up_ready"), sem("tanh_ready")
        gated, act_split = sem("gated"), sem("act_split")
        x0_filled, x0_drained = sem("x0_filled"), sem("x0_drained")
        x1_filled, x1_drained = sem("x1_filled"), sem("x1_drained")
        xq_ready = sem("xq_ready")
        conv_begun, conv_done, ffn_tanh, ffn_act = (
            sem("conv_begun"), sem("conv_done"), sem("ffn_tanh"), sem("ffn_act"))
        rate_ready, q2_ready, out_ready = sem("rate_ready"), sem("q2_ready"), sem("out_ready")

        def w(chunk, part, col, n):
            at = (2 * chunk + part) * CHUNK + col
            return WH[:, at:at + n]

        def layer_chunks(layer, group):
            if layer == 0:
                return L0_Q, L0_K, L0_V, L0_O, 1
            return L1_Q + group, L1_K + group, L1_V + group, L1_O + 2 * group, 2

        def latents_of(layer):
            keys = kv[layer][:, :, :, 0:TOK]
            return [(latq, V_GLAT), (keys, V_GATED)] if layer == 0 else [(keys, 8 + V_GLAT)]

        PASSES = ((0, 0), (0, 1), (1, 0))

        def every_iteration(eng, body, between):
            for n in range(LOOP[0]):
                between(n)
                body(Iteration(n, n))
            with eng.Fori(LOOP[0], LOOP[1]) as n:
                body(Iteration(n, LOOP[0]))
            for n in range(LOOP[1], LAST):
                body(Iteration(n, n))

        block = stack.enter_context(nc.Block())

        @block.sync
        def _(sp):
            sp.dma_start(vec[:, 0:NVEC], vectors_in).then_inc(vectors_loaded, 16)
            sp.dma_start(gates[:], gates_in.to_broadcast([128, 5])).then_inc(vectors_loaded, 16)
            sp.dma_start(router[:], router_in).then_inc(vectors_loaded, 16)

            def load_p(it):
                b = it.seq("P")
                sp.wait_ge(x1_ready, it.at({"A": 1}, 1 if "A" in it.on else 0))
                if "B" in it.on:
                    sp.wait_ge(x1_drained, it.x1_at(("b_turn", KB - 1)))
                elif it.like > 0:
                    before = Iteration(it.n - 1, it.like - 1)
                    sp.wait_ge(x1_drained, before.x1_at(("p_turn", KB - 1)))
                sp.dma_start(xa[:], x_in[b]).then_inc(p_loaded, 16)
                sp.dma_start(ctxb[0:CP], ctx_in[b].rearrange("(t p) d -> p t d", p=CP)).then_inc(p_loaded, 16)
                sp.dma_start(mask8[:], mask_in[b].to_broadcast([TOK, CTX])).then_inc(p_loaded, 16)

            def load_b(it, last):
                b = it.seq("B") + 1
                sp.wait_ge(x1_drained, it.x1_at(last))
                sp.dma_start(ctxb[0:CP], ctx_in[b].rearrange("(t p) d -> p t d", p=CP)).then_inc(b_loaded, 16)
                sp.dma_start(mask8[:], mask_in[b].to_broadcast([TOK, CTX])).then_inc(b_loaded, 16)

            def body(it):
                last = ("p_turn" if "P" in it.on else "b_turn", KB - 1)
                for slot in it.tasks:
                    for task in slot:
                        if task[0] == "p_norm":
                            load_p(it)
                        if task == last and OFFSET["B"] <= it.like + 1 < OFFSET["B"] + NSEQ:
                            load_b(it, last)
                        if task[0] == "f_down":
                            sp.wait_ge(out_ready, it.at({"F": 1}, 1))
                            sp.dma_start(out[it.seq("F")], xf[:]).then_inc(stored, 16)

            def between(n):
                if n == 1:
                    for i, (a, b) in enumerate(((0, MOE0), (MOE0, L1_Q), (L1_Q, CHUNKS))):
                        sp.dma_start(W[:, (a + SHIFT) * CHUNK:(b + SHIFT) * CHUNK],
                                     weights_in[:, a * CHUNK:b * CHUNK]).then_inc(w_loaded[i], 16)
                if n == 3:
                    for c in range(16):
                        if c >= 3:
                            sp.wait_ge(raw_used, c - 2)
                        sp.dma_start(staging[c % 3], ffn_in[:, (c % 8) * CHUNK:(c % 8 + 1) * CHUNK])\
                            .then_inc(raw_loaded[c % 3], 16)

            every_iteration(sp, body, between)
            sp.wait_ge(stored, 16 * NSEQ)

        @block.gpsimd
        def _(pool):
            pool.memset(idf[:], 0.0)
            pool.memset(idh[:], 0.0)
            pool.memset(ones[:], 1.0)
            pool.memset(minus_half[:], -0.5)
            pool.memset(eps[:], LN_EPS)
            pool.iota(rev[:], pattern=[[-1, EXPERTS]], base=EXPERTS, channel_multiplier=0,
                      allow_small_or_imprecise_dtypes=True)
            pool.drain()
            for m in (idf, idh):
                last = pool.affine_select(out=m[:], in_=m[:], compare_op=ALU.not_equal, fill=1.0,
                                          base=0, pattern=[[-1, 128]], channel_multiplier=1)
            last.then_inc(consts_set, 1)
            for s in "PBMF":
                last = pool.memset(mv[s][:], 1.0)
            last.then_inc(consts_set, 1)

            def rstd(stage, it, cols, twice):
                m, r = mv[stage], rs[stage]
                pool.wait_ge(stats_ready[stage], it.at({"A" if stage == "M" else stage: 1}, 1))
                pool.tensor_tensor(r[:, 0:cols], m[:, 0:cols, 1], eps[:, 0:cols], ALU.add)
                pool.drain()
                last = pool.tensor_tensor(r[:, 0:cols], r[:, 0:cols], minus_half[:, 0:cols], ALU.pow)
                if twice:
                    c = cols - 1
                    pool.drain()
                    pool.tensor_tensor(r[:, 4:5], m[:, c, 1:2], r[:, c:c + 1], ALU.mult)
                    pool.drain()
                    pool.tensor_tensor(r[:, 4:5], r[:, 4:5], r[:, c:c + 1], ALU.mult)
                    pool.drain()
                    pool.tensor_scalar(r[:, 4:5], r[:, 4:5], LN_EPS, None, ALU.add)
                    pool.drain()
                    pool.tensor_tensor(r[:, 4:5], r[:, 4:5], minus_half[:, 0:1], ALU.pow)
                    pool.drain()
                    last = pool.tensor_tensor(r[:, c:c + 1], r[:, c:c + 1], r[:, 4:5], ALU.mult)
                last.then_inc(rstd_ready[stage], 1)

            def split_probs(it, k):
                ready, turned = (pool.to_reg(it.at(UNITS, n)) for n in (k + 1, k - 1))
                pool.wait_ge(zeros_set, 1)
                pool.wait_ge(probs_turned, turned)
                pool.wait_ge(probs_ready, ready)
                pool.tensor_tensor(PR[0:TOK, k % 2, 1, 0:KEYS], S[0:TOK, k % 2, 0:KEYS],
                                   PR[0:TOK, k % 2, 0, 0:KEYS], ALU.subtract).then_inc(probs_split, 1)

            def split_hidden(it, h):
                m0 = 2 * (h % 2)
                f = act.rearrange("p (m t) -> p m t", m=2)
                made = pool.to_reg(it.at(HALVES, h + 1))
                if h >= 2:
                    multiplied = pool.to_reg(it.x0_at(("m_down", h // 2 - 1)))
                pool.wait_ge(zeros_set, 1)
                if h >= 2:
                    pool.wait_ge(x0_filled, multiplied)
                pool.wait_ge(gated, made)
                pool.tensor_copy(aT[:, 0, m0:m0 + 2], f)
                pool.drain()
                pool.tensor_tensor(aT[:, 1, m0:m0 + 2], f, aT[:, 0, m0:m0 + 2],
                                   ALU.subtract).then_inc(act_split, 1)

            def body(it):
                before = []
                for s, slot in enumerate(it.tasks):
                    k = s - 1 - it.lead
                    for task in before:
                        if task[0] in NORMS:
                            stage = task[0][0].upper()
                            rstd(stage, it, CT + 1 if stage in "PB" else 1, stage in "PB")
                    for task in before:
                        if task[0] == "m_up":
                            split_hidden(it, task[1])
                    if 0 <= k < it.units:
                        split_probs(it, k)
                    before = slot

            every_iteration(pool, body, lambda n: None)

        @block.scalar
        def _(act_e):
            act_e.wait_ge(vectors_loaded, 48)
            act_e.activation(tgate[:], gates[:, 0:4], ACT.Tanh).then_inc(gates_ready, 1)
            act_e.wait_ge(gates_scaled, 1)

            def split_weights(a, b):
                for c in range(a, b):
                    act_e.wait_ge(w_split, max(0, c - SHIFT + 1))
                    act_e.activation(w(c, 0, 0, CHUNK), W[:, (c + SHIFT) * CHUNK:(c + SHIFT + 1) * CHUNK],
                                     ACT.Copy, scale=WSCALE).then_inc(w_hi, 1)

            def split_experts():
                with act_e.Fori(0, EXPERTS) as e:
                    for i in range(MOE_CHUNKS):
                        c = e * MOE_CHUNKS + (MOE0 + i)
                        act_e.wait_ge(w_split, c - (SHIFT - 1))
                        act_e.activation(WH[:, bass.ds(c * (2 * CHUNK), CHUNK)],
                                         W[:, bass.ds((c + SHIFT) * CHUNK, CHUNK)],
                                         ACT.Copy, scale=WSCALE).then_inc(w_hi, 1)

            def between(n):
                if n == 1:
                    act_e.wait_ge(w_loaded[0], 16)
                    split_weights(0, MOE0)
                if n == 2:
                    act_e.wait_ge(w_loaded[1], 16)
                    split_experts()
                if n == 3:
                    act_e.wait_ge(w_loaded[2], 16)
                    split_weights(L1_Q, CHUNKS)

            def turned_copy(it, k):
                act_e.wait_ge(probs_turned, it.at(UNITS, k + 1))
                act_e.wait_ge(values_summed, it.at(UNITS, k))
                act_e.activation(PT[:, :, :, 0:TOK], bT16, ACT.Copy).then_inc(turned_copied, 1)

            def exp(it, k):
                layer, group, _ = it.group_of(k)
                g = layer + group
                act_e.wait_ge(scores_masked, it.at(UNITS, k + 1))
                act_e.activation(S[0:TOK, k % 2, 0:KEYS], S[0:TOK, k % 2, 0:KEYS], ACT.Exp,
                                 bias=rmin[0:TOK, k % 2:k % 2 + 1], scale=-1.0,
                                 accum_out=rsum[0:TOK, g, k % HEADS:k % HEADS + 1])
                act_e.drain()
                act_e.wait_ge(probs_turned, it.at(UNITS, k - 1))
                act_e.activation(PR[0:TOK, k % 2, 0, 0:KEYS], S[0:TOK, k % 2, 0:KEYS], ACT.Copy).then_inc(probs_ready, 1)

            def part(it, task):
                name = task[0]
                if name == "q":
                    p = task[1]
                    act_e.wait_ge(x0_filled, it.x0_at(task))
                    act_e.wait_ge(scores_ready, it.at(UNITS, 2 * p - 2))
                    for h in range(2):
                        r = slice(64 * h, 64 * h + 64)
                        last = act_e.activation(qT[r, p % 2, h, 0, 0:TOK], bX0[r, 0:TOK], ACT.Copy,
                                                scale=-0.125 / WSCALE)
                    last.then_inc(q_hi, 1)
                elif name == "k":
                    p = task[1]
                    act_e.wait_ge(k_ready, it.at(PAIR, p + 1))
                    act_e.wait_ge(scores_ready, it.at(UNITS, 2 * p - 2))
                    act_e.activation(kT[:, p % 2, 0, :], bK[:, 0:KW], ACT.Copy, scale=1 / WSCALE)\
                        .then_inc(k_hi, 1)
                elif name == "v":
                    p = task[1]
                    act_e.wait_ge(v_ready, it.at(PAIR, p + 1))
                    act_e.wait_ge(values_summed, it.at(UNITS, 2 * p - 2))
                    act_e.activation(vN[:, p % 2, 0], bV[:].rearrange("p (t d) -> p t d", t=4), ACT.Copy,
                                     scale=1 / WSCALE).then_inc(v_hi, 1)
                elif name in ("p_turn", "b_turn"):
                    layer, kb = int(name == "b_turn"), task[1]
                    stage = "PB"[layer]
                    c = 8 * layer + kb
                    act_e.wait_ge(x1_filled, it.x1_at(task))
                    act_e.activation(kv[layer][:, kb, 0, TOK:KEYS], bX1[:, 0:CTX], ACT.Identity,
                                     scale=vec[:, c + V_GAMMA:c + V_GAMMA + 1],
                                     bias=vec[:, c + V_BETA:c + V_BETA + 1]).then_inc(kv_hi[layer], 1)
                elif name in ("p_lat", "b_lat"):
                    layer = int(name == "b_lat")
                    stage = "PB"[layer]
                    act_e.wait_ge(x1_filled, it.x1_at(task))
                    for dst, c in latents_of(layer):
                        for kb in range(KB):
                            last = act_e.activation(dst[:, kb, 0, :], bX1[:, TOK * kb:TOK * kb + TOK],
                                                    ACT.Identity, scale=vec[:, c + kb:c + kb + 1],
                                                    bias=vec[:, c + KB + kb:c + KB + kb + 1])
                    last.then_inc(kv_hi[layer], 1)
                elif name == "o_turn":
                    act_e.wait_ge(x1_filled, it.x1_at(task))
                    act_e.activation(oT[:, 0], bX1[:, 0:4 * TOK].rearrange("p (m t) -> p m t", m=4),
                                     ACT.Copy).then_inc(o_hi, 1)
                elif name == "m_turn":
                    act_e.wait_ge(x1_filled, it.x1_at(task))
                    act_e.activation(xmT[:, 0], bX1[:, 0:KB * TOK].rearrange("p (k t) -> p k t", k=KB),
                                     ACT.Copy).then_inc(moe_hi, 1)
                elif name == "m_route":
                    act_e.wait_ge(route_shifted, it.at({"M": 1}, 1))
                    act_e.activation(sh[:], sh[:], ACT.Exp).then_inc(route_exp, 1)
                elif name == "m_up":
                    h = task[1]
                    act_e.wait_ge(up_ready, it.at(HALVES, h + 1))
                    act_e.wait_ge(act_split, it.at(HALVES, h))
                    act_e.activation(act, bH[:, 0:2 * TOK], ACT.Tanh, scale=0.5 / WSCALE).then_inc(tanh_ready, 1)
                elif name == "f_conv":
                    j = task[1]
                    act_e.wait_ge(x1_drained, it.x1_at(("f_up", j)))
                    for i in range(4):
                        b = 4 * j + i
                        last = act_e.activation(hact[:, b, :], hpad[:, i, 0:TOK], ACT.Identity,
                                                scale=vec[:, V_CONVW + b:V_CONVW + b + 1],
                                                bias=vec[:, V_CONVB + b:V_CONVB + b + 1])
                    last.then_inc(conv_begun, 1)
                elif name == "f_act":
                    j = task[1]
                    act_e.wait_ge(conv_done, it.at({"F": 2}, j + 1))
                    act_e.activation(hpad[:, :, 1:TOK + 1], hact[:, 4 * j:4 * j + 4, :], ACT.Tanh, scale=0.5)\
                        .then_inc(ffn_tanh, 1)

            def body(it):
                for s, slot in enumerate(it.tasks):
                    k = s - 1 - it.lead
                    if 0 <= k < it.units:
                        exp(it, k)
                    for task in slot:
                        part(it, task)
                    if 1 <= k <= it.units:
                        turned_copy(it, k - 1)

            every_iteration(act_e, body, between)

        @block.tensor
        def _(pe):
            pe.wait_ge(consts_set, 2)
            pe.wait_ge(zeros_set, 1)

            def proj_q(it, p):
                layer, group, j = it.pair_group(p)
                wq, _, _, _, step = layer_chunks(layer, group)
                pe.wait_ge(x0_drained, it.x0_at(("q", p), 0))
                n = 0
                for kb in range(KB):
                    for a, b in PASSES:
                        rhs = latq[:, kb, b, :] if layer == 0 else kv[1][:, kb, b, 0:TOK]
                        last = pe.matmul(bX0[:, 0:TOK], w(wq + kb * step, a, 128 * j, 128), rhs,
                                         start=n == 0, stop=n == 5)
                        n += 1
                last.then_inc(x0_filled, 1)

            def proj_k(it, p):
                layer, group, j = it.pair_group(p)
                _, wk, _, _, step = layer_chunks(layer, group)
                pe.wait_ge(k_split, it.at(PAIR, p))
                n = 0
                for kb in range(KB):
                    for a, b in PASSES:
                        last = pe.matmul(bK[:, 0:KW], w(wk + kb * step, a, 128 * j, 128),
                                         kv[layer][:, kb, b, 0:KW], start=n == 0, stop=n == 5)
                        n += 1
                last.then_inc(k_ready, 1)

            def proj_v(it, p):
                layer, group, j = it.pair_group(p)
                _, _, wv, _, step = layer_chunks(layer, group)
                pe.wait_ge(v_split, it.at(PAIR, p))
                for t in range(4):
                    n = 0
                    for kb in range(KB):
                        for a, b in PASSES:
                            last = pe.matmul(bV[:, 128 * t:128 * t + 128],
                                             kv[layer][:, kb, a, 128 * t:128 * t + 128],
                                             w(wv + kb * step, b, 128 * j, 128),
                                             start=n == 0, stop=n == 5)
                            n += 1
                last.then_inc(v_ready, 1)

            def scores(it, k):
                p, h = k // 2, k % 2
                pe.wait_ge(x0_drained, it.x0_at(("q", p)))
                pe.wait_ge(k_split, it.at(PAIR, p + 1))
                pe.wait_ge(scores_masked, it.at(UNITS, k))
                for n, (a, b) in enumerate(PASSES):
                    last = pe.matmul(bS[:, 0:KW], qT[:, p % 2, h, a, :], kT[:, p % 2, b, :],
                                     start=n == 0, stop=n == 2)
                last.then_inc(scores_ready, 1)

            def turn_probs(it, k):
                pe.wait_ge(probs_split, it.at(UNITS, k + 1))
                pe.wait_ge(turned_copied, it.at(UNITS, k))
                for a in range(2):
                    for t in range(4):
                        last = pe.transpose(bT16[:, a, t, :], PR[0:TOK, k % 2, a, 128 * t:128 * t + 128],
                                            idh[0:TOK, 0:TOK])
                last.then_inc(probs_turned, 1)

            def sum_values(it, k):
                p, h = k // 2, k % 2
                pe.wait_ge(turned_copied, it.at(UNITS, k + 1))
                pe.wait_ge(v_split, it.at(PAIR, p + 1))
                if k % HEADS == 0:
                    pe.wait_ge(out_normed, it.at(GROUP, k // HEADS))
                n = 0
                col = HD * (k % HEADS)
                for t in range(4):
                    for a, b in PASSES:
                        last = pe.matmul(bO[:, col:col + HD], PT[:, a, t, :],
                                         vN[:, p % 2, b, t, HD * h:HD * h + HD], start=n == 0, stop=n == 11)
                        n += 1
                last.then_inc(values_summed, 1)

            def group_of_task(it, stage):
                if stage == "A":
                    return 0, 0, it.at(GROUP, 1)
                if stage == "B":
                    return 1, 0, it.at(GROUP, 2 if "A" in it.on else 1)
                return 1, 1, it.at(GROUP, 0)

            def part(it, task):
                name = task[0]
                if name in ("q", "k", "v"):
                    p = task[1]
                    layer, _, j = it.pair_group(p)
                    if name == "k" and (p == 0 or (p == PAIRS and "A" in it.on)):
                        stage = "PB"[layer]
                        pe.wait_ge(kv_ready[layer], it.at({stage: 1}, layer))
                    {"q": proj_q, "k": proj_k, "v": proj_v}[name](it, p)
                    return
                if name in X1_TASKS:
                    pe.wait_ge(x1_drained, it.x1_at(task, 0))
                if name in ("p_turn", "b_turn"):
                    stage, kb = name[0].upper(), task[1]
                    pe.wait_ge(norm_ready[stage], it.at({stage: 2}, 1))
                    for t in range(CT):
                        last = pe.transpose(bX1[:, CP * t:CP * t + CP], ctxb[0:CP, t, 128 * kb:128 * kb + 128],
                                            idf[0:CP, 0:CP])
                    last.then_inc(x1_filled, 1)
                elif name in ("p_lat", "b_lat", "m_turn"):
                    stage = name[0].upper()
                    pe.wait_ge(norm_ready[stage], it.at({stage: 1 if stage == "M" else 2},
                                                        1 if stage == "M" else 2))
                    for kb in range(KB):
                        last = pe.transpose(bX1[:, TOK * kb:TOK * kb + TOK], xn[:, 128 * kb:128 * kb + 128],
                                            idf[0:TOK, 0:TOK])
                    last.then_inc(x1_filled, 1)
                elif name == "o_turn":
                    pe.wait_ge(out_normed, group_of_task(it, task[1])[2])
                    for m in range(4):
                        last = pe.transpose(bX1[:, TOK * m:TOK * m + TOK], wide[0:TOK, 128 * m:128 * m + 128],
                                            idf[0:TOK, 0:TOK])
                    last.then_inc(x1_filled, 1)
                elif name == "o_proj":
                    layer, group, _ = group_of_task(it, task[1])
                    wo = layer_chunks(layer, group)[3]
                    n = 0
                    for m in range(4):
                        for a, b in PASSES:
                            last = pe.matmul(bX1[0:TOK, 0:DIM], oT[:, a, m, :],
                                             w(wo + m // 2, b, DIM * (m % 2), DIM), start=n == 0, stop=n == 11)
                            n += 1
                    last.then_inc(x1_filled, 1)
                elif name == "m_gate":
                    pe.wait_ge(x0_drained, it.x0_at(task, 0))
                    pe.wait_ge(x1_drained, it.x1_at(("m_turn",)))
                    for kb in range(KB):
                        last = pe.matmul(bX0[0:TOK, 0:EXPERTS], xmF[:, kb, :], router[:, kb, :],
                                         start=kb == 0, stop=kb == 1)
                    last.then_inc(x0_filled, 1)
                elif name == "m_up":
                    h = task[1]
                    e = h // 2
                    if h == 0:
                        pe.wait_ge(moe_ready, it.at({"M": 1}, 1))
                    pe.wait_ge(gated, it.at(HALVES, h))
                    first = MOE0 + MOE_CHUNKS * e
                    for i in range(4):
                        mat, m = i // 2, 2 * (h % 2) + i % 2
                        n = 0
                        for kb in range(KB):
                            for a, b in PASSES:
                                last = pe.matmul(bH[:, TOK * i:TOK * i + TOK],
                                                 w(first + 2 * mat + kb, a, 128 * m, 128), xmT[:, b, kb, :],
                                                 start=n == 0, stop=n == 5)
                                n += 1
                    last.then_inc(up_ready, 1)
                elif name == "m_down":
                    e = task[1]
                    pe.wait_ge(x0_drained, it.x0_at(task, 0))
                    pe.wait_ge(act_split, it.at(HALVES, 2 * e + 2))
                    first = MOE0 + MOE_CHUNKS * e + 4
                    n = 0
                    for m in range(EB):
                        for a, b in PASSES:
                            last = pe.matmul(bX0[0:TOK, 0:DIM], aT[:, a, m, :],
                                             w(first + m // 2, b, DIM * (m % 2), DIM), start=n == 0, stop=n == 11)
                            n += 1
                    last.then_inc(x0_filled, 1)
                elif name == "f_turn":
                    pe.wait_ge(xq_ready, it.at({"F": 1}, 1))
                    pe.matmul(bX1[:, 256:256 + TOK], fs[:, 2:3].to_broadcast([TOK, 128]), idf[0:TOK, 0:TOK],
                              start=True, stop=True)
                    for kb in range(KB):
                        last = pe.transpose(bX1h[:, TOK * kb:TOK * kb + TOK], xqh[:, 128 * kb:128 * kb + 128],
                                            idh[0:TOK, 0:TOK])
                    last.then_inc(x1_filled, 1)
                elif name == "f_up":
                    j = task[1]
                    for i in range(4):
                        for kb in range(KB):
                            last = pe.matmul(bX1[:, TOK * i:TOK * i + TOK],
                                             w_up[:, kb, 128 * (4 * j + i):128 * (4 * j + i) + 128],
                                             xqT[:, kb, :], start=kb == 0, stop=kb == 1)
                    last.then_inc(x1_filled, 1)
                elif name == "f_max":
                    j = task[1]
                    pe.wait_ge(ffn_act, it.at({"F": 2}, j + 1))
                    for i in range(4):
                        last = pe.transpose(bX1[0:TOK, 128 * i:128 * i + 128], hact[:, 4 * j + i, :], idf[:])
                    last.then_inc(x1_filled, 1)
                elif name == "f_rate":
                    pe.wait_ge(rate_ready, it.at({"F": 1}, 1))
                    pe.matmul(bX1[:, 0:TOK], fs[:, 6:7].to_broadcast([TOK, 128]), idf[0:TOK, 0:TOK],
                              start=True, stop=True).then_inc(x1_filled, 1)
                elif name == "f_down":
                    pe.wait_ge(q2_ready, it.at({"F": 1}, 1))
                    for b in range(FB):
                        last = pe.matmul(bX1[0:TOK, 0:DIM], q2T[:, b, :], w_down[:, b, :],
                                         start=b == 0, stop=b == FB - 1)
                    last.then_inc(x1_filled, 1)

            def between(n):
                if n == 1:
                    pe.wait_ge(w_split, MOE0)
                if n == 2:
                    pe.wait_ge(w_split, L1_Q)
                if n == 3:
                    pe.wait_ge(wsum_ready, 1)
                    pe.matmul(bS[:, 0:2], ones[:].to_broadcast([128, 128]), wtot[:], start=True,
                              stop=True).then_inc(wsum_spread, 1)
                    pe.wait_ge(w_split, CHUNKS)
                    pe.wait_ge(ffn_w_ready, 1)

            def body(it):
                for s, slot in enumerate(it.tasks):
                    k = s - 1 - it.lead
                    if 0 <= k < it.units:
                        scores(it, k)
                    for task in slot:
                        part(it, task)
                    if 2 <= k <= it.units + 1:
                        sum_values(it, k - 2)
                    if 1 <= k <= it.units:
                        turn_probs(it, k - 1)

            every_iteration(pe, body, between)

        @block.vector
        def _(dve):
            for t in (qT, PR, PT, kv[0], kv[1]):
                dve.memset(t[:], 0.0)
            for m in (mask[0], mask[1], hpad):
                last = dve.memset(m[:], 0.0)
            last.then_inc(zeros_set, 1)
            dve.wait_ge(gates_ready, 1)
            dve.wait_ge(consts_set, 2)
            dve.tensor_scalar(tgs[:], tgate[:], 1 / WSCALE, None, ALU.mult)
            dve.tensor_scalar(vec[:, V_GATED:V_GATED + 2 * KB], vec[:, V_GLAT:V_GLAT + 2 * KB], gates[:, 4:5],
                              None, ALU.mult).then_inc(gates_scaled, 1)
            dve.drain()

            def split_chunk(raw, hi, lo, c):
                dve.wait_ge(w_hi, c + 1)
                dve.scalar_tensor_tensor(lo, raw, WSCALE, hi, ALU.mult, ALU.subtract).then_inc(w_split, 1)

            def split_weights(a, b):
                for c in range(a, b):
                    split_chunk(W[:, (c + SHIFT) * CHUNK:(c + SHIFT + 1) * CHUNK], w(c, 0, 0, CHUNK),
                                w(c, 1, 0, CHUNK), c)

            def split_experts():
                with dve.Fori(0, EXPERTS) as e:
                    for i in range(MOE_CHUNKS):
                        c = e * MOE_CHUNKS + (MOE0 + i)
                        split_chunk(W[:, bass.ds((c + SHIFT) * CHUNK, CHUNK)],
                                    WH[:, bass.ds(c * (2 * CHUNK), CHUNK)],
                                    WH[:, bass.ds(c * (2 * CHUNK) + CHUNK, CHUNK)], c)

            def quantise_ffn_weights():
                for c in range(8):
                    dve.wait_ge(raw_loaded[c % 3], 16 * (c // 3 + 1))
                    dve.tensor_reduce(wabs[:, c:c + 1], staging[c % 3], AX.X, ALU.add,
                                      apply_absolute_value=True).then_inc(raw_used, 1)
                dve.drain()
                dve.tensor_reduce(wtot[:], wabs[:].rearrange("p (m c) -> p m c", m=2), AX.X, ALU.add)\
                    .then_inc(wsum_ready, 1)
                dve.wait_ge(wsum_spread, 1)
                dve.tensor_scalar(wmean[:], bS[:, 0:2], 1 / (FB * 128 * DIM), QMIN_SCALE, ALU.mult, ALU.max)
                dve.drain()
                dve.reciprocal(winv[:], wmean[:])
                dve.tensor_scalar(qfac[:, 0:1], wmean[:, 0:1], 1 / QMAX, None, ALU.mult)
                dve.tensor_scalar(qfac[:, 1:2], wmean[:, 1:2], 0.5 / QMAX, tgate[:, 3:4], ALU.mult, ALU.mult)
                dve.drain()
                for c in range(8, 16):
                    raw = staging[c % 3]
                    i = c - 8
                    dve.wait_ge(raw_loaded[c % 3], 16 * (c // 3 + 1))
                    dve.tensor_scalar(raw, raw, winv[:, i // 4:i // 4 + 1], ROUND, ALU.mult, ALU.add)
                    dve.drain()
                    dve.tensor_scalar(raw, raw, ROUND, -1.0, ALU.subtract, ALU.max)
                    dve.drain()
                    at = ffn0 + i * CHUNK
                    last = dve.tensor_scalar(WH[:, at:at + CHUNK], raw, 1.0, None, ALU.min)
                    last.then_inc(raw_used, 1)
                dve.drain()
                dve.memset(kv[1][:], 0.0).then_inc(ffn_w_ready, 1)
                dve.drain()

            def between(n):
                if n == 1:
                    split_weights(0, MOE0)
                if n == 2:
                    split_experts()
                if n == 3:
                    split_weights(L1_Q, CHUNKS)
                    quantise_ffn_weights()

            def mask_scores(it, k):
                layer = it.group_of(k)[0]
                made, split = (dve.to_reg(it.at(UNITS, n)) for n in (k + 1, k - 1))
                dve.wait_ge(zeros_set, 1)
                dve.wait_ge(probs_split, split)
                dve.wait_ge(scores_ready, made)
                dve.tensor_tensor_reduce(out=S[0:TOK, k % 2, 0:KEYS], in0=bS[0:TOK, 0:KEYS],
                                         in1=mask[layer][:, 0:KEYS], scale=1.0, scalar=3.0e38,
                                         op0=ALU.add, op1=ALU.min,
                                         accum_out=rmin[0:TOK, k % 2:k % 2 + 1]).then_inc(scores_masked, 1)

            def norm_out(it, k):
                layer, group, _ = it.group_of(k)
                dve.wait_ge(values_summed, it.at(UNITS, k + 1))
                dve.reciprocal(rinv[0:TOK, :], rsum[0:TOK, layer + group, :])
                dve.drain()
                dve.tensor_tensor(wide[0:TOK, :].rearrange("p (h d) -> p h d", h=HEADS),
                                  bO[0:TOK, :].rearrange("p (h d) -> p h d", h=HEADS),
                                  rinv[0:TOK, :].rearrange("p (h o) -> p h o", o=1).to_broadcast([TOK, HEADS, HD]),
                                  ALU.mult).then_inc(out_normed, 1)

            def stats(stage, x, col):
                dve.bn_stats(bn[0:TOK, col, :], x[:])
                dve.drain()
                return dve.bn_aggr(mv[stage][0:TOK, col, :], bn[0:TOK, col, :])

            def norm_kv(it, stage, x):
                layer = "PB".index(stage)
                loaded, each = (p_loaded, 48) if stage == "P" else (b_loaded, 32)
                dve.wait_ge(loaded, it.at({stage: each}, each))
                for t in range(CT):
                    dve.bn_stats(bn[0:CP, t, :], ctxb[0:CP, t, :])
                dve.bn_stats(bn[0:TOK, CT, :], x[:])
                dve.drain()
                for t in range(CT):
                    dve.bn_aggr(mv[stage][0:CP, t, :], bn[0:CP, t, :])
                dve.bn_aggr(mv[stage][0:TOK, CT, :], bn[0:TOK, CT, :]).then_inc(stats_ready[stage], 1)
                a, b = (MASKED, 0.0) if layer == 0 else (-MASKED, MASKED)
                dve.tensor_scalar(mask[layer][:, TOK:KEYS], mask8[:], a, b, ALU.mult, ALU.add)

            def apply_kv(it, stage, x):
                dve.wait_ge(rstd_ready[stage], it.at({stage: 1}, 1))
                r = rs[stage]
                for t in range(CT):
                    last = dve.tensor_scalar(ctxb[0:CP, t, :], ctxb[0:CP, t, :], mv[stage][0:CP, t, 0:1],
                                             r[0:CP, t:t + 1], ALU.subtract, ALU.mult)
                last.then_inc(norm_ready[stage], 1)
                dve.tensor_scalar(xn[:], x[:], mv[stage][0:TOK, CT, 0:1], r[0:TOK, CT:CT + 1],
                                  ALU.subtract, ALU.mult).then_inc(norm_ready[stage], 1)

            def apply_x(it, stage, x):
                dve.wait_ge(rstd_ready[stage], it.at({stage: 1}, 1))
                return dve.tensor_scalar(xn[:], x[:], mv[stage][0:TOK, 0, 0:1], rs[stage][0:TOK, 0:1],
                                         ALU.subtract, ALU.mult)

            def rank_experts(it, task):
                v1, v2 = rsc[:, 0:1], rsc[:, 1:2]
                dve.wait_ge(x0_filled, it.x0_at(task))
                dve.tensor_copy(lg[:], bX0[0:TOK, 0:EXPERTS]).then_inc(x0_drained, 1)
                dve.drain()
                for i, (s, v) in enumerate(((lg, v1), (s2, v2))):
                    dve.tensor_reduce(v, s[:], AX.X, ALU.max)
                    dve.drain()
                    dve.scalar_tensor_tensor(rk[:, i, :], s[:], v, rev[:], ALU.is_equal, ALU.mult)
                    dve.drain()
                    dve.tensor_reduce(rsc[:, 2 + i:3 + i], rk[:, i, :], AX.X, ALU.max)
                    dve.drain()
                    dve.tensor_scalar(one[:, i, :], rk[:, i, :], rsc[:, 2 + i:3 + i], None, ALU.is_equal)
                    dve.tensor_scalar(gk[:, i, :], lg[:], -1.0, v, ALU.mult, ALU.max)
                    last = dve.tensor_scalar(sh[:, i, :], lg[:], v, 0.0, ALU.subtract, ALU.min)
                    if i == 0:
                        dve.drain()
                        dve.scalar_tensor_tensor(s2[:], one[:, 0, :], -3.0e38, lg[:], ALU.mult, ALU.add)
                        dve.drain()
                dve.drain()
                for i in range(2):
                    dve.tensor_tensor(gk[:, i, :], gk[:, i, :], lg[:], ALU.max)
                dve.drain()
                dve.scalar_tensor_tensor(gk[:], gk[:], JITTER, sh[:], ALU.mult, ALU.add)\
                    .then_inc(route_shifted, 1)

            def weigh_experts(it):
                dve.wait_ge(route_exp, it.at({"M": 1}, 1))
                dve.scalar_tensor_tensor(rk[:, 0, :], gk[:, 0, :], 0.0, sh[:, 0, :], ALU.is_ge, ALU.mult,
                                         accum_out=rsc[:, 4:5])
                dve.scalar_tensor_tensor(rk[:, 1, :], gk[:, 1, :], 0.0, sh[:, 1, :], ALU.is_ge, ALU.mult)
                dve.drain()
                dve.scalar_tensor_tensor(gk[:, 1, :], one[:, 0, :], 0.5, rk[:, 1, :], ALU.is_lt, ALU.mult,
                                         accum_out=rsc[:, 5:6])
                dve.drain()
                dve.reciprocal(rsc[:, 6:8], rsc[:, 4:6])
                dve.drain()
                dve.tensor_scalar(dw[:], one[:, 0, :], rsc[:, 6:7], None, ALU.mult)
                dve.drain()
                dve.scalar_tensor_tensor(dw[:], one[:, 1, :], rsc[:, 7:8], dw[:], ALU.mult, ALU.add)
                dve.drain()
                dve.tensor_scalar(dw[:], dw[:], tgs[0:TOK, 2:3], None, ALU.mult)
                dve.drain()

            def quantise(dst, src, scale_col, tmp):
                dve.tensor_scalar(tmp, src, scale_col, ROUND, ALU.mult, ALU.add)
                dve.drain()
                return dve.tensor_scalar(dst, tmp, ROUND, None, ALU.subtract)

            def part(it, task):
                name = task[0]
                if name == "q":
                    p = task[1]
                    dve.wait_ge(q_hi, it.at(PAIR, p + 1))
                    for h in range(2):
                        r = slice(64 * h, 64 * h + 64)
                        last = dve.scalar_tensor_tensor(qT[r, p % 2, h, 1, 0:TOK], bX0[r, 0:TOK],
                                                        -0.125 / WSCALE, qT[r, p % 2, h, 0, 0:TOK],
                                                        ALU.mult, ALU.subtract)
                    last.then_inc(x0_drained, 1)
                elif name == "k":
                    p = task[1]
                    dve.wait_ge(k_hi, it.at(PAIR, p + 1))
                    dve.scalar_tensor_tensor(kT[:, p % 2, 1, :], bK[:, 0:KW], 1 / WSCALE, kT[:, p % 2, 0, :],
                                             ALU.mult, ALU.subtract).then_inc(k_split, 1)
                elif name == "v":
                    p = task[1]
                    dve.wait_ge(v_hi, it.at(PAIR, p + 1))
                    dve.scalar_tensor_tensor(vN[:, p % 2, 1].rearrange("p t d -> p (t d)"), bV[:], 1 / WSCALE,
                                             vN[:, p % 2, 0].rearrange("p t d -> p (t d)"),
                                             ALU.mult, ALU.subtract).then_inc(v_split, 1)
                elif name == "p_norm":
                    norm_kv(it, "P", xa)
                elif name == "b_norm":
                    norm_kv(it, "B", xm)
                elif name in ("m_norm", "f_norm"):
                    stats(name[0].upper(), x1 if name == "m_norm" else xf, 0)\
                        .then_inc(stats_ready[name[0].upper()], 1)
                elif name == "p_apply":
                    apply_kv(it, "P", xa)
                elif name == "b_apply":
                    apply_kv(it, "B", xm)
                elif name == "m_apply":
                    apply_x(it, "M", x1).then_inc(norm_ready["M"], 1)
                elif name in ("p_turn", "b_turn"):
                    layer, kb = int(name == "b_turn"), task[1]
                    stage = "PB"[layer]
                    c = 8 * layer + kb
                    dve.wait_ge(kv_hi[layer], it.at({stage: 3}, kb + 1))
                    dve.tensor_scalar(wide[:, 0:CTX], bX1[:, 0:CTX], vec[:, c + V_GAMMA:c + V_GAMMA + 1],
                                      vec[:, c + V_BETA:c + V_BETA + 1], ALU.mult, ALU.add).then_inc(x1_drained, 1)
                    dve.drain()
                    dve.tensor_tensor(kv[layer][:, kb, 1, TOK:KEYS], wide[:, 0:CTX],
                                      kv[layer][:, kb, 0, TOK:KEYS], ALU.subtract)
                    dve.drain()
                elif name in ("p_lat", "b_lat"):
                    layer = int(name == "b_lat")
                    stage = "PB"[layer]
                    dve.wait_ge(kv_hi[layer], it.at({stage: 3}, 3))
                    places = latents_of(layer)
                    n = KB * TOK
                    for i, (_, c) in enumerate(places):
                        for kb in range(KB):
                            at = n * i + TOK * kb
                            last = dve.tensor_scalar(wide[:, at:at + TOK], bX1[:, TOK * kb:TOK * kb + TOK],
                                                     vec[:, c + kb:c + kb + 1],
                                                     vec[:, c + KB + kb:c + KB + kb + 1], ALU.mult, ALU.add)
                    last.then_inc(x1_drained, 1)
                    dve.drain()
                    for i, (dst, _) in enumerate(places):
                        last = dve.tensor_tensor(dst[:, :, 1, :],
                                                 wide[:, n * i:n * i + n].rearrange("p (k t) -> p k t", k=KB),
                                                 dst[:, :, 0, :], ALU.subtract)
                    last.then_inc(kv_ready[layer], 1)
                    if layer == 1:
                        dve.tensor_copy(xb[:], xm[:])
                elif name == "o_turn":
                    dve.wait_ge(o_hi, it.at({"A": 1, "B": 1, "F": 1}, [t for t in it.x1 if t[0] == name].index(task) + 1))
                    dve.tensor_tensor(oT[:, 1], bX1[:, 0:4 * TOK].rearrange("p (m t) -> p m t", m=4),
                                      oT[:, 0], ALU.subtract).then_inc(x1_drained, 1)
                elif name == "o_proj":
                    dve.wait_ge(x1_filled, it.x1_at(task))
                    dst, src, g = {"A": (x1, xa, 0), "B": (xb, xb, 1), "F": (xf, xb, 1)}[task[1]]
                    if task[1] == "F":
                        dve.wait_ge(stored, it.at({"F": 16}, 0))
                    dve.scalar_tensor_tensor(dst[:], bX1[0:TOK, 0:DIM], tgs[0:TOK, g:g + 1], src[:],
                                             ALU.mult, ALU.add).then_inc(x1_drained, 1)
                    dve.drain()
                    if task[1] == "A":
                        dve.memset(fs[:, 7:8], 0.0).then_inc(x1_ready, 1)
                elif name == "m_turn":
                    dve.wait_ge(moe_hi, it.at({"M": 1}, 1))
                    dve.tensor_copy(xmF[:], bX1[:, 0:KB * TOK].rearrange("p (k t) -> p k t", k=KB))\
                        .then_inc(x1_drained, 1)
                    dve.drain()
                    dve.tensor_tensor(xmT[:, 1], xmF[:], xmT[:, 0], ALU.subtract).then_inc(moe_ready, 1)
                elif name == "m_gate":
                    rank_experts(it, task)
                elif name == "m_route":
                    weigh_experts(it)
                elif name == "m_up":
                    h = task[1]
                    n = 2 * TOK
                    dve.wait_ge(tanh_ready, it.at(HALVES, h + 1))
                    dve.scalar_tensor_tensor(act, act, 1.0, bH[:, 0:n], ALU.add, ALU.mult)
                    dve.drain()
                    dve.scalar_tensor_tensor(act, act, 0.5 / (WSCALE * WSCALE), bH[:, n:2 * n],
                                             ALU.mult, ALU.mult).then_inc(gated, 1)
                elif name == "m_down":
                    e = task[1]
                    dve.wait_ge(x0_filled, it.x0_at(task))
                    dve.scalar_tensor_tensor(xm[:], bX0[0:TOK, 0:DIM], dw[:, e:e + 1], (x1 if e == 0 else xm)[:],
                                             ALU.mult, ALU.add).then_inc(x0_drained, 1)
                    dve.drain()
                elif name == "f_apply":
                    apply_x(it, "F", xf)
                    dve.drain()
                    dve.tensor_reduce(fs[:, 0:1], xn[:], AX.X, ALU.max, apply_absolute_value=True)
                    dve.drain()
                    dve.tensor_scalar(fs[:, 0:1], fs[:, 0:1], QMIN_SCALE, None, ALU.max)
                    dve.drain()
                    dve.reciprocal(fs[:, 1:2], fs[:, 0:1])
                    dve.tensor_scalar(fs[:, 2:3], fs[:, 0:1], qfac[0:TOK, 0:1], None, ALU.mult)
                    dve.drain()
                    dve.tensor_scalar(fs[:, 1:2], fs[:, 1:2], QMAX, None, ALU.mult)
                    dve.drain()
                    quantise(xqh, xn[:], fs[:, 1:2], xn[:]).then_inc(xq_ready, 1)
                elif name == "f_turn":
                    dve.wait_ge(x1_filled, it.x1_at(task))
                    dve.tensor_copy(xqT, bX1h[:, 0:KB * TOK].rearrange("p (k t) -> p k t", k=KB))
                    dve.tensor_copy(rate[:], bX1[:, 256:256 + TOK]).then_inc(x1_drained, 1)
                    dve.memset(hpad[:, :, 0:1], 0.0)
                    dve.memset(hpad[:, :, TOK + 1:TOK + 2], 0.0)
                    dve.drain()
                elif name == "f_up":
                    j = task[1]
                    dve.wait_ge(x1_filled, it.x1_at(task))
                    dve.tensor_tensor(hpad[:, :, 1:TOK + 1], bX1[:, 0:4 * TOK].rearrange("p (m t) -> p m t", m=4),
                                      rate[:].rearrange("p (o t) -> p o t", o=1).to_broadcast([128, 4, TOK]),
                                      ALU.mult).then_inc(x1_drained, 1)
                elif name == "f_conv":
                    j = task[1]
                    dve.wait_ge(conv_begun, it.at({"F": 2}, j + 1))
                    for tap in (1, 2):
                        for i in range(4):
                            b = 4 * j + i
                            c = V_CONVW + FB * tap + b
                            last = dve.scalar_tensor_tensor(hact[:, b, :], hpad[:, i, tap:tap + TOK], vec[:, c:c + 1],
                                                            hact[:, b, :], ALU.mult, ALU.add)
                        if tap == 1:
                            dve.drain()
                    last.then_inc(conv_done, 1)
                elif name == "f_act":
                    j = task[1]
                    dve.wait_ge(ffn_tanh, it.at({"F": 2}, j + 1))
                    dve.scalar_tensor_tensor(hact[:, 4 * j:4 * j + 4, :], hpad[:, :, 1:TOK + 1], 1.0,
                                             hact[:, 4 * j:4 * j + 4, :], ALU.add, ALU.mult).then_inc(ffn_act, 1)
                    dve.drain()
                elif name == "f_max":
                    j = task[1]
                    dve.wait_ge(x1_filled, it.x1_at(task))
                    dve.tensor_reduce(fs[:, 3 + j:4 + j], bX1[0:TOK, :], AX.X, ALU.max,
                                      apply_absolute_value=True).then_inc(x1_drained, 1)
                    if j == 1:
                        dve.drain()
                        dve.tensor_scalar(fs[:, 5:6], fs[:, 3:4], fs[:, 4:5], 2 * QMIN_SCALE, ALU.max, ALU.max)
                        dve.drain()
                        dve.reciprocal(fs[:, 6:7], fs[:, 5:6])
                        dve.tensor_scalar(fs[:, 5:6], fs[:, 5:6], qfac[0:TOK, 1:2], None, ALU.mult)
                        dve.drain()
                        dve.tensor_scalar(fs[:, 6:7], fs[:, 6:7], QMAX, None, ALU.mult).then_inc(rate_ready, 1)
                elif name == "f_rate":
                    dve.wait_ge(x1_filled, it.x1_at(task))
                    dve.tensor_copy(rate[:], bX1[:, 0:TOK]).then_inc(x1_drained, 1)
                    dve.drain()
                    dve.tensor_tensor(hact[:], hact[:],
                                      rate[:].rearrange("p (o t) -> p o t", o=1).to_broadcast([128, FB, TOK]), ALU.mult)
                    dve.drain()
                    dve.tensor_scalar(hact[:], hact[:], ROUND, None, ALU.add)
                    dve.drain()
                    dve.tensor_scalar(q2T, hact[:], ROUND, None, ALU.subtract).then_inc(q2_ready, 1)
                elif name == "f_down":
                    dve.wait_ge(x1_filled, it.x1_at(task))
                    dve.scalar_tensor_tensor(xf[:], bX1[0:TOK, 0:DIM], fs[:, 5:6], xf[:], ALU.mult, ALU.add)\
                        .then_inc(x1_drained, 1)
                    dve.drain()
                    dve.memset(fs[:, 7:8], 0.0).then_inc(out_ready, 1)

            def body(it):
                for s, tasks in enumerate(it.taken_up()):
                    k = s - 1 - it.lead
                    if 0 <= k < it.units:
                        mask_scores(it, k)
                    for task in tasks:
                        part(it, task)
                    if 2 <= k <= it.units + 1 and (k - 2) % HEADS == HEADS - 1:
                        norm_out(it, k - 2)

            every_iteration(dve, body, between)


def kernel(x, ctx_1024, mask_BxS2_bk0, g_xattn, g_ffn, L0_xattn_kv_gate, L0_xattn_gamma_media,
           L0_xattn_beta_media, L0_xattn_gamma_lat, L0_xattn_beta_lat, L0_xattn_Wq, L0_xattn_Wk,
           L0_xattn_Wv, L0_xattn_Wout, L0_ffn_gate_w, L0_ffn_w1, L0_ffn_w2, L0_ffn_w3, L1_xattn_g1,
           L1_xattn_b1, L1_xattn_g2, L1_xattn_b2, L1_xattn_Wq, L1_xattn_Wkv, L1_xattn_Wout,
           L1_ffn_w1, L1_ffn_conv_w, L1_ffn_conv_b, L1_ffn_w2):
    import numpy as np
    import concourse.bacc as bacc
    from concourse.bass_utils import run_bass_kernel_spmd

    arr = np.asarray

    def rows(m):
        m = arr(m)
        return m.reshape(m.shape[0] // 128, 128, m.shape[1]).transpose(1, 0, 2)

    def flat(m):
        return rows(m).reshape(128, -1)

    inner = L1_xattn_Wq.shape[1]
    experts = []
    for e in range(L0_ffn_w1.shape[0]):
        experts += [flat(arr(L0_ffn_w1)[e].T), flat(arr(L0_ffn_w3)[e].T), flat(arr(L0_ffn_w2)[e].T)]
    weights = np.concatenate(
        [flat(L0_xattn_Wq), flat(L0_xattn_Wk), flat(L0_xattn_Wv), flat(L0_xattn_Wout)] + experts +
        [flat(L1_xattn_Wq), flat(arr(L1_xattn_Wkv)[:, :inner]), flat(arr(L1_xattn_Wkv)[:, inner:]),
         flat(L1_xattn_Wout)], axis=1)
    ffn = np.concatenate([flat(arr(L1_ffn_w1).T), flat(arr(L1_ffn_w2).T)], axis=1)

    def cols(v):
        v = arr(v)
        return v.reshape(-1, 128).T

    conv_w = arr(L1_ffn_conv_w)[:, 0, :]
    vectors = np.concatenate(
        [cols(v) for v in (L0_xattn_gamma_media, L0_xattn_beta_media, L0_xattn_gamma_lat,
                           L0_xattn_beta_lat, L1_xattn_g1, L1_xattn_b1, L1_xattn_g2, L1_xattn_b2)] +
        [cols(conv_w[:, t]) for t in range(3)] + [cols(L1_ffn_conv_b)], axis=1)
    gates = np.concatenate([arr(g_xattn), arr(g_ffn), arr(L0_xattn_kv_gate).reshape(1)]).reshape(1, 5)
    arrays = {
        "x": arr(x), "ctx": arr(ctx_1024), "mask": arr(mask_BxS2_bk0).reshape(NSEQ, 1, CTX),
        "weights": weights, "ffn_weights": ffn, "vectors": vectors,
        "router": rows(arr(L0_ffn_gate_w).T), "gates": gates,
    }
    arrays = {f"in_{k}": np.ascontiguousarray(v) for k, v in arrays.items()}
    nc = bacc.Bacc("TRN2", target_bir_lowering=False, num_devices=1)
    args = [nc.dram_tensor(k, v.shape, mybir.dt.from_np(v.dtype), kind="ExternalInput").ap()
            for k, v in arrays.items()]
    out = nc.dram_tensor("out_y", (NSEQ, TOK, DIM), F32, kind="ExternalOutput").ap()
    build(nc, *args, out)
    r = run_bass_kernel_spmd(nc, [arrays], core_ids=[0])
    return r.results[0]["out_y"]
```

```python
from contextlib import ExitStack

import concourse.bass as bass
from concourse import mybir

F32 = mybir.dt.float32
F16 = mybir.dt.float16
BF16 = mybir.dt.bfloat16
U8 = mybir.dt.uint8
ALU = mybir.AluOpType
ACT = mybir.ActivationFunctionType
AX = mybir.AxisListType

NSEQ, TOK, DIM = 16, 112, 256
CTX = 375
CT, CP = 3, 125
KEYS = TOK + CTX
KW = 488
KB = 2
HEADS, HD = 8, 64
PAIRS = 4
EXPERTS, EB = 8, 4
FB = 8
CHUNK = 512
WSCALE = 64.0
LN_EPS = 1e-5
MASKED = 1e30
ROUND = 12582912.0
QMAX = 127.0
QMIN_SCALE = 1e-5
JITTER = 0.02

L0_Q, L0_K, L0_V, L0_O = 0, 2, 4, 6
MOE0 = 8
MOE_CHUNKS = 6
L1_Q = MOE0 + EXPERTS * MOE_CHUNKS
L1_K, L1_V, L1_O = L1_Q + 4, L1_Q + 8, L1_Q + 12
CHUNKS = L1_Q + 16
SHIFT = 2
FFN_CHUNKS = 8
FFN_WORDS = (KB * FB * 128 + FB * DIM) // 2

V_GAMMA, V_BETA, V_GLAT, V_BLAT = 0, 2, 4, 6
V_CONVW, V_CONVB = 16, 16 + 3 * FB
NVEC = V_CONVB + FB
V_GATED = NVEC

OFFSET = {"P": 0, "A": 1, "M": 2, "B": 3, "F": 4}
LOOP = (5, 16)
LAST = NSEQ + OFFSET["F"]
SLOTS = 24
MOE_UP = (0, 1, 3, 4, 7, 8, 9, 10, 11, 12, 13, 14, 15, 17, 19, 20)
MOE_DOWN = (3, 5, 9, 11, 13, 15, 19, 21)
FIRST_OF_B = HEADS

UNITS = {"A": HEADS, "B": 2 * HEADS}
PAIR = {"A": PAIRS, "B": 2 * PAIRS}
GROUP = {"A": 1, "B": 2}
HALVES = {"M": 2 * EXPERTS}


class Iteration:

    def __init__(self, n, like, shift=0):
        self.n, self.like, self.shift = n, like, shift
        self.on = {s for s, o in OFFSET.items() if o <= like < o + NSEQ}
        self.lead = FIRST_OF_B if "A" not in self.on else 0
        self.tasks = timeline(self.on, self.lead)
        flat = [t for slot in sorted(self.tasks) for t in self.tasks[slot]]
        self.x0 = [t for t in flat if t[0] in X0_TASKS]
        self.x1 = [t for t in flat if t[0] in X1_TASKS]
        self.units = sum(UNITS[s] for s in "AB" if s in self.on)

    def beside(self, step):
        if isinstance(self.n, int):
            return Iteration(self.n + step, self.like + step)
        return Iteration(self.n, self.like + step, self.shift + step)

    def at(self, per, local=0):
        if isinstance(self.n, int):
            past = {s: min(max(self.n - OFFSET[s], 0), NSEQ) for s in per}
            return max(0, sum(k * past[s] for s, k in per.items()) + local)
        slope = sum(per.values())
        return self.n * slope + (self.shift * slope + local - sum(k * OFFSET[s] for s, k in per.items()))

    def x0_at(self, task, local=1):
        return self.at(X0_PER, self.x0.index(task) + local)

    def x1_at(self, task, local=1):
        return self.at(X1_PER, self.x1.index(task) + local)

    def seq(self, stage):
        return self.n + (self.shift - OFFSET[stage])

    def slots(self):
        after = self.beside(1)
        for s in range(SLOTS):
            both = [(self, t) for t in self.tasks.get(s, [])]
            both += [(after, t) for t in after.tasks.get(s - SLOTS, [])]
            yield sorted(both, key=lambda x: ORDER.index(x[1][0]) if x[1][0] in ORDER else len(ORDER))

    def unit(self, slot, lag=0):
        it, k = (self, slot - lag) if slot >= lag else (self.beside(-1), slot - lag + SLOTS)
        return [(it, k - it.lead)] if 0 <= k - it.lead < it.units else []

    def taken_up(self):
        own = ("m_up",) + APPLIES + NORMS
        first = ("o_proj", "b_keep", "m_down")
        *_, before = self.beside(-1).slots()
        for slot in self.slots():
            late = [x for x in before if x[1][0] not in own][::-1]
            yield ([x for name in first for x in late if x[1][0] == name],
                   [x for x in late if x[1][0] not in LONG + first] +
                   [x for x in late if x[1][0] in LONG] +
                   [x for name in own for x in slot if x[1][0] == name])
            before = slot

    def group_of(self, unit):
        return self.pair_group(unit // 2)

    def pair_group(self, pair):
        if "A" in self.on:
            if pair < PAIRS:
                return 0, 0, pair
            pair -= PAIRS
        return 1, pair // PAIRS, pair % PAIRS


ORDER = ("k", "v", "m_up", "q", "m_gate", "m_down")
NORMS = ("p_norm", "m_norm", "b_norm", "f_norm")
APPLIES = ("p_apply", "m_apply", "b_apply", "f_apply")
X0_TASKS = ("q", "m_gate", "m_down")
X1_TASKS = ("p_turn", "p_lat", "b_turn", "b_lat", "o_turn", "o_proj", "m_turn",
            "f_turn", "f_up", "f_max", "f_rate", "f_down")
X0_PER = {"A": PAIRS, "B": 2 * PAIRS, "M": 1 + EXPERTS}
LAST_OF_SLOT = ("m_gate", "m_down") + X1_TASKS
LONG = ("m_gate", "m_route", "f_rate", "f_conv", "p_lat", "b_lat")
X1_PER = {"P": 3, "B": 3 + 2, "A": 2, "M": 1, "F": 2 + 7}


def timeline(on, lead):
    slots = {}

    def put(slot, *task):
        slots.setdefault(slot, []).append(task)

    for p in range(sum(PAIR[s] for s in "AB" if s in on)):
        put(lead + 2 * p - 2, "k", p)
        put(lead + 2 * p - 2, "q", p)
        put(lead + 2 * p - 1, "v", p)
    if "A" in on:
        put(10, "o_turn", "A")
        put(14, "o_proj", "A")
    if "B" in on:
        put(-2, "b_norm")
        put(-1, "b_apply")
        put(0, "b_turn", 0)
        put(1, "b_turn", 1)
        put(3, "b_keep")
        put(4, "b_lat")
        put(FIRST_OF_B + HEADS + 2, "o_turn", "B")
        put(FIRST_OF_B + HEADS + 4, "o_proj", "B")
    if "M" in on:
        put(-6, "m_norm")
        put(-4, "m_apply")
        put(-2, "m_turn")
        put(-1, "m_gate")
        put(1, "m_route")
        for h, slot in enumerate(MOE_UP):
            put(slot, "m_up", h)
        for e, slot in enumerate(MOE_DOWN):
            put(slot, "m_down", e)
    if "F" in on:
        put(2, "o_turn", "F")
        put(3, "o_proj", "F")
        put(4, "f_norm")
        put(6, "f_apply")
        put(7, "f_turn")
        for j in range(2):
            put(8 + 4 * j, "f_up", j)
            put(9 + 4 * j, "f_conv", j)
            put(11 + 4 * j, "f_act", j)
            put(13 + 4 * j, "f_max", j)
        put(19, "f_rate")
        put(21, "f_down")
    if "P" in on:
        put(5, "p_norm")
        put(7, "p_apply")
        put(11, "p_turn", 0)
        put(15, "p_turn", 1)
        put(16, "p_lat")
    return slots


def build(nc, x_in, ctx_in, mask_in, weights_in, ffn_in, vectors_in, router_in, gates_in, out):
    with ExitStack() as stack:
        def sb(name, shape, dt=F32):
            return stack.enter_context(nc.sbuf_tensor(name, shape, dt))

        def ps(name):
            return stack.enter_context(nc.psum_tensor(name, [128, 512], F32))

        def sem(name):
            return stack.enter_context(nc.semaphore(name))

        W = sb("weights", [128, CHUNKS * CHUNK + FFN_WORDS])
        WH = W[:].bitcast(F16)
        ffn0 = CHUNKS * 2 * CHUNK
        w_up = WH[:, ffn0:ffn0 + KB * FB * 128].rearrange("p (k c) -> p k c", k=KB)
        w_down = WH[:, ffn0 + KB * FB * 128:ffn0 + KB * FB * 128 + FB * DIM].rearrange(
            "p (k c) -> p k c", k=FB)
        vec = sb("vectors", [128, NVEC + 2 * KB])
        gates = sb("gates", [128, 5])
        tgate = sb("tanh_gates", [128, 4])
        tgs = sb("tanh_gates_unscaled", [128, 4])
        router = sb("router", [128, KB, EXPERTS])
        idf = sb("identity_f32", [128, 128])
        idh = sb("identity_f16", [128, 128], F16)
        minus_half = sb("minus_half", [128, 4])
        growth = sb("var_growth", [128, CT + 1])
        bias = sb("var_bias", [128, CT + 1])
        ones = sb("ones", [128, 1])
        rev = sb("rev_index", [TOK, EXPERTS])
        wabs = sb("weight_abs_sums", [128, 8])
        wtot = sb("weight_abs_total", [128, 2])
        wmean = sb("weight_means", [128, 2])
        winv = sb("weight_inverse_means", [128, 2])
        qfac = sb("dequant_factors", [128, 2])

        kv = {0: sb("kv_A", [128, KB, 2, 512], F16), 1: sb("kv_B", [128, KB, 2, 512], F16)}
        latq = sb("latents_A", [128, KB, 2, TOK], F16)
        kT = sb("keys", [128, 2, 2, KW], F16)
        vN = sb("values", [128, 2, 2, 4, 128], F16)
        qT = sb("queries", [128, 2, 2, 2, 128], F16)
        S = sb("scores", [128, 2, KEYS + 1])
        PR = sb("probs", [128, 2, 2, 512], F16)
        PT = sb("probs_turned", [128, 2, 4, 128], F16)
        mask = {0: sb("mask_A", [TOK, KEYS + 1], BF16), 1: sb("mask_B", [TOK, KEYS + 1], BF16)}
        mask8 = sb("mask_bytes", [TOK, CTX], U8)
        rmin = sb("score_min", [128, 2])
        rsum = sb("prob_sums", [128, 3, HEADS])
        rinv = sb("prob_sum_inverse", [128, HEADS])
        wide = sb("wide", [128, 512])
        oT = sb("heads_turned", [128, 2, 4, TOK], F16)
        ctxb = sb("context", [128, CT, DIM])
        xp = sb("x_P", [TOK, DIM])
        xa = sb("x_A", [TOK, DIM])
        x1 = sb("x_after_A", [TOK, DIM])
        xm = sb("x_M", [TOK, DIM])
        xb = sb("x_B", [TOK, DIM])
        xf = sb("x_F", [TOK, DIM])
        xn = sb("x_normed", [TOK, DIM])
        bn = sb("bn_stats", [128, 4, 6])
        mv = {s: sb(f"mean_var_{s}", [128, 4, 2]) for s in "PBMF"}
        rs = {s: sb(f"rstd_{s}", [128, CT + 1]) for s in "PBMF"}
        xmF = sb("moe_in_f32", [128, KB, TOK])
        xmT = sb("moe_in", [128, 2, KB, TOK], F16)
        act = xmF[:].rearrange("p k t -> p (k t)")
        aT = sb("moe_hidden", [128, 2, EB, TOK], F16)
        rsc = sb("route_scalars", [TOK, 8])
        dw = sb("dense_weights", [TOK, EXPERTS])
        hpad = sb("ffn_hidden_padded", [128, 4, TOK + 2])
        hact = sb("ffn_hidden", [128, FB, TOK])
        q2T = hpad[:].rearrange("p a b -> p (a b)").bitcast(F16)[:, 0:FB * TOK].rearrange(
            "p (k t) -> p k t", k=FB)
        rate = sb("ffn_rate", [128, TOK])
        fs = sb("ffn_scalars", [TOK, 8])
        hact16 = hact[:].rearrange("p a b -> p (a b)").bitcast(F16)
        xqh = hact16[0:TOK, 8 * TOK:8 * TOK + DIM]
        xqT = hact16[:, 12 * TOK:12 * TOK + KB * TOK].rearrange("p (k t) -> p k t", k=KB)
        scratch = hact[0:TOK].rearrange("p a b -> p (a b)")
        lg, s2 = (scratch[:, EXPERTS * i:EXPERTS * i + EXPERTS] for i in range(2))
        rk, one, sh, gk = (scratch[:, 2 * EXPERTS * i:2 * EXPERTS * i + 2 * EXPERTS].rearrange(
            "p (a e) -> p a e", a=2) for i in range(1, 5))
        affine = {0: wide, 1: hact[:].rearrange("p a b -> p (a b)")[:, TOK:TOK + 512]}
        kvb_flat = kv[1][:].rearrange("p a b c -> p (a b c)").bitcast(F32)

        def raw(c):
            if c < CHUNKS - SHIFT:
                return W[:, (c + SHIFT) * CHUNK:(c + SHIFT + 1) * CHUNK]
            at = (c - CHUNKS + SHIFT) * CHUNK
            return kvb_flat[:, at:at + CHUNK]

        def raw_ffn(i):
            at = (CHUNKS - FFN_CHUNKS + i) * CHUNK
            return W[:, at:at + CHUNK]

        bS, bT, bO, bK, bV, bH, bX0, bX1 = (ps(n) for n in (
            "bank_scores", "bank_turn", "bank_out", "bank_keys", "bank_values", "bank_hidden",
            "bank_x0", "bank_x1"))
        bT16 = bT[:].bitcast(F16)[:, 0:2 * 4 * TOK].rearrange("p (a t c) -> p a t c", a=2, t=4)
        bX1h = bX1[:].bitcast(F16)

        consts_set = sem("consts_set")
        zeros_set = sem("zeros_set")
        vectors_loaded = sem("vectors_loaded")
        gates_ready = sem("gates_ready")
        gates_scaled = sem("gates_scaled")
        w_loaded = {c: sem(f"weights_loaded_{c}") for c in (0, *range(MOE0, L1_Q, MOE_CHUNKS), L1_Q)}
        w_hi, w_split = sem("weights_hi"), sem("weights_split")
        ffn_loaded = sem("ffn_weights_loaded")
        wsum_ready, wsum_spread, ffn_w_ready = sem("wsum_ready"), sem("wsum_spread"), sem("ffn_w_ready")
        p_loaded, b_loaded, a_loaded = sem("p_loaded"), sem("b_loaded"), sem("a_loaded")
        mask_loaded = {0: sem("mask_loaded_A"), 1: sem("mask_loaded_B")}
        stored = sem("stored")

        stats_ready = {s: sem(f"stats_ready_{s}") for s in "PBMF"}
        rstd_ready = {s: sem(f"rstd_ready_{s}") for s in "PBMF"}
        norm_ready = {s: sem(f"norm_ready_{s}") for s in "PBM"}
        kv_hi = {0: sem("kv_hi_A"), 1: sem("kv_hi_B")}
        kv_ready = {0: sem("kv_ready_A"), 1: sem("kv_ready_B")}

        k_ready, k_hi, k_split = sem("k_ready"), sem("k_hi"), sem("k_split")
        v_ready, v_hi, v_split = sem("v_ready"), sem("v_hi"), sem("v_split")
        q_hi = sem("q_hi")
        scores_ready, scores_masked = sem("scores_ready"), sem("scores_masked")
        probs_ready, probs_split = sem("probs_ready"), sem("probs_split")
        probs_turned, turned_copied = sem("probs_turned"), sem("turned_copied")
        values_summed = sem("values_summed")
        out_normed, o_hi, x1_ready = sem("out_normed"), sem("o_hi"), sem("x1_ready")

        moe_hi, moe_ready = sem("moe_hi"), sem("moe_ready")
        route_shifted, route_exp = sem("route_shifted"), sem("route_exp")
        up_ready, tanh_ready = sem("up_ready"), sem("tanh_ready")
        gated, act_split = sem("gated"), sem("act_split")
        x0_filled, x0_drained = sem("x0_filled"), sem("x0_drained")
        x1_filled, x1_drained = sem("x1_filled"), sem("x1_drained")
        xq_ready = sem("xq_ready")
        conv_begun, conv_done, ffn_tanh, ffn_act = (
            sem("conv_begun"), sem("conv_done"), sem("ffn_tanh"), sem("ffn_act"))
        rate_ready, q2_ready, out_ready = sem("rate_ready"), sem("q2_ready"), sem("out_ready")

        def w(chunk, part, col, n):
            at = (2 * chunk + part) * CHUNK + col
            return WH[:, at:at + n]

        def layer_chunks(layer, group):
            if layer == 0:
                return L0_Q, L0_K, L0_V, L0_O, 1
            return L1_Q + group, L1_K + group, L1_V + group, L1_O + 2 * group, 2

        def latents_of(layer):
            keys = kv[layer][:, :, :, 0:TOK]
            return [(latq, V_GLAT), (keys, V_GATED)] if layer == 0 else [(keys, 8 + V_GLAT)]

        PASSES = ((0, 0), (0, 1), (1, 0))

        def every_iteration(eng, body):
            for n in range(LOOP[0]):
                body(Iteration(n, n))
            with eng.Fori(LOOP[0], LOOP[1]) as n:
                body(Iteration(n, LOOP[0]))
            for n in range(LOOP[1], LAST):
                body(Iteration(n, n))

        def chunks_due(it, s):
            if not isinstance(it.n, int):
                return range(0)
            if it.n == 0 and s == SLOTS - 2:
                return range(0, MOE0)
            if it.n == 1 and s >= SLOTS - 16:
                first = MOE0 + 3 * (s - SLOTS + 16)
                return range(first, first + 3)
            if it.n == 2 and 5 <= s < 5 + CHUNKS - L1_Q:
                return range(L1_Q + s - 5, L1_Q + s - 4)
            return range(0)

        block = stack.enter_context(nc.Block())

        @block.sync
        def _(sp):
            sp.dma_start(vec[:, 0:NVEC], vectors_in).then_inc(vectors_loaded, 16)
            sp.dma_start(gates[:], gates_in.to_broadcast([128, 5])).then_inc(vectors_loaded, 16)
            sp.dma_start(router[:], router_in).then_inc(vectors_loaded, 16)

            def load_context(b, loaded):
                sp.dma_start(ctxb[0:CP], ctx_in[b].rearrange("(t p) d -> p t d", p=CP)).then_inc(loaded, 16)

            def load_mask(layer, stage, it, b):
                if stage:
                    made = sp.to_reg(it.at({stage: 1}, 1))
                    sp.wait_ge(vectors_loaded, 48)
                    sp.wait_ge(kv_ready["PB".index(stage)], made)
                sp.dma_start(mask8[:], mask_in[b].to_broadcast([TOK, CTX]))\
                    .then_inc(mask_loaded[layer], 16)

            def load_for_p(it, s):
                b = it.seq("P")
                before = it.beside(-1)
                if s == 2:
                    if "B" in it.on:
                        sp.wait_ge(x1_drained, it.x1_at(("b_turn", KB - 1)))
                    elif "P" in before.on:
                        sp.wait_ge(x1_drained, before.x1_at(("p_turn", KB - 1)))
                    load_context(b, p_loaded)
                    sp.wait_ge(kv_ready[0], it.at({"P": 1}, 0))
                    sp.dma_start(xp[:], x_in[b]).then_inc(p_loaded, 16)
                if s == 5:
                    load_mask(0, "B" if "B" in it.on else None, it, b)
                if s == 15:
                    sp.wait_ge(x1_ready, it.at({"A": 1}, 1 if "A" in it.on else 0))
                    sp.dma_start(xa[:], x_in[b]).then_inc(a_loaded, 16)

            def load_for_b(it, s):
                b = it.seq("B") + 1
                stage = "P" if "P" in it.on else "B"
                if s == 16:
                    sp.wait_ge(x1_drained, it.x1_at((stage.lower() + "_turn", KB - 1)))
                    load_context(b, b_loaded)
                if s == 17:
                    load_mask(1, stage, it, b)

            def body(it):
                for s, tasks in enumerate(it.slots()):
                    if "P" in it.on:
                        load_for_p(it, s)
                    if "B" in it.beside(1).on:
                        load_for_b(it, s)
                    if ("f_down",) in it.tasks.get(s, []):
                        sp.wait_ge(out_ready, it.at({"F": 1}, 1))
                        sp.dma_start(out[it.seq("F")], xf[:]).then_inc(stored, 16)

            every_iteration(sp, body)
            sp.wait_ge(stored, 16 * NSEQ)

        @block.gpsimd
        def _(pool):
            pool.memset(idf[:], 0.0)
            pool.memset(idh[:], 0.0)
            pool.memset(ones[:], 1.0)
            pool.memset(minus_half[:], -0.5)
            pool.memset(growth[:, 0:CT], 1.0)
            pool.memset(growth[:, CT:CT + 1], 1.0 + LN_EPS)
            pool.memset(bias[:, 0:CT], LN_EPS)
            pool.memset(bias[:, CT:CT + 1], LN_EPS * LN_EPS)
            pool.iota(rev[:], pattern=[[-1, EXPERTS]], base=EXPERTS, channel_multiplier=0,
                      allow_small_or_imprecise_dtypes=True)
            pool.drain()
            for m in (idf, idh):
                last = pool.affine_select(out=m[:], in_=m[:], compare_op=ALU.not_equal, fill=1.0,
                                          base=0, pattern=[[-1, 128]], channel_multiplier=1)
            last.then_inc(consts_set, 1)
            for s in "PBMF":
                last = pool.memset(mv[s][:], 1.0)
            last.then_inc(consts_set, 1)

            def rstd(stage, it, cols):
                m, r = mv[stage], rs[stage]
                pool.wait_ge(stats_ready[stage], it.at({stage: 1}, 1))
                pool.tensor_tensor(r[:, 0:cols], m[:, 0:cols, 1], growth[:, 0:cols], ALU.mult)
                pool.drain()
                pool.tensor_tensor(r[:, 0:cols], r[:, 0:cols], bias[:, 0:cols], ALU.add)
                pool.drain()
                pool.tensor_tensor(r[:, 0:cols], r[:, 0:cols], minus_half[:, 0:cols], ALU.pow)\
                    .then_inc(rstd_ready[stage], 1)

            def split_probs(it, k):
                ready, turned = (pool.to_reg(it.at(UNITS, n)) for n in (k + 1, k - 1))
                pool.wait_ge(zeros_set, 1)
                pool.wait_ge(probs_turned, turned)
                pool.wait_ge(probs_ready, ready)
                pool.tensor_tensor(PR[0:TOK, k % 2, 1, 0:KEYS], S[0:TOK, k % 2, 0:KEYS],
                                   PR[0:TOK, k % 2, 0, 0:KEYS], ALU.subtract).then_inc(probs_split, 1)

            def split_hidden(it, h):
                m0 = 2 * (h % 2)
                f = act.rearrange("p (m t) -> p m t", m=2)
                made = pool.to_reg(it.at(HALVES, h + 1))
                if h >= 2:
                    multiplied = pool.to_reg(it.x0_at(("m_down", h // 2 - 1)))
                pool.wait_ge(zeros_set, 1)
                if h >= 2:
                    pool.wait_ge(x0_filled, multiplied)
                pool.wait_ge(gated, made)
                pool.tensor_copy(aT[:, 0, m0:m0 + 2], f)
                pool.drain()
                pool.tensor_tensor(aT[:, 1, m0:m0 + 2], f, aT[:, 0, m0:m0 + 2],
                                   ALU.subtract).then_inc(act_split, 1)

            def body(it):
                *_, before = it.beside(-1).slots()
                for s, slot in enumerate(it.slots()):
                    for own, task in before:
                        if task[0] == "m_up":
                            split_hidden(own, task[1])
                    for own, task in before:
                        if task[0] in NORMS:
                            stage = task[0][0].upper()
                            rstd(stage, own, CT + 1 if stage in "PB" else 1)
                    for own, k in it.unit(s):
                        split_probs(own, k)
                    before = slot

            every_iteration(pool, body)

        @block.scalar
        def _(act_e):
            act_e.wait_ge(vectors_loaded, 48)
            act_e.activation(tgate[:], gates[:, 0:4], ACT.Tanh).then_inc(gates_ready, 1)
            act_e.wait_ge(gates_scaled, 1)

            def load_chunks(c, n, first_raw):
                act_e.dma_start(first_raw, weights_in[:, c * CHUNK:(c + n) * CHUNK])\
                    .then_inc(w_loaded[next(x for x in sorted(w_loaded, reverse=True) if x <= c)], 16)

            def raws(c, n):
                return W[:, (c + SHIFT) * CHUNK:(c + SHIFT + n) * CHUNK]

            load_chunks(0, MOE0, raws(0, MOE0))
            act_e.dma_start(W[:, (CHUNKS - FFN_CHUNKS) * CHUNK:CHUNKS * CHUNK], ffn_in).then_inc(ffn_loaded, 16)
            for c in range(MOE0, L1_Q, MOE_CHUNKS):
                load_chunks(c, MOE_CHUNKS, raws(c, MOE_CHUNKS))

            def prepare(it, s):
                for c in chunks_due(it, s):
                    if c in w_loaded:
                        act_e.wait_ge(w_loaded[c], 32 if c == L1_Q else 16)
                    act_e.wait_ge(w_split, max(0, c - SHIFT + 1))
                    act_e.activation(w(c, 0, 0, CHUNK), raw(c), ACT.Copy, scale=WSCALE).then_inc(w_hi, 1)
                if it.like == 1 and s == SLOTS - 1:
                    act_e.wait_ge(ffn_w_ready, 1)
                    last = CHUNKS - SHIFT
                    load_chunks(L1_Q, last - L1_Q, raws(L1_Q, last - L1_Q))
                    load_chunks(last, SHIFT, kvb_flat[:, 0:SHIFT * CHUNK])

            def turned_copy(it, k):
                act_e.wait_ge(probs_turned, it.at(UNITS, k + 1))
                act_e.wait_ge(values_summed, it.at(UNITS, k))
                act_e.activation(PT[:, :, :, 0:TOK], bT16, ACT.Copy).then_inc(turned_copied, 1)

            def exp(it, k):
                layer, group, _ = it.group_of(k)
                g = layer + group
                act_e.wait_ge(scores_masked, it.at(UNITS, k + 1))
                act_e.activation(S[0:TOK, k % 2, 0:KEYS], S[0:TOK, k % 2, 0:KEYS], ACT.Exp,
                                 bias=rmin[0:TOK, k % 2:k % 2 + 1], scale=-1.0,
                                 accum_out=rsum[0:TOK, g, k % HEADS:k % HEADS + 1])
                act_e.drain()
                act_e.wait_ge(probs_turned, it.at(UNITS, k - 1))
                act_e.activation(PR[0:TOK, k % 2, 0, 0:KEYS], S[0:TOK, k % 2, 0:KEYS], ACT.Copy).then_inc(probs_ready, 1)

            def part(it, task):
                name = task[0]
                if name == "q":
                    p = task[1]
                    act_e.wait_ge(x0_filled, it.x0_at(task))
                    act_e.wait_ge(scores_ready, it.at(UNITS, 2 * p - 2))
                    for h in range(2):
                        r = slice(64 * h, 64 * h + 64)
                        last = act_e.activation(qT[r, p % 2, h, 0, 0:TOK], bX0[r, 0:TOK], ACT.Copy,
                                                scale=-0.125 / WSCALE)
                    last.then_inc(q_hi, 1)
                elif name == "k":
                    p = task[1]
                    act_e.wait_ge(k_ready, it.at(PAIR, p + 1))
                    act_e.wait_ge(scores_ready, it.at(UNITS, 2 * p - 2))
                    act_e.activation(kT[:, p % 2, 0, :], bK[:, 0:KW], ACT.Copy, scale=1 / WSCALE)\
                        .then_inc(k_hi, 1)
                elif name == "v":
                    p = task[1]
                    act_e.wait_ge(v_ready, it.at(PAIR, p + 1))
                    act_e.wait_ge(values_summed, it.at(UNITS, 2 * p - 2))
                    act_e.activation(vN[:, p % 2, 0], bV[:].rearrange("p (t d) -> p t d", t=4), ACT.Copy,
                                     scale=1 / WSCALE).then_inc(v_hi, 1)
                elif name in ("p_turn", "b_turn"):
                    layer, kb = int(name == "b_turn"), task[1]
                    c = 8 * layer + kb
                    act_e.wait_ge(x1_filled, it.x1_at(task))
                    act_e.activation(kv[layer][:, kb, 0, TOK:KEYS], bX1[:, 0:CTX], ACT.Identity,
                                     scale=vec[:, c + V_GAMMA:c + V_GAMMA + 1],
                                     bias=vec[:, c + V_BETA:c + V_BETA + 1]).then_inc(kv_hi[layer], 1)
                elif name in ("p_lat", "b_lat"):
                    layer = int(name == "b_lat")
                    act_e.wait_ge(x1_filled, it.x1_at(task))
                    for dst, c in latents_of(layer):
                        for kb in range(KB):
                            last = act_e.activation(dst[:, kb, 0, :], bX1[:, TOK * kb:TOK * kb + TOK],
                                                    ACT.Identity, scale=vec[:, c + kb:c + kb + 1],
                                                    bias=vec[:, c + KB + kb:c + KB + kb + 1])
                    last.then_inc(kv_hi[layer], 1)
                elif name == "o_turn":
                    act_e.wait_ge(x1_filled, it.x1_at(task))
                    act_e.activation(oT[:, 0], bX1[:, 0:4 * TOK].rearrange("p (m t) -> p m t", m=4),
                                     ACT.Copy).then_inc(o_hi, 1)
                elif name == "m_turn":
                    act_e.wait_ge(x1_filled, it.x1_at(task))
                    act_e.activation(xmT[:, 0], bX1[:, 0:KB * TOK].rearrange("p (k t) -> p k t", k=KB),
                                     ACT.Copy).then_inc(moe_hi, 1)
                elif name == "m_route":
                    act_e.wait_ge(route_shifted, it.at({"M": 1}, 1))
                    act_e.activation(sh, sh, ACT.Exp).then_inc(route_exp, 1)
                elif name == "m_up":
                    h = task[1]
                    act_e.wait_ge(up_ready, it.at(HALVES, h + 1))
                    act_e.wait_ge(act_split, it.at(HALVES, h))
                    act_e.activation(act, bH[:, 0:2 * TOK], ACT.Tanh, scale=0.5 / WSCALE).then_inc(tanh_ready, 1)
                elif name == "f_conv":
                    j = task[1]
                    act_e.wait_ge(x1_drained, it.x1_at(("f_up", j)))
                    for i in range(4):
                        b = 4 * j + i
                        last = act_e.activation(hact[:, b, :], hpad[:, i, 0:TOK], ACT.Identity,
                                                scale=vec[:, V_CONVW + b:V_CONVW + b + 1],
                                                bias=vec[:, V_CONVB + b:V_CONVB + b + 1])
                    last.then_inc(conv_begun, 1)
                elif name == "f_act":
                    j = task[1]
                    act_e.wait_ge(conv_done, it.at({"F": 2}, j + 1))
                    act_e.activation(hpad[:, :, 1:TOK + 1], hact[:, 4 * j:4 * j + 4, :], ACT.Tanh, scale=0.5)\
                        .then_inc(ffn_tanh, 1)

            def body(it):
                *_, before = it.beside(-1).slots()
                for s, slot in enumerate(it.slots()):
                    prepare(it, s)
                    for own, k in it.unit(s, 2):
                        turned_copy(own, k)
                    for own, task in before:
                        if task[0] in ("q", "k", "v") + LAST_OF_SLOT:
                            part(own, task)
                    for own, k in it.unit(s):
                        exp(own, k)
                    for own, task in slot:
                        if task[0] not in ("q", "k", "v") + LAST_OF_SLOT:
                            part(own, task)
                    before = slot

            every_iteration(act_e, body)

        @block.tensor
        def _(pe):
            pe.wait_ge(consts_set, 2)
            pe.wait_ge(zeros_set, 1)

            def proj_q(it, p):
                layer, group, j = it.pair_group(p)
                wq, _, _, _, step = layer_chunks(layer, group)
                pe.wait_ge(x0_drained, it.x0_at(("q", p), 0))
                n = 0
                for kb in range(KB):
                    for a, b in PASSES:
                        rhs = latq[:, kb, b, :] if layer == 0 else kv[1][:, kb, b, 0:TOK]
                        last = pe.matmul(bX0[:, 0:TOK], w(wq + kb * step, a, 128 * j, 128), rhs,
                                         start=n == 0, stop=n == 5)
                        n += 1
                last.then_inc(x0_filled, 1)

            def proj_k(it, p):
                layer, group, j = it.pair_group(p)
                _, wk, _, _, step = layer_chunks(layer, group)
                pe.wait_ge(k_split, it.at(PAIR, p))
                n = 0
                for kb in range(KB):
                    for a, b in PASSES:
                        last = pe.matmul(bK[:, 0:KW], w(wk + kb * step, a, 128 * j, 128),
                                         kv[layer][:, kb, b, 0:KW], start=n == 0, stop=n == 5)
                        n += 1
                last.then_inc(k_ready, 1)

            def proj_v(it, p):
                layer, group, j = it.pair_group(p)
                _, _, wv, _, step = layer_chunks(layer, group)
                pe.wait_ge(v_split, it.at(PAIR, p))
                for t in range(4):
                    n = 0
                    for kb in range(KB):
                        for a, b in PASSES:
                            last = pe.matmul(bV[:, 128 * t:128 * t + 128],
                                             kv[layer][:, kb, a, 128 * t:128 * t + 128],
                                             w(wv + kb * step, b, 128 * j, 128),
                                             start=n == 0, stop=n == 5)
                            n += 1
                last.then_inc(v_ready, 1)

            def scores(it, k):
                p, h = k // 2, k % 2
                pe.wait_ge(x0_drained, it.x0_at(("q", p)))
                pe.wait_ge(k_split, it.at(PAIR, p + 1))
                pe.wait_ge(scores_masked, it.at(UNITS, k))
                for n, (a, b) in enumerate(PASSES):
                    last = pe.matmul(bS[:, 0:KW], qT[:, p % 2, h, a, :], kT[:, p % 2, b, :],
                                     start=n == 0, stop=n == 2)
                last.then_inc(scores_ready, 1)

            def turn_probs(it, k):
                pe.wait_ge(probs_split, it.at(UNITS, k + 1))
                pe.wait_ge(turned_copied, it.at(UNITS, k))
                for a in range(2):
                    for t in range(4):
                        last = pe.transpose(bT16[:, a, t, :], PR[0:TOK, k % 2, a, 128 * t:128 * t + 128],
                                            idh[0:TOK, 0:TOK])
                last.then_inc(probs_turned, 1)

            def sum_values(it, k):
                p, h = k // 2, k % 2
                pe.wait_ge(turned_copied, it.at(UNITS, k + 1))
                pe.wait_ge(v_split, it.at(PAIR, p + 1))
                if k % HEADS == 0:
                    pe.wait_ge(out_normed, it.at(GROUP, k // HEADS))
                n = 0
                col = HD * (k % HEADS)
                for t in range(4):
                    for a, b in PASSES:
                        last = pe.matmul(bO[:, col:col + HD], PT[:, a, t, :],
                                         vN[:, p % 2, b, t, HD * h:HD * h + HD], start=n == 0, stop=n == 11)
                        n += 1
                last.then_inc(values_summed, 1)

            def group_of_task(it, stage):
                if stage == "A":
                    return 0, 0, it.at(GROUP, 1)
                if stage == "B":
                    return 1, 0, it.at(GROUP, 2 if "A" in it.on else 1)
                return 1, 1, it.at(GROUP, 0)

            def part(it, task):
                name = task[0]
                if name in ("q", "k", "v"):
                    p = task[1]
                    layer = it.pair_group(p)[0]
                    if name == "k" and (p == 0 or (p == PAIRS and "A" in it.on)):
                        stage = "PB"[layer]
                        pe.wait_ge(kv_ready[layer], it.at({stage: 1}, layer))
                    {"q": proj_q, "k": proj_k, "v": proj_v}[name](it, p)
                    return
                if name in X1_TASKS:
                    pe.wait_ge(x1_drained, it.x1_at(task, 0))
                if name in ("p_turn", "b_turn"):
                    stage, kb = name[0].upper(), task[1]
                    pe.wait_ge(norm_ready[stage], it.at({stage: 2}, 1))
                    for t in range(CT):
                        last = pe.transpose(bX1[:, CP * t:CP * t + CP], ctxb[0:CP, t, 128 * kb:128 * kb + 128],
                                            idf[0:CP, 0:CP])
                    last.then_inc(x1_filled, 1)
                elif name in ("p_lat", "b_lat", "m_turn"):
                    stage = name[0].upper()
                    pe.wait_ge(norm_ready[stage], it.at({stage: 1 if stage == "M" else 2},
                                                        1 if stage == "M" else 2))
                    for kb in range(KB):
                        last = pe.transpose(bX1[:, TOK * kb:TOK * kb + TOK], xn[:, 128 * kb:128 * kb + 128],
                                            idf[0:TOK, 0:TOK])
                    last.then_inc(x1_filled, 1)
                elif name == "o_turn":
                    pe.wait_ge(out_normed, group_of_task(it, task[1])[2])
                    for m in range(4):
                        last = pe.transpose(bX1[:, TOK * m:TOK * m + TOK], wide[0:TOK, 128 * m:128 * m + 128],
                                            idf[0:TOK, 0:TOK])
                    last.then_inc(x1_filled, 1)
                elif name == "o_proj":
                    layer, group, _ = group_of_task(it, task[1])
                    wo = layer_chunks(layer, group)[3]
                    n = 0
                    for m in range(4):
                        for a, b in PASSES:
                            last = pe.matmul(bX1[0:TOK, 0:DIM], oT[:, a, m, :],
                                             w(wo + m // 2, b, DIM * (m % 2), DIM), start=n == 0, stop=n == 11)
                            n += 1
                    last.then_inc(x1_filled, 1)
                elif name == "m_gate":
                    pe.wait_ge(x0_drained, it.x0_at(task, 0))
                    pe.wait_ge(x1_drained, it.x1_at(("m_turn",)))
                    for kb in range(KB):
                        last = pe.matmul(bX0[0:TOK, 0:EXPERTS], xmF[:, kb, :], router[:, kb, :],
                                         start=kb == 0, stop=kb == 1)
                    last.then_inc(x0_filled, 1)
                elif name == "m_up":
                    h = task[1]
                    e = h // 2
                    if h == 0:
                        pe.wait_ge(moe_ready, it.at({"M": 1}, 1))
                    pe.wait_ge(gated, it.at(HALVES, h))
                    first = MOE0 + MOE_CHUNKS * e
                    for i in range(4):
                        mat, m = i // 2, 2 * (h % 2) + i % 2
                        n = 0
                        for kb in range(KB):
                            for a, b in PASSES:
                                last = pe.matmul(bH[:, TOK * i:TOK * i + TOK],
                                                 w(first + 2 * mat + kb, a, 128 * m, 128), xmT[:, b, kb, :],
                                                 start=n == 0, stop=n == 5)
                                n += 1
                    last.then_inc(up_ready, 1)
                elif name == "m_down":
                    e = task[1]
                    pe.wait_ge(x0_drained, it.x0_at(task, 0))
                    pe.wait_ge(act_split, it.at(HALVES, 2 * e + 2))
                    first = MOE0 + MOE_CHUNKS * e + 4
                    n = 0
                    for m in range(EB):
                        for a, b in PASSES:
                            last = pe.matmul(bX0[0:TOK, 0:DIM], aT[:, a, m, :],
                                             w(first + m // 2, b, DIM * (m % 2), DIM), start=n == 0, stop=n == 11)
                            n += 1
                    last.then_inc(x0_filled, 1)
                elif name == "f_turn":
                    pe.wait_ge(xq_ready, it.at({"F": 1}, 1))
                    pe.matmul(bX1[:, 256:256 + TOK], fs[:, 2:3].to_broadcast([TOK, 128]), idf[0:TOK, 0:TOK],
                              start=True, stop=True)
                    for kb in range(KB):
                        last = pe.transpose(bX1h[:, TOK * kb:TOK * kb + TOK], xqh[:, 128 * kb:128 * kb + 128],
                                            idh[0:TOK, 0:TOK])
                    last.then_inc(x1_filled, 1)
                elif name == "f_up":
                    j = task[1]
                    for i in range(4):
                        for kb in range(KB):
                            last = pe.matmul(bX1[:, TOK * i:TOK * i + TOK],
                                             w_up[:, kb, 128 * (4 * j + i):128 * (4 * j + i) + 128],
                                             xqT[:, kb, :], start=kb == 0, stop=kb == 1)
                    last.then_inc(x1_filled, 1)
                elif name == "f_max":
                    j = task[1]
                    pe.wait_ge(ffn_act, it.at({"F": 2}, j + 1))
                    for i in range(4):
                        last = pe.transpose(bX1[0:TOK, 128 * i:128 * i + 128], hact[:, 4 * j + i, :], idf[:])
                    last.then_inc(x1_filled, 1)
                elif name == "f_rate":
                    pe.wait_ge(rate_ready, it.at({"F": 1}, 1))
                    pe.matmul(bX1[:, 0:TOK], fs[:, 6:7].to_broadcast([TOK, 128]), idf[0:TOK, 0:TOK],
                              start=True, stop=True).then_inc(x1_filled, 1)
                elif name == "f_down":
                    pe.wait_ge(q2_ready, it.at({"F": 1}, 1))
                    for b in range(FB):
                        last = pe.matmul(bX1[0:TOK, 0:DIM], q2T[:, b, :], w_down[:, b, :],
                                         start=b == 0, stop=b == FB - 1)
                    last.then_inc(x1_filled, 1)

            def prepare(it, s):
                if it.like == 0 and s == SLOTS - 2:
                    pe.wait_ge(w_split, MOE0)
                if it.like == 1 and s == 11:
                    pe.wait_ge(wsum_ready, 1)
                    pe.matmul(bS[:, 0:2], ones[:].to_broadcast([128, 128]), wtot[:], start=True,
                              stop=True).then_inc(wsum_spread, 1)
                if it.like == 2 and s == 0:
                    pe.wait_ge(w_split, L1_Q)
                if it.like == 2 and s == SLOTS - 2:
                    pe.wait_ge(w_split, CHUNKS)
                    pe.wait_ge(ffn_w_ready, 1)

            def body(it):
                for s, slot in enumerate(it.slots()):
                    prepare(it, s)
                    for own, k in it.unit(s):
                        scores(own, k)
                    for own, task in slot:
                        if task[0] not in LAST_OF_SLOT:
                            part(own, task)
                    for own, k in it.unit(s, 2):
                        sum_values(own, k)
                    for own, k in it.unit(s, 1):
                        turn_probs(own, k)
                    for own, task in slot:
                        if task[0] in LAST_OF_SLOT:
                            part(own, task)

            every_iteration(pe, body)

        @block.vector
        def _(dve):
            for t in (qT, PR, PT, kv[0], kv[1]):
                dve.memset(t[:], 0.0)
            for m in (mask[0], mask[1], hpad):
                last = dve.memset(m[:], 0.0)
            last.then_inc(zeros_set, 1)
            dve.wait_ge(gates_ready, 1)
            dve.wait_ge(consts_set, 2)
            dve.tensor_scalar(tgs[:], tgate[:], 1 / WSCALE, None, ALU.mult)
            dve.tensor_scalar(vec[:, V_GATED:V_GATED + 2 * KB], vec[:, V_GLAT:V_GLAT + 2 * KB], gates[:, 4:5],
                              None, ALU.mult).then_inc(gates_scaled, 1)
            dve.drain()

            def prepare(it, s):
                for c in chunks_due(it, s):
                    dve.wait_ge(w_hi, c + 1)
                    dve.scalar_tensor_tensor(w(c, 1, 0, CHUNK), raw(c), WSCALE, w(c, 0, 0, CHUNK), ALU.mult,
                                             ALU.subtract).then_inc(w_split, 1)
                if it.like == 1:
                    quantise_ffn_weights(s)
                if it.like == 2 and s == 5 + CHUNKS - L1_Q:
                    dve.memset(kv[1][:], 0.0)
                    dve.drain()

            def quantise_ffn_weights(s):
                if 2 <= s < 10:
                    c = s - 2
                    dve.wait_ge(ffn_loaded, 16)
                    dve.tensor_reduce(wabs[:, c:c + 1], raw_ffn(c), AX.X, ALU.add, apply_absolute_value=True)
                if s == 10:
                    dve.drain()
                    dve.tensor_reduce(wtot[:], wabs[:].rearrange("p (m c) -> p m c", m=2), AX.X, ALU.add)\
                        .then_inc(wsum_ready, 1)
                if s == 12:
                    dve.wait_ge(wsum_spread, 1)
                    dve.tensor_scalar(wmean[:], bS[:, 0:2], 1 / (FB * 128 * DIM), QMIN_SCALE, ALU.mult, ALU.max)
                    dve.drain()
                    dve.reciprocal(winv[:], wmean[:])
                    dve.tensor_scalar(qfac[:, 0:1], wmean[:, 0:1], 1 / QMAX, None, ALU.mult)
                    dve.tensor_scalar(qfac[:, 1:2], wmean[:, 1:2], 0.5 / QMAX, tgate[:, 3:4], ALU.mult, ALU.mult)
                    dve.drain()
                if 13 <= s < 13 + FFN_CHUNKS:
                    i = s - 13
                    chunk, at = raw_ffn(i), ffn0 + i * CHUNK
                    dve.tensor_scalar(chunk, chunk, winv[:, i // 4:i // 4 + 1], ROUND, ALU.mult, ALU.add)
                    dve.drain()
                    dve.tensor_scalar(chunk, chunk, ROUND, -1.0, ALU.subtract, ALU.max)
                    dve.drain()
                    last = dve.tensor_scalar(WH[:, at:at + CHUNK], chunk, 1.0, None, ALU.min)
                    if i == FFN_CHUNKS - 1:
                        last.then_inc(ffn_w_ready, 1)

            def mask_scores(it, k):
                layer = it.group_of(k)[0]
                made, split = (dve.to_reg(it.at(UNITS, n)) for n in (k + 1, k - 1))
                dve.wait_ge(zeros_set, 1)
                dve.wait_ge(probs_split, split)
                dve.wait_ge(scores_ready, made)
                dve.tensor_tensor_reduce(out=S[0:TOK, k % 2, 0:KEYS], in0=bS[0:TOK, 0:KEYS],
                                         in1=mask[layer][:, 0:KEYS], scale=1.0, scalar=3.0e38,
                                         op0=ALU.add, op1=ALU.min,
                                         accum_out=rmin[0:TOK, k % 2:k % 2 + 1]).then_inc(scores_masked, 1)

            def norm_out(it, k):
                layer, group, _ = it.group_of(k)
                dve.wait_ge(values_summed, it.at(UNITS, k + 1))
                dve.reciprocal(rinv[0:TOK, :], rsum[0:TOK, layer + group, :])
                dve.drain()
                dve.tensor_tensor(wide[0:TOK, :].rearrange("p (h d) -> p h d", h=HEADS),
                                  bO[0:TOK, :].rearrange("p (h d) -> p h d", h=HEADS),
                                  rinv[0:TOK, :].rearrange("p (h o) -> p h o", o=1).to_broadcast([TOK, HEADS, HD]),
                                  ALU.mult).then_inc(out_normed, 1)

            def stats(stage, x, col):
                dve.bn_stats(bn[0:TOK, col, :], x[:])
                dve.drain()
                return dve.bn_aggr(mv[stage][0:TOK, col, :], bn[0:TOK, col, :])

            def norm_kv(it, stage, x):
                layer = "PB".index(stage)
                loaded, each = (p_loaded, 32) if stage == "P" else (b_loaded, 16)
                dve.wait_ge(loaded, it.at({stage: each}, each))
                for t in range(CT):
                    dve.bn_stats(bn[0:CP, t, :], ctxb[0:CP, t, :])
                dve.bn_stats(bn[0:TOK, CT, :], x[:])
                dve.drain()
                for t in range(CT):
                    dve.bn_aggr(mv[stage][0:CP, t, :], bn[0:CP, t, :])
                dve.bn_aggr(mv[stage][0:TOK, CT, :], bn[0:TOK, CT, :]).then_inc(stats_ready[stage], 1)

            def make_mask(it, layer):
                dve.wait_ge(mask_loaded[layer], it.at({"PB"[layer]: 16}, 16))
                a, b = (MASKED, 0.0) if layer == 0 else (-MASKED, MASKED)
                dve.tensor_scalar(mask[layer][:, TOK:KEYS], mask8[:], a, b, ALU.mult, ALU.add)

            def apply_kv(it, stage, x):
                dve.wait_ge(rstd_ready[stage], it.at({stage: 1}, 1))
                r = rs[stage]
                for t in range(CT):
                    last = dve.tensor_scalar(ctxb[0:CP, t, :], ctxb[0:CP, t, :], mv[stage][0:CP, t, 0:1],
                                             r[0:CP, t:t + 1], ALU.subtract, ALU.mult)
                last.then_inc(norm_ready[stage], 1)
                dve.tensor_scalar(xn[:], x[:], mv[stage][0:TOK, CT, 0:1], r[0:TOK, CT:CT + 1],
                                  ALU.subtract, ALU.mult).then_inc(norm_ready[stage], 1)

            def apply_x(it, stage, x):
                dve.wait_ge(rstd_ready[stage], it.at({stage: 1}, 1))
                return dve.tensor_scalar(xn[:], x[:], mv[stage][0:TOK, 0, 0:1], rs[stage][0:TOK, 0:1],
                                         ALU.subtract, ALU.mult)

            def rank_experts(it, task):
                v1, v2 = rsc[:, 0:1], rsc[:, 1:2]
                dve.wait_ge(x0_filled, it.x0_at(task))
                dve.tensor_copy(lg, bX0[0:TOK, 0:EXPERTS]).then_inc(x0_drained, 1)
                dve.drain()
                for i, (s, v) in enumerate(((lg, v1), (s2, v2))):
                    dve.tensor_reduce(v, s, AX.X, ALU.max)
                    dve.drain()
                    dve.scalar_tensor_tensor(rk[:, i, :], s, v, rev[:], ALU.is_equal, ALU.mult)
                    dve.drain()
                    dve.tensor_reduce(rsc[:, 2 + i:3 + i], rk[:, i, :], AX.X, ALU.max)
                    dve.drain()
                    dve.tensor_scalar(one[:, i, :], rk[:, i, :], rsc[:, 2 + i:3 + i], None, ALU.is_equal)
                    dve.tensor_scalar(gk[:, i, :], lg, -1.0, v, ALU.mult, ALU.max)
                    last = dve.tensor_scalar(sh[:, i, :], lg, v, 0.0, ALU.subtract, ALU.min)
                    if i == 0:
                        dve.drain()
                        dve.scalar_tensor_tensor(s2, one[:, 0, :], -3.0e38, lg, ALU.mult, ALU.add)
                        dve.drain()
                dve.drain()
                for i in range(2):
                    dve.tensor_tensor(gk[:, i, :], gk[:, i, :], lg, ALU.max)
                dve.drain()
                dve.scalar_tensor_tensor(gk, gk, JITTER, sh, ALU.mult, ALU.add)\
                    .then_inc(route_shifted, 1)

            def weigh_experts(it):
                dve.wait_ge(route_exp, it.at({"M": 1}, 1))
                dve.scalar_tensor_tensor(rk[:, 0, :], gk[:, 0, :], 0.0, sh[:, 0, :], ALU.is_ge, ALU.mult,
                                         accum_out=rsc[:, 4:5])
                dve.scalar_tensor_tensor(rk[:, 1, :], gk[:, 1, :], 0.0, sh[:, 1, :], ALU.is_ge, ALU.mult)
                dve.drain()
                dve.scalar_tensor_tensor(gk[:, 1, :], one[:, 0, :], 0.5, rk[:, 1, :], ALU.is_lt, ALU.mult,
                                         accum_out=rsc[:, 5:6])
                dve.drain()
                dve.reciprocal(rsc[:, 6:8], rsc[:, 4:6])
                dve.drain()
                dve.tensor_scalar(dw[:], one[:, 0, :], rsc[:, 6:7], None, ALU.mult)
                dve.drain()
                dve.scalar_tensor_tensor(dw[:], one[:, 1, :], rsc[:, 7:8], dw[:], ALU.mult, ALU.add)
                dve.drain()
                dve.tensor_scalar(dw[:], dw[:], tgs[0:TOK, 2:3], None, ALU.mult)
                dve.drain()

            def quantise(dst, src, scale_col, tmp):
                dve.tensor_scalar(tmp, src, scale_col, ROUND, ALU.mult, ALU.add)
                dve.drain()
                return dve.tensor_scalar(dst, tmp, ROUND, None, ALU.subtract)

            def part(it, task):
                name = task[0]
                if name == "q":
                    p = task[1]
                    dve.wait_ge(q_hi, it.at(PAIR, p + 1))
                    for h in range(2):
                        r = slice(64 * h, 64 * h + 64)
                        last = dve.scalar_tensor_tensor(qT[r, p % 2, h, 1, 0:TOK], bX0[r, 0:TOK],
                                                        -0.125 / WSCALE, qT[r, p % 2, h, 0, 0:TOK],
                                                        ALU.mult, ALU.subtract)
                    last.then_inc(x0_drained, 1)
                elif name == "k":
                    p = task[1]
                    dve.wait_ge(k_hi, it.at(PAIR, p + 1))
                    dve.scalar_tensor_tensor(kT[:, p % 2, 1, :], bK[:, 0:KW], 1 / WSCALE, kT[:, p % 2, 0, :],
                                             ALU.mult, ALU.subtract).then_inc(k_split, 1)
                elif name == "v":
                    p = task[1]
                    dve.wait_ge(v_hi, it.at(PAIR, p + 1))
                    dve.scalar_tensor_tensor(vN[:, p % 2, 1].rearrange("p t d -> p (t d)"), bV[:], 1 / WSCALE,
                                             vN[:, p % 2, 0].rearrange("p t d -> p (t d)"),
                                             ALU.mult, ALU.subtract).then_inc(v_split, 1)
                elif name == "p_norm":
                    norm_kv(it, "P", xp)
                elif name == "b_norm":
                    norm_kv(it, "B", xm)
                elif name in ("m_norm", "f_norm"):
                    stats(name[0].upper(), x1 if name == "m_norm" else xf, 0)\
                        .then_inc(stats_ready[name[0].upper()], 1)
                elif name == "p_apply":
                    apply_kv(it, "P", xp)
                elif name == "b_apply":
                    apply_kv(it, "B", xm)
                elif name == "m_apply":
                    apply_x(it, "M", x1).then_inc(norm_ready["M"], 1)
                elif name in ("p_turn", "b_turn"):
                    layer, kb = int(name == "b_turn"), task[1]
                    stage = "PB"[layer]
                    c = 8 * layer + kb
                    dve.wait_ge(kv_hi[layer], it.at({stage: 3}, kb + 1))
                    dve.tensor_scalar(affine[layer][:, 0:CTX], bX1[:, 0:CTX], vec[:, c + V_GAMMA:c + V_GAMMA + 1],
                                      vec[:, c + V_BETA:c + V_BETA + 1], ALU.mult, ALU.add).then_inc(x1_drained, 1)
                    dve.drain()
                    dve.tensor_tensor(kv[layer][:, kb, 1, TOK:KEYS], affine[layer][:, 0:CTX],
                                      kv[layer][:, kb, 0, TOK:KEYS], ALU.subtract)
                    dve.drain()
                elif name in ("p_lat", "b_lat"):
                    layer = int(name == "b_lat")
                    stage = "PB"[layer]
                    dve.wait_ge(kv_hi[layer], it.at({stage: 3}, 3))
                    places = latents_of(layer)
                    n = KB * TOK
                    for i, (_, c) in enumerate(places):
                        for kb in range(KB):
                            at = n * i + TOK * kb
                            last = dve.tensor_scalar(affine[layer][:, at:at + TOK], bX1[:, TOK * kb:TOK * kb + TOK],
                                                     vec[:, c + kb:c + kb + 1],
                                                     vec[:, c + KB + kb:c + KB + kb + 1], ALU.mult, ALU.add)
                    last.then_inc(x1_drained, 1)
                    dve.drain()
                    make_mask(it, layer)
                    for i, (dst, _) in enumerate(places):
                        last = dve.tensor_tensor(dst[:, :, 1, :],
                                                 affine[layer][:, n * i:n * i + n].rearrange("p (k t) -> p k t", k=KB),
                                                 dst[:, :, 0, :], ALU.subtract)
                    last.then_inc(kv_ready[layer], 1)
                    dve.drain()
                elif name == "b_keep":
                    dve.tensor_copy(xb[:], xm[:])
                    dve.drain()
                elif name == "o_turn":
                    dve.wait_ge(o_hi, it.at({"A": 1, "B": 1, "F": 1}, [t for t in it.x1 if t[0] == name].index(task) + 1))
                    dve.tensor_tensor(oT[:, 1], bX1[:, 0:4 * TOK].rearrange("p (m t) -> p m t", m=4),
                                      oT[:, 0], ALU.subtract).then_inc(x1_drained, 1)
                elif name == "o_proj":
                    dve.wait_ge(x1_filled, it.x1_at(task))
                    dst, src, g = {"A": (x1, xa, 0), "B": (xb, xb, 1), "F": (xf, xb, 1)}[task[1]]
                    if task[1] == "A":
                        dve.wait_ge(a_loaded, it.at({"A": 16}, 16))
                    if task[1] == "F":
                        dve.wait_ge(stored, it.at({"F": 16}, 0))
                    dve.scalar_tensor_tensor(dst[:], bX1[0:TOK, 0:DIM], tgs[0:TOK, g:g + 1], src[:],
                                             ALU.mult, ALU.add).then_inc(x1_drained, 1)
                    dve.drain()
                    if task[1] == "A":
                        dve.memset(fs[:, 7:8], 0.0).then_inc(x1_ready, 1)
                elif name == "m_turn":
                    dve.wait_ge(moe_hi, it.at({"M": 1}, 1))
                    dve.tensor_copy(xmF[:], bX1[:, 0:KB * TOK].rearrange("p (k t) -> p k t", k=KB))\
                        .then_inc(x1_drained, 1)
                    dve.drain()
                    dve.tensor_tensor(xmT[:, 1], xmF[:], xmT[:, 0], ALU.subtract).then_inc(moe_ready, 1)
                elif name == "m_gate":
                    rank_experts(it, task)
                elif name == "m_route":
                    weigh_experts(it)
                elif name == "m_up":
                    h = task[1]
                    n = 2 * TOK
                    dve.wait_ge(tanh_ready, it.at(HALVES, h + 1))
                    dve.scalar_tensor_tensor(act, act, 1.0, bH[:, 0:n], ALU.add, ALU.mult)
                    dve.drain()
                    dve.scalar_tensor_tensor(act, act, 0.5 / (WSCALE * WSCALE), bH[:, n:2 * n],
                                             ALU.mult, ALU.mult).then_inc(gated, 1)
                elif name == "m_down":
                    e = task[1]
                    dve.wait_ge(x0_filled, it.x0_at(task))
                    dve.scalar_tensor_tensor(xm[:], bX0[0:TOK, 0:DIM], dw[:, e:e + 1], (x1 if e == 0 else xm)[:],
                                             ALU.mult, ALU.add).then_inc(x0_drained, 1)
                    dve.drain()
                elif name == "f_apply":
                    apply_x(it, "F", xf)
                    dve.drain()
                    dve.tensor_reduce(fs[:, 0:1], xn[:], AX.X, ALU.max, apply_absolute_value=True)
                    dve.drain()
                    dve.tensor_scalar(fs[:, 0:1], fs[:, 0:1], QMIN_SCALE, None, ALU.max)
                    dve.drain()
                    dve.reciprocal(fs[:, 1:2], fs[:, 0:1])
                    dve.tensor_scalar(fs[:, 2:3], fs[:, 0:1], qfac[0:TOK, 0:1], None, ALU.mult)
                    dve.drain()
                    dve.tensor_scalar(fs[:, 1:2], fs[:, 1:2], QMAX, None, ALU.mult)
                    dve.drain()
                    quantise(xqh, xn[:], fs[:, 1:2], xn[:]).then_inc(xq_ready, 1)
                elif name == "f_turn":
                    dve.wait_ge(x1_filled, it.x1_at(task))
                    dve.tensor_copy(xqT, bX1h[:, 0:KB * TOK].rearrange("p (k t) -> p k t", k=KB))
                    dve.tensor_copy(rate[:], bX1[:, 256:256 + TOK]).then_inc(x1_drained, 1)
                    dve.memset(hpad[:, :, 0:1], 0.0)
                    dve.memset(hpad[:, :, TOK + 1:TOK + 2], 0.0)
                    dve.drain()
                elif name == "f_up":
                    dve.wait_ge(x1_filled, it.x1_at(task))
                    dve.tensor_tensor(hpad[:, :, 1:TOK + 1], bX1[:, 0:4 * TOK].rearrange("p (m t) -> p m t", m=4),
                                      rate[:].rearrange("p (o t) -> p o t", o=1).to_broadcast([128, 4, TOK]),
                                      ALU.mult).then_inc(x1_drained, 1)
                elif name == "f_conv":
                    j = task[1]
                    dve.wait_ge(conv_begun, it.at({"F": 2}, j + 1))
                    for tap in (1, 2):
                        for i in range(4):
                            b = 4 * j + i
                            c = V_CONVW + FB * tap + b
                            last = dve.scalar_tensor_tensor(hact[:, b, :], hpad[:, i, tap:tap + TOK], vec[:, c:c + 1],
                                                            hact[:, b, :], ALU.mult, ALU.add)
                        if tap == 1:
                            dve.drain()
                    last.then_inc(conv_done, 1)
                elif name == "f_act":
                    j = task[1]
                    dve.wait_ge(ffn_tanh, it.at({"F": 2}, j + 1))
                    dve.scalar_tensor_tensor(hact[:, 4 * j:4 * j + 4, :], hpad[:, :, 1:TOK + 1], 1.0,
                                             hact[:, 4 * j:4 * j + 4, :], ALU.add, ALU.mult).then_inc(ffn_act, 1)
                    dve.drain()
                elif name == "f_max":
                    j = task[1]
                    dve.wait_ge(x1_filled, it.x1_at(task))
                    dve.tensor_reduce(fs[:, 3 + j:4 + j], bX1[0:TOK, :], AX.X, ALU.max,
                                      apply_absolute_value=True).then_inc(x1_drained, 1)
                    if j == 1:
                        dve.drain()
                        dve.tensor_scalar(fs[:, 5:6], fs[:, 3:4], fs[:, 4:5], 2 * QMIN_SCALE, ALU.max, ALU.max)
                        dve.drain()
                        dve.reciprocal(fs[:, 6:7], fs[:, 5:6])
                        dve.tensor_scalar(fs[:, 5:6], fs[:, 5:6], qfac[0:TOK, 1:2], None, ALU.mult)
                        dve.drain()
                        dve.tensor_scalar(fs[:, 6:7], fs[:, 6:7], QMAX, None, ALU.mult).then_inc(rate_ready, 1)
                elif name == "f_rate":
                    dve.wait_ge(x1_filled, it.x1_at(task))
                    dve.tensor_copy(rate[:], bX1[:, 0:TOK]).then_inc(x1_drained, 1)
                    dve.drain()
                    dve.tensor_tensor(hact[:], hact[:],
                                      rate[:].rearrange("p (o t) -> p o t", o=1).to_broadcast([128, FB, TOK]), ALU.mult)
                    dve.drain()
                    dve.tensor_scalar(hact[:], hact[:], ROUND, None, ALU.add)
                    dve.drain()
                    dve.tensor_scalar(q2T, hact[:], ROUND, None, ALU.subtract).then_inc(q2_ready, 1)
                elif name == "f_down":
                    dve.wait_ge(x1_filled, it.x1_at(task))
                    dve.scalar_tensor_tensor(xf[:], bX1[0:TOK, 0:DIM], fs[:, 5:6], xf[:], ALU.mult, ALU.add)\
                        .then_inc(x1_drained, 1)
                    dve.drain()
                    dve.memset(fs[:, 7:8], 0.0).then_inc(out_ready, 1)

            def body(it):
                for s, (first, tasks) in enumerate(it.taken_up()):
                    prepare(it, s)
                    for own, task in first:
                        part(own, task)
                    for own, k in it.unit(s):
                        mask_scores(own, k)
                    for own, task in tasks:
                        part(own, task)
                    for own, k in it.unit(s, 2):
                        if k % HEADS == HEADS - 1:
                            norm_out(own, k)

            every_iteration(dve, body)


def kernel(x, ctx_1024, mask_BxS2_bk0, g_xattn, g_ffn, L0_xattn_kv_gate, L0_xattn_gamma_media,
           L0_xattn_beta_media, L0_xattn_gamma_lat, L0_xattn_beta_lat, L0_xattn_Wq, L0_xattn_Wk,
           L0_xattn_Wv, L0_xattn_Wout, L0_ffn_gate_w, L0_ffn_w1, L0_ffn_w2, L0_ffn_w3, L1_xattn_g1,
           L1_xattn_b1, L1_xattn_g2, L1_xattn_b2, L1_xattn_Wq, L1_xattn_Wkv, L1_xattn_Wout,
           L1_ffn_w1, L1_ffn_conv_w, L1_ffn_conv_b, L1_ffn_w2):
    import numpy as np
    import concourse.bacc as bacc
    from concourse.bass_utils import run_bass_kernel_spmd

    arr = np.asarray

    def rows(m):
        m = arr(m)
        return m.reshape(m.shape[0] // 128, 128, m.shape[1]).transpose(1, 0, 2)

    def flat(m):
        return rows(m).reshape(128, -1)

    inner = L1_xattn_Wq.shape[1]
    experts = []
    for e in range(L0_ffn_w1.shape[0]):
        experts += [flat(arr(L0_ffn_w1)[e].T), flat(arr(L0_ffn_w3)[e].T), flat(arr(L0_ffn_w2)[e].T)]
    weights = np.concatenate(
        [flat(L0_xattn_Wq), flat(L0_xattn_Wk), flat(L0_xattn_Wv), flat(L0_xattn_Wout)] + experts +
        [flat(L1_xattn_Wq), flat(arr(L1_xattn_Wkv)[:, :inner]), flat(arr(L1_xattn_Wkv)[:, inner:]),
         flat(L1_xattn_Wout)], axis=1)
    ffn = np.concatenate([flat(arr(L1_ffn_w1).T), flat(arr(L1_ffn_w2).T)], axis=1)

    def cols(v):
        v = arr(v)
        return v.reshape(-1, 128).T

    conv_w = arr(L1_ffn_conv_w)[:, 0, :]
    vectors = np.concatenate(
        [cols(v) for v in (L0_xattn_gamma_media, L0_xattn_beta_media, L0_xattn_gamma_lat,
                           L0_xattn_beta_lat, L1_xattn_g1, L1_xattn_b1, L1_xattn_g2, L1_xattn_b2)] +
        [cols(conv_w[:, t]) for t in range(3)] + [cols(L1_ffn_conv_b)], axis=1)
    gates = np.concatenate([arr(g_xattn), arr(g_ffn), arr(L0_xattn_kv_gate).reshape(1)]).reshape(1, 5)
    arrays = {
        "x": arr(x), "ctx": arr(ctx_1024), "mask": arr(mask_BxS2_bk0).reshape(NSEQ, 1, CTX),
        "weights": weights, "ffn_weights": ffn, "vectors": vectors,
        "router": rows(arr(L0_ffn_gate_w).T), "gates": gates,
    }
    arrays = {f"in_{k}": np.ascontiguousarray(v) for k, v in arrays.items()}
    nc = bacc.Bacc("TRN2", target_bir_lowering=False, num_devices=1)
    args = [nc.dram_tensor(k, v.shape, mybir.dt.from_np(v.dtype), kind="ExternalInput").ap()
            for k, v in arrays.items()]
    out = nc.dram_tensor("out_y", (NSEQ, TOK, DIM), F32, kind="ExternalOutput").ap()
    build(nc, *args, out)
    r = run_bass_kernel_spmd(nc, [arrays], core_ids=[0])
    return r.results[0]["out_y"]
```
